# Optimizing a Trainium2 kernel written in Bass

```python
import numpy as np
import jax
import jax.numpy as jnp

def _softmax(x, axis=-1):
    return jax.nn.softmax(x, axis=axis)

def _gelu(x):
    return jax.nn.gelu(x, approximate=True)

def _silu(x):
    return jax.nn.silu(x)

def _sigmoid(x):
    return jax.nn.sigmoid(x)

def _layernorm(x, axis=-1, eps=1e-05):
    m = jnp.mean(x, axis=axis, keepdims=True)
    v = jnp.var(x, axis=axis, keepdims=True)
    return (x - m) / jnp.sqrt(v + eps)

def _scatter_add(tgt, idx, src, axis=0):
    return tgt.at[idx].add(src)

def _segment_sum(src, seg, n):
    return jax.ops.segment_sum(src, seg, n)
kernel_name = 'mk_xattn_ffn_d4_seqx_r4_10b516'

def setup_inputs(seed: int=0):
    np.random.seed(seed)
    _w = jnp.asarray

    def _rec_inputs():
        import jax
        import jax.numpy as jnp
        _rk = jax.random.key(seed)
        x = 7.22e-05 + 1 * jax.random.normal(jax.random.fold_in(_rk, 1), (4, 512, 256), jnp.float32)
        _lenS = 512 - jax.random.randint(jax.random.fold_in(_rk, 7), (4,), 0, max(1, 512 // 4) + 1, jnp.int32)
        _lenS2 = 512 - jax.random.randint(jax.random.fold_in(_rk, 8), (4,), 0, max(1, 512 // 4) + 1, jnp.int32)
        _ctx_1024P = jax.random.normal(jax.random.fold_in(_rk, 11), (4, 16, 256), jnp.float32)
        _ctx_1024c = jax.random.dirichlet(jax.random.fold_in(_rk, 511), 0.3 * jnp.ones((16,), jnp.float32), (4, 512))
        _ctx_1024t = jnp.einsum('bsk,bkd->bsd', _ctx_1024c, _ctx_1024P)
        _ctx_1024t = _ctx_1024t * jax.lax.rsqrt(jnp.mean(jnp.square(_ctx_1024t)) + 1e-12) * 0.953939
        ctx_1024 = 4.13588e-05 + 0.999923 * (_ctx_1024t + 0.3 * jax.random.normal(jax.random.fold_in(_rk, 611), (4, 512, 256), jnp.float32))
        _validS = jnp.arange(512)[None, :] < _lenS[:, None]
        _validS2 = jnp.arange(512)[None, :] < _lenS2[:, None]
        _causal = jnp.tril(jnp.ones((512, 512), dtype=bool))
        mask_BxSxS2_ik1 = jnp.where(jnp.broadcast_to(_validS2[:, None, :], (4, 512, 512)), 1, 0).astype(jnp.int32)
        mask_Bx1x1xS2_ff0 = jnp.where(jnp.ones((4, 1, 1, 512), dtype=bool), 0.0, -1000000000.0).astype(jnp.float32)
        return (x, ctx_1024, mask_BxSxS2_ik1, mask_Bx1x1xS2_ff0)
    x, ctx_1024, mask_BxSxS2_ik1, mask_Bx1x1xS2_ff0 = _rec_inputs()

    def _L0_xattn_setup():
        import jax, jax.numpy as jnp
        import numpy as np
        D_MODEL = 256
        N_HEAD = 16
        EPS = 1e-11
        key = jax.random.key(seed)
        ks = jax.random.split(key, 12)
        B, S, D = (4, 512, D_MODEL)
        s = 1.0 / np.sqrt(D)
        return {'query': jax.random.normal(ks[0], (B, S, D), dtype=jnp.float32), 'key': jax.random.normal(ks[1], (B, S, D), dtype=jnp.float32), 'value': jax.random.normal(ks[2], (B, S, D), dtype=jnp.float32), 'mask': jax.random.randint(ks[3], (B, S, S), 0, 2, dtype=jnp.int32), 'wq': jax.random.normal(ks[4], (D, D), dtype=jnp.float32) * s, 'bq': jnp.zeros((D,), dtype=jnp.float32), 'wk': jax.random.normal(ks[5], (D, D), dtype=jnp.float32) * s, 'bk': jnp.zeros((D,), dtype=jnp.float32), 'wv': jax.random.normal(ks[6], (D, D), dtype=jnp.float32) * s, 'bv': jnp.zeros((D,), dtype=jnp.float32), 'wo': jax.random.normal(ks[7], (D, D), dtype=jnp.float32) * s, 'bo': jnp.zeros((D,), dtype=jnp.float32)}
    _L0_xattn_all = _L0_xattn_setup()
    _L0_xattn_in = {k: v for k, v in _L0_xattn_all.items() if k in ('wq', 'bq', 'wk', 'bk', 'wv', 'bv', 'wo', 'bo')}
    del _L0_xattn_all

    def _L0_ffn_setup():
        import jax, jax.numpy as jnp
        import numpy as np
        EPS = 1e-05
        NUM_HEADS = 16
        NUM_KV_HEADS = 4
        NUM_EXPERTS = 8
        TOP_K = 2

        def _layernorm(x, w, b):
            mu = jnp.mean(x, axis=-1, keepdims=True)
            var = jnp.mean((x - mu) ** 2, axis=-1, keepdims=True)
            return (x - mu) * jax.lax.rsqrt(var + EPS) * w + b
        key = jax.random.key(seed)
        ks = jax.random.split(key, 8)
        S, B, H = (256, 4, 256)
        F = 512
        hd = H // NUM_HEADS
        qkv_out = (NUM_HEADS + 2 * NUM_KV_HEADS) * hd
        w_scale = 0.02
        return {'hidden_states': jax.random.normal(ks[0], (S, B, H), jnp.float32), 'ln1_weight': jnp.ones((H,), jnp.float32), 'ln1_bias': jnp.zeros((H,), jnp.float32), 'ln2_weight': jnp.ones((H,), jnp.float32), 'ln2_bias': jnp.zeros((H,), jnp.float32), 'qkv_weight': jax.random.normal(ks[1], (qkv_out, H), jnp.float32) * w_scale, 'proj_weight': jax.random.normal(ks[2], (H, H), jnp.float32) * w_scale, 'router_weight': jax.random.normal(ks[3], (NUM_EXPERTS, H), jnp.float32) * w_scale, 'moe_w1': jax.random.normal(ks[4], (NUM_EXPERTS, H, F), jnp.float32) * w_scale, 'moe_w2': jax.random.normal(ks[5], (NUM_EXPERTS, F, H), jnp.float32) * w_scale}
    _L0_ffn_all = _L0_ffn_setup()
    _L0_ffn_in = {k: v for k, v in _L0_ffn_all.items() if k in ('ln1_weight', 'ln1_bias', 'ln2_weight', 'ln2_bias', 'qkv_weight', 'proj_weight', 'router_weight', 'moe_w1', 'moe_w2')}
    del _L0_ffn_all

    def _L1_xattn_setup():
        import jax, jax.numpy as jnp
        import numpy as np
        N_HEADS, D_MODEL, D_HEAD, N_CTX = (16, 256, 64, 512)
        IGNORE = -100000.0
        key = jax.random.key(seed)
        ks = jax.random.split(key, 8)
        B, S = (2, 512)
        return {'query_input': jax.random.normal(ks[0], (B, S, D_MODEL), jnp.float32), 'key_input': jax.random.normal(ks[1], (B, S, D_MODEL), jnp.float32), 'value_input': jax.random.normal(ks[2], (B, S, D_MODEL), jnp.float32), 'additive_attention_mask': jnp.zeros((B, 1, 1, S), jnp.float32), 'W_Q': jax.random.normal(ks[3], (N_HEADS, D_MODEL, D_HEAD), jnp.float32) * 0.02, 'W_K': jax.random.normal(ks[4], (N_HEADS, D_MODEL, D_HEAD), jnp.float32) * 0.02, 'W_V': jax.random.normal(ks[5], (N_HEADS, D_MODEL, D_HEAD), jnp.float32) * 0.02, 'W_O': jax.random.normal(ks[6], (N_HEADS, D_HEAD, D_MODEL), jnp.float32) * 0.02, 'b_Q': jnp.zeros((N_HEADS, D_HEAD), jnp.float32), 'b_K': jnp.zeros((N_HEADS, D_HEAD), jnp.float32), 'b_V': jnp.zeros((N_HEADS, D_HEAD), jnp.float32), 'b_O': jnp.zeros((D_MODEL,), jnp.float32)}
    _L1_xattn_all = _L1_xattn_setup()
    _L1_xattn_in = {k: v for k, v in _L1_xattn_all.items() if k in ('W_Q', 'W_K', 'W_V', 'W_O', 'b_Q', 'b_K', 'b_V', 'b_O')}
    del _L1_xattn_all

    def _L1_ffn_setup():
        import jax, jax.numpy as jnp
        import numpy as np
        NUM_EXPERTS = 8
        TOP_K = 2
        CAPACITY_FACTOR = 1.0

        def _dispatch_compute(xf, top_expert, w1, w2, capacity):
            tokens, hs = xf.shape
            tpe = jnp.bincount(top_expert, length=NUM_EXPERTS)
            indices = jnp.argsort(top_expert)
            offsets = jnp.concatenate([jnp.zeros((1,), tpe.dtype), jnp.cumsum(tpe)[:-1]])
            slot = jnp.arange(capacity)
            pos = offsets[:, None] + slot[None, :]
            valid = slot[None, :] < tpe[:, None]
            tok_idx = indices[jnp.minimum(pos, tokens - 1)]
            xe = jnp.where(valid[..., None], xf[tok_idx], 0.0)
            h = jax.nn.gelu(jnp.einsum('ech,ehf->ecf', xe, w1), approximate=True)
            ye = jnp.einsum('ecf,efh->ech', h, w2)
            tok_safe = jnp.where(valid, tok_idx, tokens)
            out = jnp.zeros((tokens + 1, hs), xf.dtype).at[tok_safe.reshape(-1)].add(ye.reshape(-1, hs))
            return out[:tokens]
        key = jax.random.key(seed)
        k1, k2, k3, k4 = jax.random.split(key, 4)
        hs, ffn = (256, 1024)
        x = jax.random.normal(k1, (512, 2, hs), dtype=jnp.float32)
        router_w = jax.random.normal(k2, (hs, NUM_EXPERTS), dtype=jnp.float32) * hs ** (-0.5)
        w1 = jax.random.normal(k3, (NUM_EXPERTS, hs, ffn), dtype=jnp.float32) * 0.02
        w2 = jax.random.normal(k4, (NUM_EXPERTS, ffn, hs), dtype=jnp.float32) * 0.02
        bias = jnp.zeros((1, 1, hs), dtype=jnp.float32)
        return {'x': x, 'router_w': router_w, 'w1': w1, 'w2': w2, 'bias': bias}
    _L1_ffn_all = _L1_ffn_setup()
    _L1_ffn_in = {k: v for k, v in _L1_ffn_all.items() if k in ('router_w', 'w1', 'w2', 'bias')}
    del _L1_ffn_all

    def _L2_xattn_setup():
        import jax, jax.numpy as jnp
        import numpy as np
        B, L_ENC, L_DEC, D = (16, 128, 128, 256)
        key = jax.random.key(seed)
        k1, k2, k3, k4, k5, k6 = jax.random.split(key, 6)
        encoder_hc = jax.random.normal(k1, (B, L_ENC, D), dtype=jnp.float32)
        decoder_hq = jax.random.normal(k2, (B, L_DEC, D), dtype=jnp.float32)
        w_sim = jax.random.normal(k3, (3 * D,), dtype=jnp.float32) * 0.02
        b_sim = jax.random.normal(k4, (1,), dtype=jnp.float32) * 0.02
        W_qv = jax.random.normal(k5, (4 * D, D), dtype=jnp.float32) * 0.02
        b_qv = jax.random.normal(k6, (D,), dtype=jnp.float32) * 0.02
        return {'encoder_hc': encoder_hc, 'decoder_hq': decoder_hq, 'w_sim': w_sim, 'b_sim': b_sim, 'W_qv': W_qv, 'b_qv': b_qv}
    _L2_xattn_all = _L2_xattn_setup()
    _L2_xattn_in = {k: v for k, v in _L2_xattn_all.items() if k in ('w_sim', 'b_sim', 'W_qv', 'b_qv')}
    del _L2_xattn_all

    def _L2_ffn_setup():
        import jax, jax.numpy as jnp
        import numpy as np
        DIM = 256
        MOE_HID = 128
        SHARED_HID = 512
        N_EXPERTS = 16
        TOP_K = 2
        NORM_TOPK_PROB = True
        key = jax.random.key(seed)
        ks = jax.random.split(key, 9)
        s = 0.02
        x = jax.random.normal(ks[0], (2, 256, DIM), dtype=jnp.float32)
        Wg = jax.random.normal(ks[1], (N_EXPERTS, DIM), dtype=jnp.float32) * s
        We_gate = jax.random.normal(ks[2], (N_EXPERTS, MOE_HID, DIM), dtype=jnp.float32) * s
        We_up = jax.random.normal(ks[3], (N_EXPERTS, MOE_HID, DIM), dtype=jnp.float32) * s
        We_down = jax.random.normal(ks[4], (N_EXPERTS, DIM, MOE_HID), dtype=jnp.float32) * s
        Ws_gate = jax.random.normal(ks[5], (SHARED_HID, DIM), dtype=jnp.float32) * s
        Ws_up = jax.random.normal(ks[6], (SHARED_HID, DIM), dtype=jnp.float32) * s
        Ws_down = jax.random.normal(ks[7], (DIM, SHARED_HID), dtype=jnp.float32) * s
        Wsg = jax.random.normal(ks[8], (1, DIM), dtype=jnp.float32) * s
        return {'x': x, 'Wg': Wg, 'We_gate': We_gate, 'We_up': We_up, 'We_down': We_down, 'Ws_gate': Ws_gate, 'Ws_up': Ws_up, 'Ws_down': Ws_down, 'Wsg': Wsg}
    _L2_ffn_all = _L2_ffn_setup()
    _L2_ffn_in = {k: v for k, v in _L2_ffn_all.items() if k in ('Wg', 'We_gate', 'We_up', 'We_down', 'Ws_gate', 'Ws_up', 'Ws_down', 'Wsg')}
    del _L2_ffn_all

    def _L3_xattn_setup():
        import jax, jax.numpy as jnp
        import numpy as np
        WIDTH = 256
        DATA_WIDTH = 256
        HEADS = 16
        INIT_SCALE = 0.02
        key = jax.random.key(seed)
        ks = jax.random.split(key, 8)
        x = jax.random.normal(ks[0], (2, 256, WIDTH), dtype=jnp.float32)
        data = jax.random.normal(ks[1], (2, 1024, DATA_WIDTH), dtype=jnp.float32)
        Wq = jax.random.normal(ks[2], (WIDTH, WIDTH), dtype=jnp.float32) * INIT_SCALE
        bq = jnp.zeros((WIDTH,), dtype=jnp.float32)
        Wkv = jax.random.normal(ks[3], (DATA_WIDTH, 2 * WIDTH), dtype=jnp.float32) * INIT_SCALE
        bkv = jnp.zeros((2 * WIDTH,), dtype=jnp.float32)
        Wp = jax.random.normal(ks[4], (WIDTH, WIDTH), dtype=jnp.float32) * INIT_SCALE
        bp = jnp.zeros((WIDTH,), dtype=jnp.float32)
        return {'x': x, 'data': data, 'Wq': Wq, 'bq': bq, 'Wkv': Wkv, 'bkv': bkv, 'Wp': Wp, 'bp': bp}
    _L3_xattn_all = _L3_xattn_setup()
    _L3_xattn_in = {k: v for k, v in _L3_xattn_all.items() if k in ('Wq', 'bq', 'Wkv', 'bkv', 'Wp', 'bp')}
    del _L3_xattn_all

    def _L3_ffn_setup():
        import jax, jax.numpy as jnp
        import numpy as np
        TAU = 1.0
        K_ROUTE = 3
        EPS = 1e-08

        def _route_combine_weights(x_addr, U, k, tau):
            z = x_addr @ U.T
            topv, topi = jax.lax.top_k(z, k)
            w = jax.nn.softmax(topv / (tau + EPS), axis=1)
            N, L = z.shape
            rows = jnp.arange(N)[:, None]
            return jnp.zeros((N, L), z.dtype).at[rows, topi].add(w)

        def _mixture(inp, C, W):
            L = W.shape[0]
            y = jnp.zeros((inp.shape[0], W.shape[1]), inp.dtype)
            for e in range(L):
                y = y + C[:, e:e + 1] * (inp @ W[e].T)
            return y
        key = jax.random.key(seed)
        ks = jax.random.split(key, 8)
        B, T, D_in, H, D_out, L, d_addr = (8, 2048, 256, 256, 256, 12, 64)

        def unit_rows(k, L_, d_):
            U = jax.random.normal(k, (L_, d_), dtype=jnp.float32)
            U = U - U.mean(axis=1, keepdims=True)
            return U / (jnp.linalg.norm(U, axis=1, keepdims=True) + EPS)

        def norm_tape(k, shape):
            W = jax.random.normal(k, shape, dtype=jnp.float32)
            n = jnp.sqrt(jnp.sum(W * W, axis=tuple(range(1, W.ndim)), keepdims=True)) + 1e-12
            return W / n
        x = jax.random.normal(ks[0], (B, T, D_in), dtype=jnp.float32)
        P_w = jax.random.normal(ks[1], (d_addr, D_in), dtype=jnp.float32) / np.sqrt(D_in)
        U1 = unit_rows(ks[2], L, d_addr)
        U2 = unit_rows(ks[3], L, d_addr)
        U3 = unit_rows(ks[4], L, d_addr)
        W1 = norm_tape(ks[5], (L, H, D_in))
        W2 = norm_tape(ks[6], (L, D_out, H))
        b2 = norm_tape(ks[7], (L, D_out))
        return {'x': x, 'P_w': P_w, 'U1': U1, 'U2': U2, 'U3': U3, 'W1': W1, 'W2': W2, 'b2': b2}
    _L3_ffn_all = _L3_ffn_setup()
    _L3_ffn_in = {k: v for k, v in _L3_ffn_all.items() if k in ('P_w', 'U1', 'U2', 'U3', 'W1', 'W2', 'b2')}
    del _L3_ffn_all
    return {'x': x, 'ctx_1024': ctx_1024, 'mask_BxSxS2_ik1': mask_BxSxS2_ik1, 'mask_Bx1x1xS2_ff0': mask_Bx1x1xS2_ff0, 'L0_xattn_wq': _L0_xattn_in['wq'], 'L0_xattn_bq': _L0_xattn_in['bq'], 'L0_xattn_wk': _L0_xattn_in['wk'], 'L0_xattn_bk': _L0_xattn_in['bk'], 'L0_xattn_wv': _L0_xattn_in['wv'], 'L0_xattn_bv': _L0_xattn_in['bv'], 'L0_xattn_wo': _L0_xattn_in['wo'], 'L0_xattn_bo': _L0_xattn_in['bo'], 'L0_ffn_ln1_weight': _L0_ffn_in['ln1_weight'], 'L0_ffn_ln1_bias': _L0_ffn_in['ln1_bias'], 'L0_ffn_ln2_weight': _L0_ffn_in['ln2_weight'], 'L0_ffn_ln2_bias': _L0_ffn_in['ln2_bias'], 'L0_ffn_qkv_weight': _L0_ffn_in['qkv_weight'], 'L0_ffn_proj_weight': _L0_ffn_in['proj_weight'], 'L0_ffn_router_weight': _L0_ffn_in['router_weight'], 'L0_ffn_moe_w1': _L0_ffn_in['moe_w1'], 'L0_ffn_moe_w2': _L0_ffn_in['moe_w2'], 'L1_xattn_W_Q': _L1_xattn_in['W_Q'], 'L1_xattn_W_K': _L1_xattn_in['W_K'], 'L1_xattn_W_V': _L1_xattn_in['W_V'], 'L1_xattn_W_O': _L1_xattn_in['W_O'], 'L1_xattn_b_Q': _L1_xattn_in['b_Q'], 'L1_xattn_b_K': _L1_xattn_in['b_K'], 'L1_xattn_b_V': _L1_xattn_in['b_V'], 'L1_xattn_b_O': _L1_xattn_in['b_O'], 'L1_ffn_router_w': _L1_ffn_in['router_w'], 'L1_ffn_w1': _L1_ffn_in['w1'], 'L1_ffn_w2': _L1_ffn_in['w2'], 'L1_ffn_bias': _L1_ffn_in['bias'], 'L2_xattn_w_sim': _L2_xattn_in['w_sim'], 'L2_xattn_b_sim': _L2_xattn_in['b_sim'], 'L2_xattn_W_qv': _L2_xattn_in['W_qv'], 'L2_xattn_b_qv': _L2_xattn_in['b_qv'], 'L2_ffn_Wg': _L2_ffn_in['Wg'], 'L2_ffn_We_gate': _L2_ffn_in['We_gate'], 'L2_ffn_We_up': _L2_ffn_in['We_up'], 'L2_ffn_We_down': _L2_ffn_in['We_down'], 'L2_ffn_Ws_gate': _L2_ffn_in['Ws_gate'], 'L2_ffn_Ws_up': _L2_ffn_in['Ws_up'], 'L2_ffn_Ws_down': _L2_ffn_in['Ws_down'], 'L2_ffn_Wsg': _L2_ffn_in['Wsg'], 'L3_xattn_Wq': _L3_xattn_in['Wq'], 'L3_xattn_bq': _L3_xattn_in['bq'], 'L3_xattn_Wkv': _L3_xattn_in['Wkv'], 'L3_xattn_bkv': _L3_xattn_in['bkv'], 'L3_xattn_Wp': _L3_xattn_in['Wp'], 'L3_xattn_bp': _L3_xattn_in['bp'], 'L3_ffn_P_w': _L3_ffn_in['P_w'], 'L3_ffn_U1': _L3_ffn_in['U1'], 'L3_ffn_U2': _L3_ffn_in['U2'], 'L3_ffn_U3': _L3_ffn_in['U3'], 'L3_ffn_W1': _L3_ffn_in['W1'], 'L3_ffn_W2': _L3_ffn_in['W2'], 'L3_ffn_b2': _L3_ffn_in['b2']}

def reference(x, ctx_1024, mask_BxSxS2_ik1, mask_Bx1x1xS2_ff0, L0_xattn_wq, L0_xattn_bq, L0_xattn_wk, L0_xattn_bk, L0_xattn_wv, L0_xattn_bv, L0_xattn_wo, L0_xattn_bo, L0_ffn_ln1_weight, L0_ffn_ln1_bias, L0_ffn_ln2_weight, L0_ffn_ln2_bias, L0_ffn_qkv_weight, L0_ffn_proj_weight, L0_ffn_router_weight, L0_ffn_moe_w1, L0_ffn_moe_w2, L1_xattn_W_Q, L1_xattn_W_K, L1_xattn_W_V, L1_xattn_W_O, L1_xattn_b_Q, L1_xattn_b_K, L1_xattn_b_V, L1_xattn_b_O, L1_ffn_router_w, L1_ffn_w1, L1_ffn_w2, L1_ffn_bias, L2_xattn_w_sim, L2_xattn_b_sim, L2_xattn_W_qv, L2_xattn_b_qv, L2_ffn_Wg, L2_ffn_We_gate, L2_ffn_We_up, L2_ffn_We_down, L2_ffn_Ws_gate, L2_ffn_Ws_up, L2_ffn_Ws_down, L2_ffn_Wsg, L3_xattn_Wq, L3_xattn_bq, L3_xattn_Wkv, L3_xattn_bkv, L3_xattn_Wp, L3_xattn_bp, L3_ffn_P_w, L3_ffn_U1, L3_ffn_U2, L3_ffn_U3, L3_ffn_W1, L3_ffn_W2, L3_ffn_b2):
    import jax
    import jax.numpy as jnp

    def _L0_xattn_ref(query, key, value, mask, wq, bq, wk, bk, wv, bv, wo, bo):
        import jax, jax.numpy as jnp
        import numpy as np
        D_MODEL = 256
        N_HEAD = 16
        EPS = 1e-11
        B, S, D = query.shape
        H = N_HEAD
        dk = D // H
        q = query @ wq.T + bq
        k = key @ wk.T + bk
        v = value @ wv.T + bv
        q = q.reshape(B, S, H, dk).transpose(0, 2, 1, 3)
        k = k.reshape(B, S, H, dk).transpose(0, 2, 1, 3)
        v = v.reshape(B, S, H, dk).transpose(0, 2, 1, 3)
        scores = jnp.einsum('bhqd,bhkd->bhqk', q, k) / jnp.sqrt(jnp.float32(dk))
        m = mask[:, None, :, :]
        scores = jnp.where(m == 0, jnp.float32(EPS), scores)
        attn = jax.nn.softmax(scores, axis=-1)
        out = jnp.einsum('bhqk,bhkd->bhqd', attn, v)
        out = out.transpose(0, 2, 1, 3).reshape(B, S, D)
        return out @ wo.T + bo

    def _L0_ffn_ref(hidden_states, ln1_weight, ln1_bias, ln2_weight, ln2_bias, qkv_weight, proj_weight, router_weight, moe_w1, moe_w2):
        import jax, jax.numpy as jnp
        import numpy as np
        EPS = 1e-05
        NUM_HEADS = 16
        NUM_KV_HEADS = 4
        NUM_EXPERTS = 8
        TOP_K = 2

        def _layernorm(x, w, b):
            mu = jnp.mean(x, axis=-1, keepdims=True)
            var = jnp.mean((x - mu) ** 2, axis=-1, keepdims=True)
            return (x - mu) * jax.lax.rsqrt(var + EPS) * w + b
        S, B, H = hidden_states.shape
        hd = H // NUM_HEADS
        rep = NUM_HEADS // NUM_KV_HEADS
        scale = 1.0 / hd ** 0.5
        ln1_out = _layernorm(hidden_states, ln1_weight, ln1_bias)
        qkv = jnp.einsum('sbh,oh->sbo', ln1_out, qkv_weight)
        q = qkv[..., :NUM_HEADS * hd].reshape(S, B, NUM_HEADS, hd)
        k = qkv[..., NUM_HEADS * hd:(NUM_HEADS + NUM_KV_HEADS) * hd].reshape(S, B, NUM_KV_HEADS, hd)
        v = qkv[..., (NUM_HEADS + NUM_KV_HEADS) * hd:].reshape(S, B, NUM_KV_HEADS, hd)
        k = jnp.repeat(k, rep, axis=2)
        v = jnp.repeat(v, rep, axis=2)
        scores = jnp.einsum('sbhd,tbhd->bhst', q, k) * scale
        causal = jnp.tril(jnp.ones((S, S), bool))
        scores = jnp.where(causal, scores, jnp.finfo(scores.dtype).min)
        probs = jax.nn.softmax(scores, axis=-1)
        attn = jnp.einsum('bhst,tbhd->sbhd', probs, v).reshape(S, B, H)
        proj_out = jnp.einsum('sbh,oh->sbo', attn, proj_weight)
        hidden_after_attn = hidden_states + proj_out
        ln2_out = _layernorm(hidden_after_attn, ln2_weight, ln2_bias)
        x = ln2_out.reshape(-1, H)
        logits = jnp.einsum('th,eh->te', x, router_weight)
        gate = jax.nn.softmax(logits, axis=-1)
        top_probs, top_idx = jax.lax.top_k(gate, TOP_K)
        h_mid = jax.nn.gelu(jnp.einsum('th,ehf->etf', x, moe_w1))
        expert_out = jnp.einsum('etf,efh->eth', h_mid, moe_w2)
        e_ids = jnp.arange(NUM_EXPERTS)[:, None, None]
        weights = jnp.sum(jnp.where(top_idx[None] == e_ids, top_probs[None], 0.0), axis=-1)
        moe_out = jnp.einsum('eth,et->th', expert_out, weights).reshape(S, B, H)
        return hidden_after_attn + moe_out

    def _L1_xattn_ref(query_input, key_input, value_input, additive_attention_mask, W_Q, W_K, W_V, W_O, b_Q, b_K, b_V, b_O):
        import jax, jax.numpy as jnp
        import numpy as np
        N_HEADS, D_MODEL, D_HEAD, N_CTX = (16, 256, 64, 512)
        IGNORE = -100000.0
        attn_scale = jnp.float32(np.sqrt(D_HEAD))
        q = jnp.einsum('bpm,hmd->bphd', query_input, W_Q) + b_Q
        k = jnp.einsum('bpm,hmd->bphd', key_input, W_K) + b_K
        v = jnp.einsum('bpm,hmd->bphd', value_input, W_V) + b_V
        attn_scores = jnp.einsum('bqhd,bkhd->bhqk', q, k) / attn_scale
        S_q, S_k = (attn_scores.shape[-2], attn_scores.shape[-1])
        causal = jnp.tril(jnp.ones((N_CTX, N_CTX), bool))[:S_q, :S_k]
        attn_scores = jnp.where(causal, attn_scores, jnp.float32(IGNORE))
        attn_scores = attn_scores + additive_attention_mask
        pattern = jax.nn.softmax(attn_scores, axis=-1)
        z = jnp.einsum('bkhd,bhqk->bqhd', v, pattern)
        out = jnp.einsum('bqhd,hdm->bqm', z, W_O) + b_O
        return out

    def _L1_ffn_ref(x, router_w, w1, w2, bias):
        import jax, jax.numpy as jnp
        import numpy as np
        NUM_EXPERTS = 8
        TOP_K = 2
        CAPACITY_FACTOR = 1.0

        def _dispatch_compute(xf, top_expert, w1, w2, capacity):
            tokens, hs = xf.shape
            tpe = jnp.bincount(top_expert, length=NUM_EXPERTS)
            indices = jnp.argsort(top_expert)
            offsets = jnp.concatenate([jnp.zeros((1,), tpe.dtype), jnp.cumsum(tpe)[:-1]])
            slot = jnp.arange(capacity)
            pos = offsets[:, None] + slot[None, :]
            valid = slot[None, :] < tpe[:, None]
            tok_idx = indices[jnp.minimum(pos, tokens - 1)]
            xe = jnp.where(valid[..., None], xf[tok_idx], 0.0)
            h = jax.nn.gelu(jnp.einsum('ech,ehf->ecf', xe, w1), approximate=True)
            ye = jnp.einsum('ecf,efh->ech', h, w2)
            tok_safe = jnp.where(valid, tok_idx, tokens)
            out = jnp.zeros((tokens + 1, hs), xf.dtype).at[tok_safe.reshape(-1)].add(ye.reshape(-1, hs))
            return out[:tokens]
        sl, bs, hs = x.shape
        tokens = sl * bs
        capacity = int(CAPACITY_FACTOR * tokens / NUM_EXPERTS)
        xf = x.reshape(tokens, hs)
        scores = jax.nn.softmax(xf @ router_w, axis=-1)
        expert_weights, top_experts = jax.lax.top_k(scores, TOP_K)
        out = jnp.zeros_like(xf)
        for k in range(TOP_K):
            y = _dispatch_compute(xf, top_experts[:, k].astype(jnp.int32), w1, w2, capacity)
            out = out + y * expert_weights[:, k][:, None]
        return out.reshape(sl, bs, hs) + bias

    def _L2_xattn_ref(encoder_hc, decoder_hq, w_sim, b_sim, W_qv, b_qv):
        import jax, jax.numpy as jnp
        import numpy as np
        B, L_ENC, L_DEC, D = (16, 128, 128, 256)
        d = encoder_hc.shape[-1]
        w1, w2, w3 = (w_sim[:d], w_sim[d:2 * d], w_sim[2 * d:])
        Sim = (encoder_hc @ w1)[:, :, None] + (decoder_hq @ w2)[:, None, :] + jnp.einsum('bid,bjd->bij', encoder_hc * w3, decoder_hq) + b_sim[0]
        A = jax.nn.softmax(Sim, axis=2)
        hq_hat = jnp.einsum('bij,bjd->bid', A, decoder_hq)
        Batt = jax.nn.softmax(jnp.max(Sim, axis=2), axis=1)
        hc_bar = jnp.einsum('bi,bid->bd', Batt, encoder_hc)[:, None, :]
        hc_hat = jnp.broadcast_to(hc_bar, encoder_hc.shape)
        feats = jnp.concatenate([encoder_hc, hq_hat, encoder_hc * hq_hat, encoder_hc * hc_hat], axis=-1)
        hcq = feats @ W_qv + b_qv
        return hcq

    def _L2_ffn_ref(x, Wg, We_gate, We_up, We_down, Ws_gate, Ws_up, Ws_down, Wsg):
        import jax, jax.numpy as jnp
        import numpy as np
        DIM = 256
        MOE_HID = 128
        SHARED_HID = 512
        N_EXPERTS = 16
        TOP_K = 2
        NORM_TOPK_PROB = True
        B, S, D = x.shape
        xt = x.reshape(-1, D)
        gates = jax.nn.softmax(xt @ Wg.T, axis=-1)
        scores, inds = jax.lax.top_k(gates, TOP_K)
        if NORM_TOPK_PROB:
            scores = scores / jnp.sum(scores, axis=-1, keepdims=True)
        g = jnp.einsum('td,ehd->teh', xt, We_gate)
        u = jnp.einsum('td,ehd->teh', xt, We_up)
        h = jax.nn.silu(g) * u
        y_all = jnp.einsum('teh,edh->ted', h, We_down)
        y_sel = jnp.take_along_axis(y_all, inds[:, :, None], axis=1)
        y = jnp.sum(y_sel * scores[:, :, None], axis=1)
        shared = jax.nn.silu(xt @ Ws_gate.T) * (xt @ Ws_up.T) @ Ws_down.T
        y = y + jax.nn.sigmoid(xt @ Wsg.T) * shared
        return y.reshape(B, S, D)

    def _L3_xattn_ref(x, data, Wq, bq, Wkv, bkv, Wp, bp):
        import jax, jax.numpy as jnp
        import numpy as np
        WIDTH = 256
        DATA_WIDTH = 256
        HEADS = 16
        INIT_SCALE = 0.02
        bs, n_ctx, _ = x.shape
        _, n_data, _ = data.shape
        d = WIDTH // HEADS
        q = (x @ Wq + bq).reshape(bs, n_ctx, HEADS, d)
        kv = (data @ Wkv + bkv).reshape(bs, n_data, HEADS, 2 * d)
        k, v = (kv[..., :d], kv[..., d:])
        scale = 1.0 / np.sqrt(d).astype(np.float32)
        scores = jnp.einsum('bqhd,bkhd->bhqk', q, k) * scale
        attn = jax.nn.softmax(scores, axis=-1)
        out = jnp.einsum('bhqk,bkhd->bqhd', attn, v).reshape(bs, n_ctx, WIDTH)
        return out @ Wp + bp

    def _L3_ffn_ref(x, P_w, U1, U2, U3, W1, W2, b2):
        import jax, jax.numpy as jnp
        import numpy as np
        TAU = 1.0
        K_ROUTE = 3
        EPS = 1e-08

        def _route_combine_weights(x_addr, U, k, tau):
            z = x_addr @ U.T
            topv, topi = jax.lax.top_k(z, k)
            w = jax.nn.softmax(topv / (tau + EPS), axis=1)
            N, L = z.shape
            rows = jnp.arange(N)[:, None]
            return jnp.zeros((N, L), z.dtype).at[rows, topi].add(w)

        def _mixture(inp, C, W):
            L = W.shape[0]
            y = jnp.zeros((inp.shape[0], W.shape[1]), inp.dtype)
            for e in range(L):
                y = y + C[:, e:e + 1] * (inp @ W[e].T)
            return y
        B, T, D = x.shape
        xf = x.reshape(B * T, D)
        xa = xf @ P_w.T
        C1 = _route_combine_weights(xa, U1, K_ROUTE, TAU)
        C2 = _route_combine_weights(xa, U2, K_ROUTE, TAU)
        C3 = _route_combine_weights(xa, U3, K_ROUTE, TAU)
        h = jax.nn.gelu(_mixture(xf, C1, W1), approximate=False)
        y = _mixture(h, C2, W2) + C3 @ b2
        return y.reshape(B, T, -1)
    x = x + _L0_xattn_ref(_layernorm(x, axis=-1), ctx_1024, ctx_1024, mask_BxSxS2_ik1, L0_xattn_wq, L0_xattn_bq, L0_xattn_wk, L0_xattn_bk, L0_xattn_wv, L0_xattn_bv, L0_xattn_wo, L0_xattn_bo)
    x = x + _L0_ffn_ref(_layernorm(x, axis=-1), L0_ffn_ln1_weight, L0_ffn_ln1_bias, L0_ffn_ln2_weight, L0_ffn_ln2_bias, L0_ffn_qkv_weight, L0_ffn_proj_weight, L0_ffn_router_weight, L0_ffn_moe_w1, L0_ffn_moe_w2)
    x = x + _L1_xattn_ref(_layernorm(x, axis=-1), ctx_1024, ctx_1024, mask_Bx1x1xS2_ff0, L1_xattn_W_Q, L1_xattn_W_K, L1_xattn_W_V, L1_xattn_W_O, L1_xattn_b_Q, L1_xattn_b_K, L1_xattn_b_V, L1_xattn_b_O)
    x = x + _L1_ffn_ref(_layernorm(x, axis=-1), L1_ffn_router_w, L1_ffn_w1, L1_ffn_w2, L1_ffn_bias)
    x = x + _L2_xattn_ref(_layernorm(x, axis=-1), ctx_1024, L2_xattn_w_sim, L2_xattn_b_sim, L2_xattn_W_qv, L2_xattn_b_qv)
    x = x + _L2_ffn_ref(_layernorm(x, axis=-1), L2_ffn_Wg, L2_ffn_We_gate, L2_ffn_We_up, L2_ffn_We_down, L2_ffn_Ws_gate, L2_ffn_Ws_up, L2_ffn_Ws_down, L2_ffn_Wsg)
    x = x + _L3_xattn_ref(_layernorm(x, axis=-1), ctx_1024, L3_xattn_Wq, L3_xattn_bq, L3_xattn_Wkv, L3_xattn_bkv, L3_xattn_Wp, L3_xattn_bp)
    x = x + _L3_ffn_ref(_layernorm(x, axis=-1), L3_ffn_P_w, L3_ffn_U1, L3_ffn_U2, L3_ffn_U3, L3_ffn_W1, L3_ffn_W2, L3_ffn_b2)
    return x

_drawn_inputs = setup_inputs


def setup_inputs(seed=0):
    import zlib

    import numpy as np

    out = dict(_drawn_inputs(seed))
    spreads = {'L0_xattn_bq': (0.0, 0.415),
     'L0_xattn_bk': (0.0, 0.8),
     'L0_xattn_bv': (0.0, 0.1),
     'L0_xattn_bo': (0.0, 0.1),
     'L0_ffn_ln1_weight': (1.0, 0.6),
     'L0_ffn_ln1_bias': (0.0, 0.8),
     'L0_ffn_ln2_weight': (1.0, 0.6),
     'L0_ffn_ln2_bias': (0.0, 0.8),
     'L1_xattn_b_Q': (0.0, 0.8),
     'L1_xattn_b_K': (0.0, 2.0),
     'L1_xattn_b_V': (0.0, 0.282),
     'L1_xattn_b_O': (0.0, 0.1),
     'L1_ffn_bias': (0.0, 0.1),
     'L3_xattn_bq': (0.0, 2.0),
     'L3_xattn_bkv': (0.0, 2.0),
     'L3_xattn_bp': (0.0, 0.8)}
    factors = {'L0_ffn_router_weight': 6.692,
     'L0_ffn_moe_w1': 6.042,
     'L0_ffn_moe_w2': 5.897,
     'L1_xattn_W_Q': 8.0,
     'L1_xattn_W_K': 8.0,
     'L1_ffn_router_w': 3.148,
     'L1_ffn_w1': 2.856,
     'L1_ffn_w2': 2.772,
     'L2_xattn_w_sim': 2.675,
     'L2_xattn_b_qv': 5.877,
     'L2_ffn_Wg': 8.0,
     'L2_ffn_We_gate': 8.0,
     'L2_ffn_We_up': 8.0,
     'L2_ffn_We_down': 8.0,
     'L2_ffn_Ws_gate': 8.0,
     'L2_ffn_Ws_up': 8.0,
     'L2_ffn_Ws_down': 8.0,
     'L2_ffn_Wsg': 8.0,
     'L3_xattn_Wq': 64.0,
     'L3_ffn_P_w': 10.351,
     'L3_ffn_U1': 41.35,
     'L3_ffn_U2': 39.182,
     'L3_ffn_U3': 12.992,
     'L3_ffn_W1': 40.195,
     'L3_ffn_W2': 37.626,
     'L3_ffn_b2': 11.151,
     'L3_xattn_Wkv': 8.0,
     'L3_xattn_Wp': 3.616}
    for name, (base, spread) in spreads.items():
        noise = np.random.default_rng([zlib.crc32(name.encode()), seed]).standard_normal(out[name].shape)
        drawn = base * np.exp(spread * noise) if base else spread * noise
        out[name] = jnp.asarray(drawn.astype(out[name].dtype))
    for name, factor in factors.items():
        out[name] = (out[name] * factor).astype(out[name].dtype)
    return out
```

```python
import concourse.bass as bass
from concourse import mybir
from contextlib import ExitStack

F32 = mybir.dt.float32
BF16 = mybir.dt.bfloat16
I32 = mybir.dt.int32
U32 = mybir.dt.uint32
ALU = mybir.AluOpType
ACT = mybir.ActivationFunctionType
AX = mybir.AxisListType

P = 128
D = 256
DC = D // P
B = 4
S = 512
T = B * S
NT = T // P
QT = S // P
BIG = -1.0e30
EPS = 1e-5

H16 = 16
HD = 16
GH = 4
NG = H16 // GH
NPART = 3
Q_PARTS = (0, 0, 1, 0, 2, 1)
K_PARTS = (0, 1, 0, 2, 0, 1)
KR = len(Q_PARTS) * HD
MR = NPART * GH


class Stage:

    USED = []

    def __init__(self, nc, name):
        self.nc, self.name, self.ctx, self.sems = nc, name, ExitStack(), []

    def __enter__(self):
        self.ctx.__enter__()
        return self

    def __exit__(self, *a):
        self.ctx.__exit__(*a)
        self.USED.extend(self.sems)
        if len(self.USED) > 150:
            self.nc.clear_and_free_semaphores(list(self.USED))
            self.nc.all_engine_barrier()
            self.USED.clear()

    def sb(self, name, shape, dt=F32):
        return self.ctx.enter_context(self.nc.sbuf_tensor(f"{self.name}_{name}", shape, dt))

    def ps(self, name, shape, dt=F32):
        return self.ctx.enter_context(self.nc.psum_tensor(f"{self.name}_{name}", shape, dt))

    def sem(self, name):
        self.sems.append(self.nc.alloc_semaphore(f"{self.name}_{name}"))
        return self.sems[-1]

    def block(self):
        return self.ctx.enter_context(self.nc.Block())


class InOrder:

    def __init__(self, eng, sem):
        self.eng, self.sem, self.n = eng, sem, 0

    def after(self, ins):
        self.n += 1
        ins.then_inc(self.sem, 1)
        self.eng.wait_ge(self.sem, self.n)


def layernorm(nc, name, x, xn, xnT, ident, affine=None):
    with Stage(nc, name) as st:
        stats = st.sb("stats", [P, NT, 6])
        mv = st.sb("mv", [P, NT, 2])
        ve = st.sb("ve", [P, NT])
        std = st.sb("std", [P, NT])
        rstd = st.sb("rstd", [P, NT])
        wb = st.sb("wb", [P, 2, DC])
        tp = [st.ps(f"tp{i}", [P, S]) for i in range(4)]
        s_own, s_var, s_std, s_norm, s_tr, s_ev, s_wb = (
            st.sem(n) for n in ("own", "var", "std", "norm", "tr", "ev", "wb"))
        block = st.block()

        @block.sync
        def _(sp):
            if affine is not None:
                for i in range(2):
                    for c in range(DC):
                        sp.dma_start(wb[:, i, c:c + 1], affine[i][c * P:(c + 1) * P].unsqueeze(1)).then_inc(s_wb, 16)

        @block.vector
        def _(dve):
            own = InOrder(dve, s_own)
            for t in range(NT):
                last = nc.vector.bn_stats(stats[:, t, :], x[:, t, :])
            own.after(last)
            for t in range(NT):
                last = nc.vector.bn_aggr(mv[:, t, :], stats[:, t, :])
            own.after(last)
            nc.vector.tensor_scalar(ve[:, :], mv[:, :, 1], EPS, None, ALU.add).then_inc(s_var, 1)
            dve.wait_ge(s_std, 1)
            own.after(nc.vector.reciprocal(rstd[:, :], std[:, :]))
            for t in range(NT):
                nc.vector.tensor_scalar(xn[:, t, :], x[:, t, :], mv[:, t, 0:1], rstd[:, t:t + 1],
                                        ALU.subtract, ALU.mult).then_inc(s_norm, 1)

        @block.tensor
        def _(pe):
            for n in range(B * DC):
                g, c = n // DC, n % DC
                pe.wait_ge(s_norm, QT * (g + 1))
                if n >= 4:
                    pe.wait_ge(s_ev, n - 3)
                for i in range(QT):
                    last = nc.tensor.transpose(tp[n % 4][:, i * P:(i + 1) * P],
                                               xn[:, g * QT + i, c * P:(c + 1) * P], ident[:, :])
                last.then_inc(s_tr, 1)

        @block.scalar
        def _(act):
            act.wait_ge(s_var, 1)
            nc.scalar.activation(std[:, :], ve[:, :], ACT.Sqrt).then_inc(s_std, 1)
            if affine is not None:
                act.wait_ge(s_wb, 16 * 2 * DC)
            for n in range(B * DC):
                g, c = n // DC, n % DC
                act.wait_ge(s_tr, n + 1)
                dst = xnT[:, c, g * S:(g + 1) * S]
                if affine is None:
                    nc.scalar.activation(dst, tp[n % 4][:, :], ACT.Identity).then_inc(s_ev, 1)
                else:
                    nc.scalar.activation(dst, tp[n % 4][:, :], ACT.Identity, bias=wb[:, 1, c:c + 1],
                                         scale=wb[:, 0, c:c + 1]).then_inc(s_ev, 1)


def project16(nc, name, srcT_q, srcT_kv, w, scratch):
    qp, kp, vp = scratch
    scale = HD ** -0.5
    with Stage(nc, name) as st:
        wsb = {k: st.sb("w" + k, [P, DC, D]) for k in "qkv"}
        bqk = st.sb("bqk", [P, 2, DC])
        bv = st.sb("bv", [P, D])
        full = st.sb("full", [P, 2, S])
        rest = st.sb("rest", [P, 2, S])
        parts = st.sb("parts", [P, 2, NPART, S], BF16)
        vt = st.sb("vt", [P, 2, H16, 32])
        pj = [st.ps(f"pj{i}", [P, S]) for i in range(4)]
        pv = [st.ps(f"pv{i}", [P, D]) for i in range(2)]
        s_w, s_pj, s_full, s_hi, s_rest, s_mid, s_low, s_pv, s_vt, s_own = (
            st.sem(n) for n in ("w", "pj", "full", "hi", "rest", "mid", "low", "pv", "vt", "own"))
        s_out = [st.sem(f"out{i}") for i in range(2)]
        s_vo = [st.sem(f"vo{i}") for i in range(2)]
        JOBS = [(k, hb, b) for b in range(B) for k in range(2) for hb in range(DC)]
        block = st.block()

        @block.sync
        def _(sp):
            for k in "qkv":
                sp.dma_start(wsb[k][:, :, :], w["w" + k].rearrange("(c p) n -> p c n", p=P)).then_inc(s_w, 16)
            for i, k in enumerate("qk"):
                for c in range(DC):
                    sp.dma_start(bqk[:, i, c:c + 1], w["b" + k][c * P:(c + 1) * P].unsqueeze(1)).then_inc(s_w, 16)
            sp.dma_start(bv[:, :], w["bv"].partition_broadcast(P)).then_inc(s_w, 16)
            for j, (k, hb, b) in enumerate(JOBS):
                sp.wait_ge(s_low, j + 1)
                dst = (qp, kp)[k][:, hb * P:(hb + 1) * P, b * S:(b + 1) * S].rearrange("a p n -> p a n")
                sp.dma_start(dst, parts[:, j % 2, :, :]).then_inc(s_out[j % 2], 16)
            for i in range(2):
                sp.wait_ge(s_out[i], 16 * (len(JOBS) // 2))
                sp.wait_ge(s_vo[i], 16 * (NT // 2))

        @block.tensor
        def _(pe):
            pe.wait_ge(s_w, 16 * 8)
            for j, (k, hb, b) in enumerate(JOBS):
                if j >= 4:
                    pe.wait_ge(s_full, j - 3)
                src = (srcT_q, srcT_kv)[k]
                for c in range(DC):
                    last = nc.tensor.matmul(pj[j % 4][:, :], wsb["qk"[k]][:, c, hb * P:(hb + 1) * P],
                                            src[:, c, b * S:(b + 1) * S], start=(c == 0), stop=(c == DC - 1))
                last.then_inc(s_pj, 1)
                t = j
                if t >= 2:
                    pe.wait_ge(s_vt, t - 1)
                for c in range(DC):
                    last = nc.tensor.matmul(pv[t % 2][:, :], srcT_kv[:, c, t * P:(t + 1) * P],
                                            wsb["v"][:, c, :], start=(c == 0), stop=(c == DC - 1))
                last.then_inc(s_pv, 1)

        @block.vector
        def _(dve):
            own = InOrder(dve, s_own)
            own.after(nc.vector.memset(vt[:, :, :, :], 0.0))
            own.after(nc.vector.memset(vt[:, :, :, HD:HD + 1], 1.0))
            dve.wait_ge(s_w, 16 * 8)
            for j, (k, hb, b) in enumerate(JOBS):
                dve.wait_ge(s_pj, j + 1)
                if j >= 2:
                    dve.wait_ge(s_low, j - 1)
                nc.vector.tensor_scalar(full[:, j % 2, :], pj[j % 4][:, :], bqk[:, k, hb:hb + 1],
                                        scale if k == 0 else 1.0, ALU.add, ALU.mult).then_inc(s_full, 1)
                dve.wait_ge(s_hi, j + 1)
                nc.vector.tensor_tensor(rest[:, j % 2, :], full[:, j % 2, :], parts[:, j % 2, 0, :],
                                        ALU.subtract).then_inc(s_rest, 1)
                dve.wait_ge(s_pv, j + 1)
                if j >= 2:
                    dve.wait_ge(s_vo[j % 2], 16 * (j // 2))
                nc.vector.tensor_tensor(vt[:, j % 2, :, 0:HD], pv[j % 2][:, :].rearrange("p (h d) -> p h d", h=H16),
                                        bv[:, :].rearrange("p (h d) -> p h d", h=H16), ALU.add).then_inc(s_vt, 1)

        @block.scalar
        def _(act):
            for j in range(len(JOBS)):
                act.wait_ge(s_full, j + 1)
                if j >= 2:
                    act.wait_ge(s_out[j % 2], 16 * (j // 2))
                nc.scalar.activation(parts[:, j % 2, 0, :], full[:, j % 2, :], ACT.Identity).then_inc(s_hi, 1)
                act.wait_ge(s_rest, j + 1)
                nc.scalar.activation(parts[:, j % 2, 1, :], rest[:, j % 2, :], ACT.Identity).then_inc(s_mid, 1)

        @block.gpsimd
        def _(pool):
            for j in range(len(JOBS)):
                pool.wait_ge(s_mid, j + 1)
                nc.gpsimd.tensor_tensor(parts[:, j % 2, 2, :], rest[:, j % 2, :], parts[:, j % 2, 1, :],
                                        ALU.subtract).then_inc(s_low, 1)
                pool.wait_ge(s_vt, j + 1)
                pool.dma_start(vp[j * P:(j + 1) * P, :], vt[:, j % 2, :, :].rearrange("p h d -> p (h d)")
                               ).then_inc(s_vo[j % 2], 16)


def masks16(nc, name, mask, maskT, vp, neg_q, neg_k, any_masked, vmasked):
    with Stage(nc, name) as st:
        mi = st.sb("mi", [P, 2, S], I32)
        mk = st.sb("mk", [P, QT, S], I32)
        zk = st.sb("zk", [P, QT, S])
        vs = st.sb("vs", [P, QT, H16 * 32])
        vm = [st.ps(f"vm{i}", [P, S]) for i in range(2)]
        s_mi = [st.sem(f"mi{i}") for i in range(2)]
        s_q, s_mk, s_vs, s_z, s_vm, s_own, s_vsum, s_row = (
            st.sem(n) for n in ("q", "mk", "vs", "z", "vm", "own", "vsum", "row"))
        block = st.block()

        @block.sync
        def _(sp):
            for t in range(NT):
                if t >= 2:
                    sp.wait_ge(s_row, t - 1)
                sp.dma_start(mi[:, t % 2, :], mask[t // QT, (t % QT) * P:(t % QT + 1) * P, :]).then_inc(s_mi[t % 2], 16)

        @block.scalar
        def _(act):
            for b in range(B):
                if b >= 1:
                    act.wait_ge(s_z, 2 * QT * b)
                    act.wait_ge(s_vm, NG * b)
                act.dma_start(mk[:, :, :], maskT[b].rearrange("(t p) q -> p t q", p=P)).then_inc(s_mk, 16)
                act.dma_start(vs[:, :, :], vp[b * S:(b + 1) * S, :].rearrange("(t p) n -> p t n", p=P)
                              ).then_inc(s_vs, 16)
                for g in range(NG):
                    n = b * NG + g
                    act.wait_ge(s_vm, n + 1)
                    nc.scalar.activation(vmasked[:, n, :], vm[n % 2][:, :], ACT.Identity).then_inc(s_vsum, 1)

        @block.vector
        def _(dve):
            for t in range(NT):
                dve.wait_ge(s_mi[t % 2], 16 * (t // 2 + 1))
                nc.vector.tensor_scalar(neg_q[:, t, :], mi[:, t % 2, :], 0.0, BIG, ALU.is_equal, ALU.mult
                                        ).then_inc(s_q, 1)
                dve.wait_ge(s_q, t + 1)
                nc.vector.tensor_reduce(any_masked[:, t:t + 1], neg_q[:, t, :], AX.X, ALU.min).then_inc(s_row, 1)
            dve.wait_ge(s_row, NT)
            own = InOrder(dve, s_own)
            own.after(nc.vector.tensor_scalar(any_masked[:, :], any_masked[:, :], 0.0, BIG, ALU.is_equal, ALU.mult))
            own.after(nc.vector.tensor_scalar(any_masked[:, :], any_masked[:, :], 1e-11, None, ALU.add))
            for b in range(B):
                dve.wait_ge(s_mk, 16 * (b + 1))
                if b >= 1:
                    dve.wait_ge(s_vm, NG * b)
                for t in range(QT):
                    nc.vector.tensor_scalar(neg_k[:, b * QT + t, :], mk[:, t, :], 0.0, BIG, ALU.is_equal, ALU.mult
                                            ).then_inc(s_z, 1)
                    nc.vector.tensor_scalar(zk[:, t, :], mk[:, t, :], 0.0, None, ALU.is_equal).then_inc(s_z, 1)

        @block.tensor
        def _(pe):
            for b in range(B):
                pe.wait_ge(s_z, 2 * QT * (b + 1))
                pe.wait_ge(s_vs, 16 * (b + 1))
                for g in range(NG):
                    n = b * NG + g
                    if n >= 2:
                        pe.wait_ge(s_vsum, n - 1)
                    for t in range(QT):
                        last = nc.tensor.matmul(vm[n % 2][:, :], vs[:, t, g * P:(g + 1) * P], zk[:, t, :],
                                                start=(t == 0), stop=(t == QT - 1))
                    last.then_inc(s_vm, 1)


def attend16(nc, name, scratch, consts, outT, masks=None):
    qp, kp, vp = scratch
    ident, identb, sel_head, sel_sum = consts
    N = B * NG
    with Stage(nc, name) as st:
        qs = st.sb("qs", [P, 2, GH, S], BF16)
        ks = st.sb("ks", [P, 2, GH, S], BF16)
        vs = st.sb("vs", [P, 2, QT, P])
        junk = st.sb("junk", [P, 2, S], BF16)
        rowmax = st.sb("rowmax", [P, 2, QT, GH])
        neg = st.sb("neg", [P, 2, QT, GH])
        negr = st.sb("negr", [P, QT, GH])
        negp = st.sb("negp", [P, QT, P], BF16)
        prob = st.sb("prob", [P, 2, GH, 2, S])
        expand = st.sb("expand", [P, QT, GH, 32])
        em = st.sb("em", [P, QT, GH])
        rec = st.sb("rec", [P, QT, GH])
        oT = st.sb("oT", [P, S])
        sq = [st.ps(f"sq{i}", [P, S]) for i in range(2)]
        sk = [st.ps(f"sk{i}", [P, 2, S]) for i in range(2)]
        acc = st.ps("acc", [P, S])
        misc = st.ps("misc", [P, S])
        miscb = misc[:, :].bitcast(BF16)[:, 0:S]
        s_q = [st.sem(f"q{i}") for i in range(2)]
        s_v = [st.sem(f"v{i}") for i in range(2)]
        (s_sq, s_max, s_negp, s_mt, s_qm, s_sk, s_exp, s_pv, s_em, s_ex, s_eb, s_o,
         s_sum, s_rec, s_rb, s_out, s_own, s_am, s_hd) = (
            st.sem(n) for n in ("sq", "max", "negp", "mt", "qm", "sk", "exp", "pv", "em",
                                "ex", "eb", "o", "sum", "rec", "rb", "out", "own", "am", "hd"))
        block = st.block()
        NB = 1 if masks is None else 2

        @block.sync
        def _(sp):
            for i in range(2):
                sp.dma_start(ks[KR:KR + MR, i, :, :], sel_head).then_inc(s_hd, 16)
            for n in range(N):
                b, g = n // NG, n % NG
                if n >= 2:
                    sp.wait_ge(s_sk, 8 * (n - 1))
                for buf, src, order in ((qs, qp, Q_PARTS), (ks, kp, K_PARTS)):
                    for r, a in enumerate(order):
                        sp.dma_start(buf[r * HD:(r + 1) * HD, n % 2, :, :],
                                     src[a, g * GH * HD:(g + 1) * GH * HD, b * S:(b + 1) * S]
                                     .rearrange("(h d) n -> d h n", h=GH)).then_inc(s_q[n % 2], 16)
                if n >= 2:
                    sp.wait_ge(s_pv, 2 * (n - 1))
                sp.dma_start(vs[:, n % 2, :, :], vp[b * S:(b + 1) * S, g * P:(g + 1) * P]
                             .rearrange("(t p) n -> p t n", p=P)).then_inc(s_v[n % 2], 16)

        @block.tensor
        def _(pe):
            def row_scores(n, i):
                h, t = i // QT, i % QT
                k = n * GH * QT + i
                if k >= 2:
                    pe.wait_ge(s_max, k - 1)
                nc.tensor.matmul(sq[k % 2][:, :], qs[0:KR, n % 2, h, t * P:(t + 1) * P], ks[0:KR, n % 2, h, :],
                                 start=True, stop=True).then_inc(s_sq, 1)

            def turn_max(n):
                pe.wait_ge(s_negp, n + 1)
                if n >= 1:
                    pe.wait_ge(s_out, n)
                for t in range(QT):
                    last = nc.tensor.transpose(miscb[:, t * P:(t + 1) * P], negp[:, t, :], identb[:, :])
                last.then_inc(s_mt, 1)

            def key_scores(n, u):
                h, k = u % GH, n * 8 + u
                if k >= 2:
                    pe.wait_ge(s_exp, k - 1)
                for i in range(2):
                    t = 2 * (u // GH) + i
                    last = nc.tensor.matmul(sk[k % 2][:, i, :], ks[0:KR + MR, n % 2, h, t * P:(t + 1) * P],
                                            qs[0:KR + MR, n % 2, h, :], start=True, stop=(masks is None))
                    if masks is not None:
                        last = nc.tensor.matmul(sk[k % 2][:, i, :], identb[:, :],
                                                masks["neg_k"][:, (n // NG) * QT + t, :], start=False, stop=True)
                last.then_inc(s_sk, 1)

            def values(n, half):
                pe.wait_ge(s_exp, n * 8 + 4 * half + 4)
                if half == 0:
                    pe.wait_ge(s_v[n % 2], 16 * (n // 2 + 1))
                    if n >= 1:
                        pe.wait_ge(s_o, n)
                for i in range(2):
                    for h in range(GH):
                        t = 2 * half + i
                        last = nc.tensor.matmul(acc[32 * h:32 * h + 32, :], vs[:, n % 2, t, 32 * h:32 * h + 32],
                                                prob[:, half, h, i, :], start=(t == 0), stop=(t == QT - 1),
                                                tile_position=(0, 32 * h), skip_group_check=True)
                last.then_inc(s_pv, 1)

            def broadcast(n, which):
                pe.wait_ge(s_ex, NB * n + which + 1)
                for t in range(QT):
                    last = nc.tensor.transpose(misc[:, t * P:(t + 1) * P],
                                               expand[:, t, :, :].rearrange("p h d -> p (h d)"), ident[:, :])
                last.then_inc(s_rb if which == NB - 1 else s_eb, 1)

            def sums(n):
                pe.wait_ge(s_o, n + 1)
                for t in range(QT):
                    last = nc.tensor.matmul(misc[:, t * GH:(t + 1) * GH], oT[:, t * P:(t + 1) * P], sel_sum[:, :],
                                            start=True, stop=True)
                last.then_inc(s_sum, 1)

            for n in range(N + 1):
                if n < N:
                    pe.wait_ge(s_q[n % 2], 16 * 12 * (n // 2 + 1))
                if n == 0:
                    pe.wait_ge(s_hd, 32)
                for u in range(8):
                    if n >= 1:
                        if u == 0:
                            pe.wait_ge(s_qm, n)
                        key_scores(n - 1, u)
                        if u == 5:
                            values(n - 1, 0)
                    if n < N:
                        row_scores(n, 2 * u)
                        row_scores(n, 2 * u + 1)
                if n >= 1:
                    values(n - 1, 1)
                    if masks is not None:
                        broadcast(n - 1, 0)
                    sums(n - 1)
                    broadcast(n - 1, NB - 1)
                if n < N:
                    turn_max(n)

        @block.vector
        def _(dve):
            own = InOrder(dve, s_own)
            own.after(nc.vector.memset(negp[:, :, :], 0.0))

            def row_max(n, i):
                h, t = i // QT, i % QT
                k = n * GH * QT + i
                dve.wait_ge(s_sq, k + 1)
                dst = rowmax[:, n % 2, t, h:h + 1]
                if masks is None:
                    ins = nc.vector.tensor_reduce(dst, sq[k % 2][:, :], AX.X, ALU.max)
                else:
                    if k >= 2:
                        dve.wait_ge(s_max, k - 1)
                    ins = nc.vector.tensor_tensor_reduce(junk[:, k % 2, :], sq[k % 2][:, :],
                                                         masks["neg_q"][:, (n // NG) * QT + t, :], 1.0, 3.0 * BIG,
                                                         ALU.add, ALU.max, dst)
                ins.then_inc(s_max, 1)

            def minus_max(n):
                dve.wait_ge(s_max, GH * QT * (n + 1))
                m, x = rowmax[:, n % 2, :, :], neg[:, n % 2, :, :]
                if masks is not None:
                    for t in range(QT):
                        c = (n // NG) * QT + t
                        last = nc.vector.tensor_scalar(m[:, t, :], m[:, t, :], masks["any_masked"][:, c:c + 1], None,
                                                       ALU.max)
                    own.after(last)
                if n >= 2 and masks is not None:
                    dve.wait_ge(s_em, n - 1)
                own.after(nc.vector.tensor_scalar(x, m, -1.0, None, ALU.mult))
                if n >= 1:
                    dve.wait_ge(s_mt, n)
                part = [negp[:, :, KR + a * GH:KR + (a + 1) * GH] for a in range(NPART)]
                own.after(nc.vector.tensor_copy(part[0], x))
                own.after(nc.vector.tensor_tensor(negr[:, :, :], x, part[0], ALU.subtract))
                own.after(nc.vector.tensor_copy(part[1], negr[:, :, :]))
                nc.vector.tensor_tensor(part[2], negr[:, :, :], part[1], ALU.subtract).then_inc(s_negp, 1)

            def finish(n):
                if masks is not None:
                    dve.wait_ge(s_em, n + 1)
                    if n >= 1:
                        dve.wait_ge(s_rb, n)
                    nc.vector.tensor_copy(expand[:, :, :, :], em[:, :, :].unsqueeze(3).to_broadcast([P, QT, GH, 32])
                                          ).then_inc(s_ex, 1)
                    dve.wait_ge(s_eb, n + 1)
                    own.after(nc.vector.tensor_tensor(oT[:, :], misc[:, :], masks["vmasked"][:, n, :], ALU.mult))
                    dve.wait_ge(s_pv, 2 * (n + 1))
                    nc.vector.tensor_tensor(oT[:, :], acc[:, :], oT[:, :], ALU.add).then_inc(s_o, 1)
                else:
                    dve.wait_ge(s_pv, 2 * (n + 1))
                    nc.vector.tensor_copy(oT[:, :], acc[:, :]).then_inc(s_o, 1)
                dve.wait_ge(s_sum, n + 1)
                own.after(nc.vector.reciprocal(rec[:, :, :], misc[:, 0:QT * GH].rearrange("p (t h) -> p t h", t=QT)))
                if masks is None and n >= 1:
                    dve.wait_ge(s_rb, n)
                nc.vector.tensor_copy(expand[:, :, :, :], rec[:, :, :].unsqueeze(3).to_broadcast([P, QT, GH, 32])
                                      ).then_inc(s_ex, 1)
                dve.wait_ge(s_rb, n + 1)
                nc.vector.tensor_tensor(outT[:, n, :], oT[:, :], misc[:, :], ALU.mult).then_inc(s_out, 1)

            for n in range(N + 1):
                if n < N:
                    for i in range(GH * QT):
                        row_max(n, i)
                    minus_max(n)
                if n >= 1:
                    finish(n - 1)

        @block.scalar
        def _(act):
            for n in range(N + 1):
                if n >= 1:
                    for u in range(8):
                        k = (n - 1) * 8 + u
                        act.wait_ge(s_sk, k + 1)
                        if n >= 2:
                            act.wait_ge(s_pv, 2 * (n - 2) + u // GH + 1)
                        nc.scalar.activation(prob[:, u // GH, u % GH, :, :], sk[k % 2][:, :, :], ACT.Exp
                                             ).then_inc(s_exp, 1)
                    if masks is not None:
                        if n >= 2:
                            act.wait_ge(s_ex, NB * (n - 2) + 1)
                        act.wait_ge(s_negp, n)
                        nc.scalar.activation(em[:, :, :], neg[:, (n - 1) % 2, :, :], ACT.Exp, bias=masks["tiny"][:, 0:1]
                                             ).then_inc(s_em, 1)
                if n < N:
                    act.wait_ge(s_mt, n + 1)
                    for h in range(GH):
                        last = nc.scalar.activation(qs[KR:KR + MR, n % 2, h, :], miscb[KR:KR + MR, :], ACT.Identity)
                    last.then_inc(s_qm, 1)


def output16(nc, name, aT, wo, bo, x):
    with Stage(nc, name) as st:
        w = st.sb("w", [P, NG, D])
        bb = st.sb("bb", [P, D])
        pp = [st.ps(f"pp{i}", [P, D]) for i in range(4)]
        s_w, s_p, s_x, s_b = (st.sem(n) for n in ("w", "p", "x", "b"))
        block = st.block()

        @block.sync
        def _(sp):
            sp.dma_start(w[:, :, :], wo.rearrange("(g p) n -> p g n", p=P)).then_inc(s_w, 16)
            sp.dma_start(bb[:, :], bo.partition_broadcast(P)).then_inc(s_w, 16)

        @block.tensor
        def _(pe):
            pe.wait_ge(s_w, 32)
            for t in range(NT):
                if t >= 4:
                    pe.wait_ge(s_x, t - 3)
                for g in range(NG):
                    last = nc.tensor.matmul(pp[t % 4][:, :], aT[:, (t // QT) * NG + g, (t % QT) * P:(t % QT + 1) * P],
                                            w[:, g, :], start=(g == 0), stop=(g == NG - 1))
                last.then_inc(s_p, 1)

        @block.vector
        def _(dve):
            dve.wait_ge(s_w, 32)
            for t in range(NT):
                nc.vector.tensor_tensor(x[:, t, :], x[:, t, :], bb[:, :], ALU.add).then_inc(s_b, 1)
            for t in range(NT):
                dve.wait_ge(s_b, t + 1)
                dve.wait_ge(s_p, t + 1)
                nc.vector.tensor_tensor(x[:, t, :], x[:, t, :], pp[t % 4][:, :], ALU.add).then_inc(s_x, 1)


def transpose_rows(nc, name, src, dstT, ident):
    with Stage(nc, name) as st:
        tp = [st.ps(f"tp{i}", [P, S]) for i in range(4)]
        s_tr, s_ev = st.sem("tr"), st.sem("ev")
        block = st.block()

        @block.tensor
        def _(pe):
            for n in range(B * DC):
                g, c = n // DC, n % DC
                if n >= 4:
                    pe.wait_ge(s_ev, n - 3)
                for i in range(QT):
                    last = nc.tensor.transpose(tp[n % 4][:, i * P:(i + 1) * P],
                                               src[:, g * QT + i, c * P:(c + 1) * P], ident[:, :])
                last.then_inc(s_tr, 1)

        @block.scalar
        def _(act):
            for n in range(B * DC):
                g, c = n // DC, n % DC
                act.wait_ge(s_tr, n + 1)
                nc.scalar.activation(dstT[:, c, g * S:(g + 1) * S], tp[n % 4][:, :], ACT.Identity).then_inc(s_ev, 1)


def small_attention(nc, name, srcT, wqkv, att):
    HK = 4
    R = H16 // HK
    SL = B
    NB = NT // SL
    W = (H16 + 2 * HK) * HD
    PAIRS = [(s, t) for s in range(SL) for t in range(s + 1)]
    with Stage(nc, name) as st:
        w = st.sb("w", [P, DC, W])
        qkv = st.sb("qkv", [P, NT, W])
        prod = st.sb("prod", [P, 2, NB, H16 * HD])
        sc = st.sb("sc", [P, len(PAIRS), NB * H16])
        mx = st.sb("mx", [P, SL, NB * H16])
        pp = [st.ps(f"pp{i}", [P, W]) for i in range(4)]
        s_w, s_p, s_ev, s_own, s_sc, s_ex = (st.sem(n) for n in ("w", "p", "ev", "own", "sc", "ex"))
        block = st.block()

        def q(s, b):
            return qkv[:, s * NB + b, 0:H16 * HD].rearrange("p (g r d) -> p g r d", g=HK, r=R)

        def kv(s, b, which):
            lo = (H16 + which * HK) * HD
            v = qkv[:, s * NB + b, lo:lo + HK * HD].rearrange("p (g d) -> p g d", g=HK)
            return v.unsqueeze(2).to_broadcast([P, HK, R, HD])

        @block.sync
        def _(sp):
            sp.dma_start(w[:, :, :], cols(wqkv)).then_inc(s_w, 16)

        @block.tensor
        def _(pe):
            pe.wait_ge(s_w, 16)
            for t in range(NT):
                if t >= 4:
                    pe.wait_ge(s_ev, t - 3)
                for c in range(DC):
                    last = nc.tensor.matmul(pp[t % 4][:, :], srcT[:, c, t * P:(t + 1) * P], w[:, c, :],
                                            start=(c == 0), stop=(c == DC - 1))
                last.then_inc(s_p, 1)

        @block.scalar
        def _(act):
            for t in range(NT):
                act.wait_ge(s_p, t + 1)
                nc.scalar.activation(qkv[:, t, :], pp[t % 4][:, :], ACT.Identity).then_inc(s_ev, 1)
            act.wait_ge(s_sc, 1)
            nc.scalar.activation(sc[:, :, :], sc[:, :, :], ACT.Exp, scale=HD ** -0.5).then_inc(s_ex, 1)

        @block.vector
        def _(dve):
            own = InOrder(dve, s_own)
            dve.wait_ge(s_ev, NT)
            for i, (s, t) in enumerate(PAIRS):
                for b in range(NB):
                    last = nc.vector.tensor_tensor(prod[:, i % 2, b, :].rearrange("p (g r d) -> p g r d", g=HK, r=R),
                                                   q(s, b), kv(t, b, 0), ALU.mult)
                own.after(last)
                last = nc.vector.tensor_reduce(sc[:, i, :], prod[:, i % 2, :, :].rearrange("p b (h d) -> p (b h) d", h=H16),
                                        AX.X, ALU.add)
            own.after(last)
            first = [s * (s + 1) // 2 for s in range(SL + 1)]
            for s in range(SL):
                last = nc.vector.tensor_reduce(mx[:, s, :], sc[:, first[s]:first[s + 1], :].rearrange("p t n -> p n t"),
                                               AX.X, ALU.max)
            own.after(last)
            for s in range(SL):
                v = sc[:, first[s]:first[s + 1], :]
                last = nc.vector.tensor_tensor(v, v, mx[:, s, :].unsqueeze(1).to_broadcast([P, s + 1, NB * H16]),
                                               ALU.subtract)
            last.then_inc(s_sc, 1)
            dve.wait_ge(s_ex, 1)
            for s in range(SL):
                last = nc.vector.tensor_reduce(mx[:, s, :], sc[:, first[s]:first[s + 1], :].rearrange("p t n -> p n t"),
                                               AX.X, ALU.add)
            own.after(last)
            own.after(nc.vector.reciprocal(mx[:, :, :], mx[:, :, :]))
            for s in range(SL):
                v = sc[:, first[s]:first[s + 1], :]
                last = nc.vector.tensor_tensor(v, v, mx[:, s, :].unsqueeze(1).to_broadcast([P, s + 1, NB * H16]),
                                               ALU.mult)
            own.after(last)
            for i, (s, t) in enumerate(PAIRS):
                prob = sc[:, i, :].rearrange("p (b g r) -> p b g r", b=NB, g=HK)
                for b in range(NB):
                    dst = att[:, s * NB + b, :] if t == 0 else prod[:, i % 2, b, :]
                    last = nc.vector.tensor_tensor(dst.rearrange("p (g r d) -> p g r d", g=HK, r=R), kv(t, b, 1),
                                                   prob[:, b].unsqueeze(3).to_broadcast([P, HK, R, HD]), ALU.mult)
                own.after(last)
                if t > 0:
                    a = att[:, s * NB:(s + 1) * NB, :]
                    last = nc.vector.tensor_tensor(a, a, prod[:, i % 2, :, :], ALU.add)
            own.after(last)


def project_rows(nc, name, srcT, w_dram, tiles_out):
    with Stage(nc, name) as st:
        K = w_dram.shape[0] // P
        w = st.sb("w", [P, K, w_dram.shape[1]])
        pp = [st.ps(f"pp{i}", [P, w_dram.shape[1]]) for i in range(4)]
        s_w, s_p, s_ev, s_own = (st.sem(n) for n in ("w", "p", "ev", "own"))
        block = st.block()

        @block.sync
        def _(sp):
            sp.dma_start(w[:, :, :], cols(w_dram)).then_inc(s_w, 16)

        @block.tensor
        def _(pe):
            pe.wait_ge(s_w, 16)
            for t in range(NT):
                if t >= 4:
                    pe.wait_ge(s_ev, t - 3)
                for c in range(K):
                    last = nc.tensor.matmul(pp[t % 4][:, :], srcT[:, c, t * P:(t + 1) * P], w[:, c, :],
                                            start=(c == 0), stop=(c == K - 1))
                last.then_inc(s_p, 1)

        @block.vector
        def _(dve):
            own = InOrder(dve, s_own)
            for t in range(NT):
                dve.wait_ge(s_p, t + 1)
                tiles_out(own, t, pp[t % 4][:, :]).then_inc(s_ev, 1)


def route(nc, name, logits, K, weights, iota, over_all=False, capacity=None, tri=None, ones=None):
    E = logits.shape[2]
    with Stage(nc, name) as st:
        top = st.sb("top", [P, NT, 8])
        idx = st.sb("idx", [P, NT, 8], U32)
        idf = st.sb("idf", [P, NT, K])
        et = st.sb("et", [P, NT, 8])
        ea = st.sb("ea", [P, NT, E])
        den = st.sb("den", [P, NT])
        hot = st.sb("hot", [P, K, NT, E])
        s_own, s_sub, s_exp, s_hot, s_rank = (st.sem(n) for n in ("own", "sub", "exp", "hot", "rank"))
        if capacity:
            hotb = st.sb("hotb", [P, K, NT, E], BF16)
            seen = st.sb("seen", [P, K, NT, E], BF16)
            rank = st.ps("rank", [P, K, NT, E])
        block = st.block()

        @block.vector
        def _(dve):
            own = InOrder(dve, s_own)
            for t in range(NT):
                last = nc.vector.max(top[:, t, :], logits[:, t, :])
            own.after(last)
            for t in range(NT):
                nc.vector.max_index(idx[:, t, :], top[:, t, :], logits[:, t, :])
            best = top[:, :, 0:1]
            if over_all:
                nc.vector.tensor_tensor(ea[:, :, :], logits[:, :, :], best.to_broadcast([P, NT, E]), ALU.subtract)
            nc.vector.tensor_tensor(et[:, :, :], top[:, :, :], best.to_broadcast([P, NT, 8]), ALU.subtract
                                    ).then_inc(s_sub, 1)
            dve.wait_ge(s_sub, 1)
            own.after(nc.vector.tensor_copy(idf[:, :, :], idx[:, :, 0:K]))
            for k in range(K):
                last = nc.vector.tensor_tensor(hot[:, k, :, :], iota[:, 0:E].unsqueeze(1).to_broadcast([P, NT, E]),
                                        idf[:, :, k:k + 1].to_broadcast([P, NT, E]), ALU.is_equal)
            own.after(last)
            if capacity:
                own.after(nc.vector.tensor_copy(hotb[:, :, :, :], hot[:, :, :, :]))
                own.after(nc.vector.memset(seen[:, :, 0, :], 0.0))
                for t in range(1, NT):
                    own.after(nc.vector.tensor_tensor(seen[:, :, t, :], seen[:, :, t - 1, :], hotb[:, :, t - 1, :],
                                                      ALU.add))
                nc.vector.memset(den[:, :], 0.0).then_inc(s_hot, 1)
                dve.wait_ge(s_rank, 1)
                own.after(nc.vector.scalar_tensor_tensor(hot[:, :, :, :], rank[:, :, :, :], float(capacity),
                                                         hot[:, :, :, :], ALU.is_lt, ALU.mult))
            dve.wait_ge(s_exp, 1)
            own.after(nc.vector.tensor_reduce(den[:, :], ea[:, :, :] if over_all else et[:, :, 0:K], AX.X, ALU.add))
            own.after(nc.vector.reciprocal(den[:, :], den[:, :]))
            own.after(nc.vector.tensor_tensor(et[:, :, 0:K], et[:, :, 0:K],
                                              den[:, :].unsqueeze(2).to_broadcast([P, NT, K]), ALU.mult))
            for k in range(K):
                last = nc.vector.tensor_tensor(hot[:, k, :, :], hot[:, k, :, :],
                                               et[:, :, k:k + 1].to_broadcast([P, NT, E]), ALU.mult)
            own.after(last)
            own.after(nc.vector.tensor_tensor(weights, hot[:, 0, :, :], hot[:, 1, :, :], ALU.add))
            for k in range(2, K):
                own.after(nc.vector.tensor_tensor(weights, weights, hot[:, k, :, :], ALU.add))

        @block.scalar
        def _(act):
            act.wait_ge(s_sub, 1)
            if over_all:
                nc.scalar.activation(ea[:, :, :], ea[:, :, :], ACT.Exp)
            nc.scalar.activation(et[:, :, :], et[:, :, :], ACT.Exp).then_inc(s_exp, 1)

        if capacity:
            @block.tensor
            def _(pe):
                pe.wait_ge(s_hot, 1)
                for k in range(K):
                    for t in range(NT):
                        nc.tensor.matmul(rank[:, k, t, :], tri[:, :], hotb[:, k, t, :], start=True, stop=False)
                        last = nc.tensor.matmul(rank[:, k, t, :], ones[:, :], seen[:, k, t, :], start=False, stop=True)
                last.then_inc(s_rank, 1)


def experts(nc, name, xT, w1, w2, weights, x, func, w1u=None, w_of=None):
    E, _, F = w1.shape
    FT = F // P
    NS = E * B
    w_of = w_of or (lambda e: e)
    with Stage(nc, name) as st:
        wa = st.sb("wa", [P, 2, DC, F])
        wu = st.sb("wu", [P, 2, DC, F]) if w1u is not None else None
        wd = st.sb("wd", [P, 2, FT, D])
        hT = st.sb("hT", [P, 2, FT, S])
        NU = 4 if w1u is None else 2
        up = [st.ps(f"up{i}", [P, 4 // NU, S]) for i in range(NU)]
        down = [st.ps(f"down{i}", [P, D]) for i in range(4)]
        sg = st.sb("sg", [P, 2, S]) if w1u is not None else None
        s_w = [st.sem(f"w{i}") for i in range(2)]
        s_up, s_h, s_dn, s_x, s_sg = (st.sem(n) for n in ("up", "h", "dn", "x", "sg"))
        NW = 2 if w1u is None else 3
        block = st.block()

        @block.sync
        def _(sp):
            for e in range(E):
                if e >= 2:
                    sp.wait_ge(s_dn, NT * (e - 1))
                sp.dma_start(wa[:, e % 2, :, :], cols(w1[e])).then_inc(s_w[e % 2], 16)
                if w1u is not None:
                    sp.dma_start(wu[:, e % 2, :, :], cols(w1u[e])).then_inc(s_w[e % 2], 16)
                sp.dma_start(wd[:, e % 2, :, :], cols(w2[e])).then_inc(s_w[e % 2], 16)

        @block.tensor
        def _(pe):
            def go_up(n):
                e, g = n // B, n % B
                if g == 0:
                    pe.wait_ge(s_w[e % 2], 16 * NW * (e // 2 + 1))
                for f in range(FT):
                    k = n * FT + f
                    if k >= NU:
                        pe.wait_ge(s_h, k - NU + 1)
                    for j, w in enumerate([wa] if w1u is None else [wa, wu]):
                        for c in range(DC):
                            last = nc.tensor.matmul(up[k % NU][:, j, :], w[:, e % 2, c, f * P:(f + 1) * P],
                                                    xT[:, c, g * S:(g + 1) * S], start=(c == 0), stop=(c == DC - 1))
                    last.then_inc(s_up, 1)

            def go_down(n):
                e = n // B
                pe.wait_ge(s_h, FT * (n + 1))
                for i in range(QT):
                    m = n * QT + i
                    if m >= 4:
                        pe.wait_ge(s_x, m - 3)
                    for f in range(FT):
                        last = nc.tensor.matmul(down[m % 4][:, :], hT[:, n % 2, f, i * P:(i + 1) * P],
                                                wd[:, e % 2, f, :], start=(f == 0), stop=(f == FT - 1))
                    last.then_inc(s_dn, 1)

            for n in range(NS + 1):
                if n < NS:
                    go_up(n)
                if n >= 1:
                    go_down(n - 1)

        @block.scalar
        def _(act):
            for k in range(NS * FT):
                n, f = k // FT, k % FT
                act.wait_ge(s_up, k + 1)
                if w1u is None:
                    if n >= 2:
                        act.wait_ge(s_dn, QT * (n - 1))
                    nc.scalar.activation(hT[:, n % 2, f, :], up[k % NU][:, 0, :], func).then_inc(s_h, 1)
                else:
                    if k >= 2:
                        act.wait_ge(s_h, k - 1)
                    nc.scalar.activation(sg[:, k % 2, :], up[k % NU][:, 0, :], func).then_inc(s_sg, 1)

        @block.vector
        def _(dve):
            def gate(n):
                for f in range(FT):
                    k = n * FT + f
                    dve.wait_ge(s_sg, k + 1)
                    if n >= 2:
                        dve.wait_ge(s_dn, QT * (n - 1))
                    nc.vector.tensor_tensor(hT[:, n % 2, f, :], sg[:, k % 2, :], up[k % NU][:, 1, :], ALU.mult
                                            ).then_inc(s_h, 1)

            for n in range(NS + 1):
                if w1u is not None and n < NS:
                    gate(n)
                if n == 0:
                    continue
                for i in range(QT):
                    m = (n - 1) * QT + i
                    t, e = m % NT, m // NT
                    dve.wait_ge(s_dn, m + 1)
                    if m >= NT:
                        dve.wait_ge(s_x, m - NT + 1)
                    nc.vector.scalar_tensor_tensor(x[:, t, :], down[m % 4][:, :], weights[:, t, w_of(e):w_of(e) + 1],
                                                   x[:, t, :], ALU.mult, ALU.add).then_inc(s_x, 1)


def add_rows(nc, name, vec, x):
    with Stage(nc, name) as st:
        vb = st.sb("vb", [P, D])
        s_ld = st.sem("ld")
        block = st.block()

        @block.sync
        def _(sp):
            sp.dma_start(vb[:, :], vec.partition_broadcast(P)).then_inc(s_ld, 16)

        @block.vector
        def _(dve):
            dve.wait_ge(s_ld, 16)
            for t in range(NT):
                nc.vector.tensor_tensor(x[:, t, :], x[:, t, :], vb[:, :], ALU.add)


HB = 64
NP = H16 * HB // P


def tri_at(k):
    return slice(k * (k + 1) // 2 * P, (k + 1) * (k + 2) // 2 * P)


def causal_masks(nc, name, a, am, mk_col, uT, sufmax, usum, ident):
    with Stage(nc, name) as st:
        later = st.sb("later", [P, QT, S])
        fill = st.sb("fill", [P, QT, S])
        mb = st.sb("mb", [P, B, S])
        sc = st.sb("sc", [P, 2, S])
        u = st.sb("u", [P, QT, S])
        ns = st.sb("ns", [P, NT])
        tp = [st.ps(f"tp{i}", [P, S]) for i in range(2)]
        s_ld, s_sc, s_mx, s_ns, s_u, s_tr, s_ev, s_am = (
            st.sem(n) for n in ("ld", "sc", "mx", "ns", "u", "tr", "ev", "am"))
        block = st.block()

        @block.sync
        def _(sp):
            sp.dma_start(later[:, :, :], a["c_later"]).then_inc(s_ld, 16)
            sp.dma_start(fill[:, :, :], a["c_fill"]).then_inc(s_ld, 16)
            sp.dma_start(mk_col[:, :], a["addm_col"]).then_inc(s_ld, 16)
            sp.dma_start(mb[:, :, :].rearrange("p b n -> p (b n)"), a["addm"].partition_broadcast(P)
                         ).then_inc(s_ld, 16)
            sp.wait_ge(s_ld, 64)

        @block.vector
        def _(dve):
            dve.wait_ge(s_ld, 64)
            for m in range(NT):
                b, t = m // QT, m % QT
                nc.vector.tensor_tensor(am[:, m, :], mb[:, b, :], later[:, t, :], ALU.add).then_inc(s_am, 1)
                if m >= 2:
                    dve.wait_ge(s_u, m - 1)
                nc.vector.tensor_tensor(sc[:, m % 2, :], mb[:, b, :], fill[:, t, :], ALU.add).then_inc(s_sc, 1)
                dve.wait_ge(s_sc, m + 1)
                nc.vector.tensor_reduce(sufmax[:, m:m + 1], sc[:, m % 2, :], AX.X, ALU.max).then_inc(s_mx, 1)
                dve.wait_ge(s_mx, m + 1)
                nc.vector.tensor_scalar(ns[:, m:m + 1], sufmax[:, m:m + 1], -1.0, None, ALU.mult).then_inc(s_ns, 1)

        @block.scalar
        def _(act):
            j = 0
            for m in range(NT):
                b, t = m // QT, m % QT
                act.wait_ge(s_ns, m + 1)
                if b >= 1:
                    act.wait_ge(s_tr, QT * b)
                nc.scalar.activation(u[:, t, :], sc[:, m % 2, :], ACT.Exp, bias=ns[:, m:m + 1],
                                     accum_out=usum[:, m:m + 1]).then_inc(s_u, 1)
                if t == QT - 1:
                    for k in range(QT):
                        act.wait_ge(s_tr, j + 1)
                        nc.scalar.activation(uT[:, b, tri_at(k)], tp[j % 2][:, 0:(k + 1) * P], ACT.Identity
                                             ).then_inc(s_ev, 1)
                        j += 1

        @block.tensor
        def _(pe):
            for j in range(B * QT):
                b, k = j // QT, j % QT
                pe.wait_ge(s_u, QT * (b + 1))
                if j >= 2:
                    pe.wait_ge(s_ev, j - 1)
                for t in range(k + 1):
                    last = nc.tensor.transpose(tp[j % 2][:, t * P:(t + 1) * P], u[:, t, k * P:(k + 1) * P], ident[:, :])
                last.then_inc(s_tr, 1)


def attend64(nc, name, a, xT, cT, masks, x, ident, identb, ones):
    am, mk_col, uT, sufmax, usum = masks
    N = B * NP
    scale = HB ** -0.5
    with Stage(nc, name) as st:
        w = [st.sb("w" + k, [P, DC, H16 * HB]) for k in "qkv"]
        wo = st.sb("wo", [P, NP, D])
        bqk = st.sb("bqk", [P, 2, NP])
        bv = st.sb("bv", [P, H16 * HB])
        bo = st.sb("bo", [P, D])
        selm = st.sb("selm", [P, P], BF16)
        self_ = st.sb("self", [P, P])
        selc = st.sb("selc", [P, 2])
        qT = st.sb("qT", [P, 2, S])
        kT = st.sb("kT", [P, 2, S])
        v = st.sb("v", [P, 2, QT, P])
        wmT = st.sb("wmT", [P, 2, S])
        junk = st.sb("junk", [P, 2, S], BF16)
        rowmax = st.sb("rowmax", [P, QT, 2])
        neg = st.sb("neg", [P, QT, 2])
        negr = st.sb("negr", [P, QT, 2])
        negp = st.sb("negp", [P, QT, P], BF16)
        en = st.sb("en", [P, 2, QT, 2])
        em = st.sb("em", [P, 2, QT, 2])
        den = st.sb("den", [P, QT, 2])
        rec = st.sb("rec", [P, QT, 2])
        nmT = st.sb("nmT", [P, S], BF16)
        prob = st.sb("prob", [P, 2, QT, S])
        smT = st.sb("smT", [P, S])
        accT = st.sb("accT", [P, S])
        expand = st.sb("expand", [P, 2, QT, 2, HB])
        t1 = st.sb("t1", [P, S])
        t2 = st.sb("t2", [P, S])
        oT = st.sb("oT", [P, NP, S])
        pj = st.ps("pj", [P, S])
        sq = [st.ps(f"sq{i}", [P, S]) for i in range(2)]
        sk = [st.ps(f"sk{i}", [P, S]) for i in range(2)]
        acc = st.ps("acc", [P, S])
        sm = st.ps("sm", [P, S])
        misc = st.ps("misc", [P, S])
        miscb = misc[:, :].bitcast(BF16)[:, 0:S]
        names = ("w c pj qkv wm sq max negp en em mt qm sk exp pv sme sum ex rb t1 fb out op x own acc keep".split())
        (s_w, s_c, s_pj, s_qkv, s_wm, s_sq, s_max, s_negp, s_en, s_em, s_mt, s_qm, s_sk, s_exp, s_pv, s_sme,
         s_sum, s_ex, s_rb, s_t1, s_fb, s_out, s_op, s_x, s_own, s_acc, s_keep) = (st.sem(n) for n in names)
        block = st.block()

        @block.sync
        def _(sp):
            for i, k in enumerate(("WQ", "WK", "WV")):
                sp.dma_start(w[i][:, :, :], cols(a["L1_" + k])).then_inc(s_w, 16)
            sp.dma_start(wo[:, :, :], cols(a["L1_WO"])).then_inc(s_w, 16)
            for i, k in enumerate(("bQ", "bK")):
                sp.dma_start(bqk[:, i, :], a["L1_" + k]).then_inc(s_w, 16)
            sp.dma_start(bv[:, :], a["L1_bV"].partition_broadcast(P)).then_inc(s_w, 16)
            sp.dma_start(bo[:, :], a["L1_bO"].partition_broadcast(P)).then_inc(s_w, 16)
            sp.dma_start(self_[:, :], a["c_selm"]).then_inc(s_w, 16)
            sp.dma_start(selc[:, :], a["c_selc"]).then_inc(s_w, 16)
            sp.wait_ge(s_w, 16 * 10)

        @block.tensor
        def _(pe):
            def project(n, which):
                b, p = n // NP, n % NP
                if which == 0 and n >= 1:
                    pe.wait_ge(s_wm, n)
                    if p == 1 and b >= 1:
                        pe.wait_ge(s_x, QT * b)
                elif which > 0:
                    pe.wait_ge(s_qkv, 3 * n + which)
                if which < 2:
                    src = (xT, cT)[which]
                    for c in range(DC):
                        last = nc.tensor.matmul(pj[:, :], w[which][:, c, p * P:(p + 1) * P], src[:, c, b * S:(b + 1) * S],
                                                start=(c == 0), stop=(c == DC - 1))
                elif which == 2:
                    for t in range(QT):
                        for c in range(DC):
                            last = nc.tensor.matmul(pj[:, t * P:(t + 1) * P], cT[:, c, b * S + t * P:b * S + (t + 1) * P],
                                                    w[2][:, c, p * P:(p + 1) * P], start=(c == 0), stop=(c == DC - 1))
                else:
                    for t in reversed(range(QT)):
                        last = nc.tensor.matmul(pj[:, 0:(t + 1) * P], v[:, n % 2, t, :], uT[:, b, tri_at(t)],
                                                start=(t == QT - 1), stop=(t == 0), skip_group_check=True)
                last.then_inc(s_pj, 1)

            def row_scores(n, i):
                h, t = i // QT, i % QT
                k = n * 8 + i
                if k >= 2:
                    pe.wait_ge(s_max, k - 1)
                r = slice(h * HB, (h + 1) * HB)
                nc.tensor.matmul(sq[k % 2][:, 0:(t + 1) * P], qT[r, n % 2, t * P:(t + 1) * P],
                                 kT[r, n % 2, 0:(t + 1) * P], start=True, stop=True).then_inc(s_sq, 1)

            def turn_max(n):
                pe.wait_ge(s_negp, n + 1)
                if n >= 1:
                    pe.wait_ge(s_out, n)
                for t in range(QT):
                    last = nc.tensor.transpose(miscb[:, t * P:(t + 1) * P], negp[:, t, :], identb[:, :])
                last.then_inc(s_mt, 1)

            def key_scores(n, u):
                h, t = u // QT, u % QT
                k = n * 8 + u
                if u == 0:
                    pe.wait_ge(s_qm, n + 1)
                if k >= 2:
                    pe.wait_ge(s_exp, k - 1)
                r = slice(h * HB, (h + 1) * HB)
                nc.tensor.matmul(sk[k % 2][:, t * P:S], kT[r, n % 2, t * P:(t + 1) * P], qT[r, n % 2, t * P:S],
                                 start=True, stop=False)
                nc.tensor.matmul(sk[k % 2][:, t * P:S], selm[r, :], nmT[r, t * P:S], start=False, stop=True
                                 ).then_inc(s_sk, 1)

            def values(n, h):
                pe.wait_ge(s_keep, 8 * n + QT * (h + 1))
                if h == 0 and n >= 1:
                    pe.wait_ge(s_acc, n)
                    pe.wait_ge(s_sme, n)
                o = slice(h * HB, (h + 1) * HB)
                for t in reversed(range(QT)):
                    for dst, lhs in ((acc, v[:, n % 2, t, h * HB:(h + 1) * HB]), (sm, ones[:, 0:HB])):
                        last = nc.tensor.matmul(dst[o, t * P:S], lhs, prob[:, h, t, t * P:S], start=(t == QT - 1),
                                                stop=(t == 0), tile_position=(0, h * HB), skip_group_check=True)
                last.then_inc(s_pv, 1)

            def finish(n):
                pe.wait_ge(s_sme, n + 1)
                for t in range(QT):
                    last = nc.tensor.matmul(misc[:, 2 * t:2 * t + 2], smT[:, t * P:(t + 1) * P], selc[:, :],
                                            start=True, stop=True)
                last.then_inc(s_sum, 1)
                for j, sem in enumerate((s_rb, s_fb)):
                    pe.wait_ge(s_ex, 2 * n + j + 1)
                    if j == 1:
                        pe.wait_ge(s_t1, n + 1)
                    for t in range(QT):
                        last = nc.tensor.transpose(misc[:, t * P:(t + 1) * P],
                                                   expand[:, j, t, :, :].rearrange("p h d -> p (h d)"), ident[:, :])
                    last.then_inc(sem, 1)

            def output(b):
                pe.wait_ge(s_out, NP * (b + 1))
                if b < B - 1:
                    pe.wait_ge(s_wm, NP * (b + 1) + 1)
                for i in range(QT):
                    if i >= 1:
                        pe.wait_ge(s_x, QT * b + i)
                    for p in range(NP):
                        last = nc.tensor.matmul(pj[:, 0:D], oT[:, p, i * P:(i + 1) * P], wo[:, p, :],
                                                start=(p == 0), stop=(p == NP - 1))
                    last.then_inc(s_op, 1)

            pe.wait_ge(s_w, 16 * 10)
            pe.wait_ge(s_c, 1)
            for n in range(-1, N):
                nxt = n + 1 < N
                for u in range(8):
                    if n >= 0:
                        key_scores(n, u)
                        if u == 5:
                            values(n, 0)
                    if nxt:
                        if u < 4:
                            project(n + 1, u)
                        else:
                            row_scores(n + 1, 2 * (u - 4))
                            row_scores(n + 1, 2 * (u - 4) + 1)
                if n >= 0:
                    values(n, 1)
                    finish(n)
                    if n % NP == NP - 1:
                        output(n // NP)
                if nxt:
                    turn_max(n + 1)

        @block.vector
        def _(dve):
            own = InOrder(dve, s_own)
            dve.wait_ge(s_w, 16 * 10)
            nc.vector.tensor_copy(selm[:, :], self_[:, :]).then_inc(s_c, 1)
            nc.vector.memset(negp[:, :, :], 0.0)
            for t in range(NT):
                last = nc.vector.tensor_tensor(x[:, t, :], x[:, t, :], bo[:, :], ALU.add)
            own.after(last)

            def evacuate(n):
                p = n % NP
                for i, dst in enumerate((qT, kT)):
                    dve.wait_ge(s_pj, 4 * n + i + 1)
                    if n >= 2:
                        dve.wait_ge(s_sk, 8 * (n - 1))
                    nc.vector.tensor_scalar(dst[:, n % 2, :], pj[:, :], bqk[:, i, p:p + 1], scale if i == 0 else 1.0,
                                            ALU.add, ALU.mult).then_inc(s_qkv, 1)
                dve.wait_ge(s_pj, 4 * n + 3)
                if n >= 2:
                    dve.wait_ge(s_pv, 2 * (n - 1))
                nc.vector.tensor_tensor(v[:, n % 2, :, :], pj[:, :].rearrange("p (t n) -> p t n", t=QT),
                                        bv[:, p * P:(p + 1) * P].unsqueeze(1).to_broadcast([P, QT, P]), ALU.add
                                        ).then_inc(s_qkv, 1)

            def row_max(n, i):
                h, t = i // QT, i % QT
                k = n * 8 + i
                dve.wait_ge(s_sq, k + 1)
                if k >= 2:
                    dve.wait_ge(s_max, k - 1)
                nc.vector.tensor_tensor_reduce(junk[:, k % 2, 0:(t + 1) * P], sq[k % 2][:, 0:(t + 1) * P],
                                               am[:, (n // NP) * QT + t, 0:(t + 1) * P], 1.0, 3.0 * BIG,
                                               ALU.add, ALU.max, rowmax[:, t, h:h + 1]).then_inc(s_max, 1)

            def minus_max(n):
                dve.wait_ge(s_max, 8 * (n + 1))
                m0 = (n // NP) * QT
                for t in range(QT):
                    last = nc.vector.tensor_scalar(rowmax[:, t, :], rowmax[:, t, :], sufmax[:, m0 + t:m0 + t + 1], None,
                                                   ALU.max)
                own.after(last)
                own.after(nc.vector.tensor_scalar(neg[:, :, :], rowmax[:, :, :], -1.0, None, ALU.mult))
                if n >= 2:
                    dve.wait_ge(s_em, n - 1)
                for t in range(QT):
                    last = nc.vector.tensor_scalar(en[:, n % 2, t, :], neg[:, t, :], sufmax[:, m0 + t:m0 + t + 1], None,
                                                   ALU.add)
                last.then_inc(s_en, 1)
                if n >= 1:
                    dve.wait_ge(s_mt, n)
                part = [negp[:, :, i:i + HB + 1:HB] for i in range(NPART)]
                own.after(nc.vector.tensor_copy(part[0], neg[:, :, :]))
                own.after(nc.vector.tensor_tensor(negr[:, :, :], neg[:, :, :], part[0], ALU.subtract))
                own.after(nc.vector.tensor_copy(part[1], negr[:, :, :]))
                nc.vector.tensor_tensor(part[2], negr[:, :, :], part[1], ALU.subtract).then_inc(s_negp, 1)

            def finish(n):
                b, p = n // NP, n % NP
                e = em[:, n % 2, :, :]
                dve.wait_ge(s_em, n + 1)
                own.after(nc.vector.tensor_tensor(den[:, :, :], e,
                                                  usum[:, b * QT:(b + 1) * QT].unsqueeze(2).to_broadcast([P, QT, 2]),
                                                  ALU.mult))
                dve.wait_ge(s_sum, n + 1)
                own.after(nc.vector.tensor_tensor(den[:, :, :], den[:, :, :],
                                                  misc[:, 0:2 * QT].rearrange("p (t h) -> p t h", t=QT), ALU.add))
                own.after(nc.vector.reciprocal(rec[:, :, :], den[:, :, :]))
                if n >= 1:
                    dve.wait_ge(s_fb, n)
                nc.vector.tensor_copy(expand[:, 0, :, :, :], rec[:, :, :].unsqueeze(3).to_broadcast([P, QT, 2, HB])
                                      ).then_inc(s_ex, 1)
                own.after(nc.vector.tensor_tensor(den[:, :, :], e, rec[:, :, :], ALU.mult))
                nc.vector.tensor_copy(expand[:, 1, :, :, :], den[:, :, :].unsqueeze(3).to_broadcast([P, QT, 2, HB])
                                      ).then_inc(s_ex, 1)
                dve.wait_ge(s_rb, n + 1)
                dve.wait_ge(s_acc, n + 1)
                nc.vector.tensor_tensor(t1[:, :], accT[:, :], misc[:, :], ALU.mult).then_inc(s_t1, 1)
                dve.wait_ge(s_fb, n + 1)
                own.after(nc.vector.tensor_tensor(t2[:, :], wmT[:, n % 2, :], misc[:, :], ALU.mult))
                if b >= 1:
                    dve.wait_ge(s_op, QT * b)
                nc.vector.tensor_tensor(oT[:, p, :], t1[:, :], t2[:, :], ALU.add).then_inc(s_out, 1)

            for n in range(-1, N):
                if n + 1 < N:
                    evacuate(n + 1)
                    for i in range(8):
                        row_max(n + 1, i)
                    minus_max(n + 1)
                if n >= 0:
                    dve.wait_ge(s_wm, n + 1)
                    finish(n)
                    if n % NP == NP - 1:
                        for i in range(QT):
                            m = (n // NP) * QT + i
                            dve.wait_ge(s_op, m + 1)
                            nc.vector.tensor_tensor(x[:, m, :], x[:, m, :], pj[:, 0:D], ALU.add).then_inc(s_x, 1)

        @block.gpsimd
        def _(pool):
            for k in range(N * 8):
                n, u = k // 8, k % 8
                pool.wait_ge(s_exp, k + 1)
                tile = prob[:, u // QT, u % QT, (u % QT) * P:(u % QT + 1) * P]
                nc.gpsimd.affine_select(out=tile, in_=tile, compare_op=ALU.is_ge, fill=0.0, base=0,
                                        pattern=[[1, P]], channel_multiplier=-1).then_inc(s_keep, 1)

        @block.scalar
        def _(act):
            for n in range(-1, N):
                for u in range(8):
                    if n >= 0:
                        h, t = u // QT, u % QT
                        k = n * 8 + u
                        m = (n // NP) * QT + t
                        act.wait_ge(s_sk, k + 1)
                        if n >= 1:
                            act.wait_ge(s_pv, 2 * (n - 1) + h + 1)
                        nc.scalar.activation(prob[:, h, t, t * P:S], sk[k % 2][:, t * P:S], ACT.Exp,
                                             bias=mk_col[:, m:m + 1]).then_inc(s_exp, 1)
                    if u == 3 and n + 1 < N:
                        act.wait_ge(s_pj, 4 * (n + 2))
                        if n >= 1:
                            act.wait_ge(s_out, n)
                        nc.scalar.activation(wmT[:, (n + 1) % 2, :], pj[:, :], ACT.Identity).then_inc(s_wm, 1)
                if n >= 0:
                    act.wait_ge(s_pv, 2 * (n + 1))
                    nc.scalar.activation(smT[:, :], sm[:, :], ACT.Identity).then_inc(s_sme, 1)
                    if n >= 1:
                        act.wait_ge(s_t1, n)
                    nc.scalar.activation(accT[:, :], acc[:, :], ACT.Identity).then_inc(s_acc, 1)
                if n + 1 < N:
                    act.wait_ge(s_en, n + 2)
                    nc.scalar.activation(em[:, (n + 1) % 2, :, :], en[:, (n + 1) % 2, :, :], ACT.Exp).then_inc(s_em, 1)
                    act.wait_ge(s_mt, n + 2)
                    nc.scalar.activation(nmT[:, :], miscb, ACT.Identity).then_inc(s_qm, 1)


def similarity(nc, name, a, xnT, cT, crow, hqT, mcol, ident):
    with Stage(nc, name) as st:
        w3 = st.sb("w3", [P, 3, DC])
        bsim = st.sb("bsim", [P, 1])
        e3T = st.sb("e3T", [P, DC, T])
        A = st.sb("A", [P, 2, QT, S])
        AT = st.sb("AT", [P, QT, S])
        neg = st.sb("neg", [P, NT])
        tot = st.sb("tot", [P, NT])
        sc = [st.ps(f"sc{i}", [P, S]) for i in range(2)]
        tp = [st.ps(f"tp{i}", [P, S]) for i in range(2)]
        hq = [st.ps(f"hq{i}", [P, S]) for i in range(2)]
        e1 = st.ps("e1", [P, NT])
        s_w, s_e3, s_sc, s_neg, s_exp, s_A, s_tr, s_at, s_hq, s_ev, s_e1, s_own, s_tot = (
            st.sem(n) for n in ("w", "e3", "sc", "neg", "exp", "A", "tr", "at", "hq", "ev", "e1", "own", "tot"))
        block = st.block()

        @block.sync
        def _(sp):
            sp.dma_start(w3[:, :, :], a["L2_wsim"]).then_inc(s_w, 16)
            sp.dma_start(bsim[:, :], a["L2_bsim"].partition_broadcast(P)).then_inc(s_w, 16)
            sp.wait_ge(s_w, 32)

        @block.tensor
        def _(pe):
            pe.wait_ge(s_w, 32)
            for t in range(NT):
                for c in range(DC):
                    last = nc.tensor.matmul(e1[:, t:t + 1], xnT[:, c, t * P:(t + 1) * P], w3[:, 0, c:c + 1],
                                            start=(c == 0), stop=(c == DC - 1))
            last.then_inc(s_e1, 1)

            def scores(b):
                for t in range(QT):
                    m = b * QT + t
                    pe.wait_ge(s_e3, DC * (b + 1))
                    if m >= 2:
                        pe.wait_ge(s_exp, m - 1)
                    for c in range(DC):
                        last = nc.tensor.matmul(sc[m % 2][:, :], e3T[:, c, m * P:(m + 1) * P], cT[:, c, b * S:(b + 1) * S],
                                                start=(c == 0), stop=(c == DC - 1))
                    last.then_inc(s_sc, 1)

            scores(0)
            for b in range(B):
                if b + 1 < B:
                    scores(b + 1)
                pe.wait_ge(s_A, QT * (b + 1))
                for j in range(QT):
                    k = b * QT + j
                    if k >= 2:
                        pe.wait_ge(s_at, k - 1)
                    for t in range(QT):
                        last = nc.tensor.transpose(tp[k % 2][:, t * P:(t + 1) * P], A[:, b % 2, t, j * P:(j + 1) * P],
                                                   ident[:, :])
                    last.then_inc(s_tr, 1)
                pe.wait_ge(s_at, QT * (b + 1))
                for c in range(DC):
                    if b >= 1:
                        pe.wait_ge(s_ev, DC * (b - 1) + c + 1)
                    for j in range(QT):
                        last = nc.tensor.matmul(hq[c][:, :], crow[:, b * QT + j, c * P:(c + 1) * P], AT[:, j, :],
                                                start=(j == 0), stop=(j == QT - 1))
                    last.then_inc(s_hq, 1)

        @block.vector
        def _(dve):
            own = InOrder(dve, s_own)
            dve.wait_ge(s_w, 32)
            for b in range(B):
                for c in range(DC):
                    nc.vector.tensor_scalar(e3T[:, c, b * S:(b + 1) * S], xnT[:, c, b * S:(b + 1) * S],
                                            w3[:, 2, c:c + 1], w3[:, 1, c:c + 1], ALU.mult, ALU.add).then_inc(s_e3, 1)
            for m in range(NT):
                b, t = m // QT, m % QT
                dve.wait_ge(s_sc, m + 1)
                own.after(nc.vector.tensor_reduce(mcol[:, m:m + 1], sc[m % 2][:, :], AX.X, ALU.max))
                nc.vector.tensor_scalar(neg[:, m:m + 1], mcol[:, m:m + 1], -1.0, None, ALU.mult).then_inc(s_neg, 1)
                dve.wait_ge(s_exp, m + 1)
                own.after(nc.vector.reciprocal(tot[:, m:m + 1], tot[:, m:m + 1]))
                nc.vector.tensor_scalar(A[:, b % 2, t, :], A[:, b % 2, t, :], tot[:, m:m + 1], None, ALU.mult
                                        ).then_inc(s_A, 1)
            dve.wait_ge(s_e1, 1)
            own.after(nc.vector.tensor_tensor(mcol[:, :], mcol[:, :], e1[:, :], ALU.add))
            own.after(nc.vector.tensor_scalar(mcol[:, :], mcol[:, :], bsim[:, 0:1], None, ALU.add))

        @block.scalar
        def _(act):
            def exps(b):
                for t in range(QT):
                    m = b * QT + t
                    act.wait_ge(s_neg, m + 1)
                    if b >= 2:
                        act.wait_ge(s_tr, QT * (b - 1))
                    nc.scalar.activation(A[:, b % 2, t, :], sc[m % 2][:, :], ACT.Exp, bias=neg[:, m:m + 1],
                                         accum_out=tot[:, m:m + 1]).then_inc(s_exp, 1)

            exps(0)
            for b in range(B):
                if b + 1 < B:
                    exps(b + 1)
                for j in range(QT):
                    k = b * QT + j
                    act.wait_ge(s_tr, k + 1)
                    if b >= 1:
                        act.wait_ge(s_hq, DC * b)
                    nc.scalar.activation(AT[:, j, :], tp[k % 2][:, :], ACT.Identity).then_inc(s_at, 1)
                for c in range(DC):
                    act.wait_ge(s_hq, DC * b + c + 1)
                    nc.scalar.activation(hqT[:, c, b * S:(b + 1) * S], hq[c][:, :], ACT.Identity).then_inc(s_ev, 1)


def attended_row(nc, name, xnT, hqT, mcol, xhT, xcT, ident, ones):
    with Stage(nc, name) as st:
        row = st.sb("row", [1, B, S])
        mx = st.sb("mx", [1, B])
        junk = st.sb("junk", [P, 2, S])
        hc = st.sb("hc", [P, B, DC])
        r = st.ps("r", [1, B, S])
        rb = [st.ps(f"rb{i}", [P, S]) for i in range(2)]
        s_r, s_sub, s_exp, s_row, s_rb, s_hc, s_own, s_xh = (
            st.sem(n) for n in ("r", "sub", "exp", "row", "rb", "hc", "own", "xh"))
        block = st.block()

        @block.tensor
        def _(pe):
            for t in range(NT):
                last = nc.tensor.matmul(r[:, t // QT, (t % QT) * P:(t % QT + 1) * P], mcol[:, t:t + 1], ident[:, :],
                                        start=True, stop=True)
            last.then_inc(s_r, 1)
            pe.wait_ge(s_row, 1)
            for b in range(B):
                if b >= 2:
                    pe.wait_ge(s_hc, DC * (b - 1))
                nc.tensor.matmul(rb[b % 2][:, :], ones[0:1, :], row[:, b, :], start=True, stop=True).then_inc(s_rb, 1)

        @block.scalar
        def _(act):
            act.wait_ge(s_sub, 1)
            nc.scalar.activation(row[:, :, :], row[:, :, :], ACT.Exp).then_inc(s_exp, 1)

        @block.vector
        def _(dve):
            own = InOrder(dve, s_own)
            dve.wait_ge(s_r, 1)
            own.after(nc.vector.tensor_reduce(mx[:, :], r[:, :, :], AX.X, ALU.max))
            nc.vector.tensor_tensor(row[:, :, :], r[:, :, :], mx[:, :].unsqueeze(2).to_broadcast([1, B, S]),
                                    ALU.subtract).then_inc(s_sub, 1)
            for c in range(DC):
                nc.vector.tensor_tensor(xhT[:, c, :], xnT[:, c, :], hqT[:, c, :], ALU.mult)
            dve.wait_ge(s_exp, 1)
            own.after(nc.vector.tensor_reduce(mx[:, :], row[:, :, :], AX.X, ALU.add))
            own.after(nc.vector.reciprocal(mx[:, :], mx[:, :]))
            nc.vector.tensor_tensor(row[:, :, :], row[:, :, :], mx[:, :].unsqueeze(2).to_broadcast([1, B, S]), ALU.mult
                                    ).then_inc(s_row, 1)
            for b in range(B):
                dve.wait_ge(s_rb, b + 1)
                for c in range(DC):
                    k = b * DC + c
                    if k >= 2:
                        dve.wait_ge(s_hc, k - 1)
                    nc.vector.tensor_tensor_reduce(junk[:, k % 2, :], xnT[:, c, b * S:(b + 1) * S], rb[b % 2][:, :],
                                                   1.0, 0.0, ALU.mult, ALU.add, hc[:, b, c:c + 1]).then_inc(s_hc, 1)
            dve.wait_ge(s_hc, B * DC)
            for b in range(B):
                for c in range(DC):
                    nc.vector.tensor_scalar(xcT[:, c, b * S:(b + 1) * S], xnT[:, c, b * S:(b + 1) * S],
                                            hc[:, b, c:c + 1], None, ALU.mult)


def project_parts(nc, name, parts, w_dram, b_dram, x):
    with Stage(nc, name) as st:
        K = len(parts) * DC
        w = st.sb("w", [P, K, D])
        bb = st.sb("bb", [P, D])
        pp = [st.ps(f"pp{i}", [P, D]) for i in range(4)]
        s_w, s_p, s_ev, s_b = (st.sem(n) for n in ("w", "p", "ev", "b"))
        block = st.block()

        @block.sync
        def _(sp):
            sp.dma_start(w[:, :, :], cols(w_dram)).then_inc(s_w, 16)
            sp.dma_start(bb[:, :], b_dram.partition_broadcast(P)).then_inc(s_w, 16)

        @block.tensor
        def _(pe):
            pe.wait_ge(s_w, 32)
            for t in range(NT):
                if t >= 4:
                    pe.wait_ge(s_ev, t - 3)
                for k in range(K):
                    last = nc.tensor.matmul(pp[t % 4][:, :], parts[k // DC][:, k % DC, t * P:(t + 1) * P], w[:, k, :],
                                            start=(k == 0), stop=(k == K - 1))
                last.then_inc(s_p, 1)

        @block.vector
        def _(dve):
            dve.wait_ge(s_w, 32)
            for t in range(NT):
                nc.vector.tensor_tensor(x[:, t, :], x[:, t, :], bb[:, :], ALU.add).then_inc(s_b, 1)
            for t in range(NT):
                dve.wait_ge(s_b, t + 1)
                dve.wait_ge(s_p, t + 1)
                nc.vector.tensor_tensor(x[:, t, :], x[:, t, :], pp[t % 4][:, :], ALU.add).then_inc(s_ev, 1)


def address_scores(nc, name, xT, pw, u, z):
    R = pw.shape[1]
    with Stage(nc, name) as st:
        w = st.sb("w", [P, DC, R])
        us = st.sb("us", [R, u.shape[1]])
        aT = st.sb("aT", [R, T])
        pa = [st.ps(f"pa{i}", [R, S]) for i in range(2)]
        pz = [st.ps(f"pz{i}", [P, u.shape[1]]) for i in range(2)]
        s_w, s_a, s_ae, s_z, s_ze = (st.sem(n) for n in ("w", "a", "ae", "z", "ze"))
        block = st.block()

        @block.sync
        def _(sp):
            sp.dma_start(w[:, :, :], cols(pw)).then_inc(s_w, 16)
            sp.dma_start(us[:, :], u).then_inc(s_w, 16)

        @block.tensor
        def _(pe):
            pe.wait_ge(s_w, 32)
            for b in range(B):
                if b >= 2:
                    pe.wait_ge(s_ae, b - 1)
                for c in range(DC):
                    last = nc.tensor.matmul(pa[b % 2][:, :], w[:, c, :], xT[:, c, b * S:(b + 1) * S],
                                            start=(c == 0), stop=(c == DC - 1))
                last.then_inc(s_a, 1)
            for t in range(NT):
                pe.wait_ge(s_ae, t // QT + 1)
                if t >= 2:
                    pe.wait_ge(s_ze, t - 1)
                nc.tensor.matmul(pz[t % 2][:, :], aT[:, t * P:(t + 1) * P], us[:, :], start=True, stop=True
                                 ).then_inc(s_z, 1)

        @block.scalar
        def _(act):
            for b in range(B):
                act.wait_ge(s_a, b + 1)
                nc.scalar.activation(aT[:, b * S:(b + 1) * S], pa[b % 2][:, :], ACT.Identity).then_inc(s_ae, 1)

        @block.vector
        def _(dve):
            for t in range(NT):
                dve.wait_ge(s_z, t + 1)
                nc.vector.tensor_copy(z[:, t, :], pz[t % 2][:, :]).then_inc(s_ze, 1)


def mixture(nc, name, xT, w_dram, weights, acc, fresh):
    E = w_dram.shape[0]
    with Stage(nc, name) as st:
        w = st.sb("w", [P, 2, DC, D])
        pp = [st.ps(f"pp{i}", [P, D]) for i in range(4)]
        s_w = [st.sem(f"w{i}") for i in range(2)]
        s_p, s_x = st.sem("p"), st.sem("x")
        block = st.block()

        @block.sync
        def _(sp):
            for e in range(E):
                if e >= 2:
                    sp.wait_ge(s_p, NT * (e - 1))
                sp.dma_start(w[:, e % 2, :, :], cols(w_dram[e])).then_inc(s_w[e % 2], 16)

        @block.tensor
        def _(pe):
            for m in range(E * NT):
                e, t = m // NT, m % NT
                if t == 0:
                    pe.wait_ge(s_w[e % 2], 16 * (e // 2 + 1))
                if m >= 4:
                    pe.wait_ge(s_x, m - 3)
                for c in range(DC):
                    last = nc.tensor.matmul(pp[m % 4][:, :], xT[:, c, t * P:(t + 1) * P], w[:, e % 2, c, :],
                                            start=(c == 0), stop=(c == DC - 1))
                last.then_inc(s_p, 1)

        @block.vector
        def _(dve):
            for m in range(E * NT):
                e, t = m // NT, m % NT
                dve.wait_ge(s_p, m + 1)
                if m >= NT:
                    dve.wait_ge(s_x, m - NT + 1)
                if fresh and e == 0:
                    ins = nc.vector.tensor_scalar(acc[:, t, :], pp[m % 4][:, :], weights[:, t, 0:1], None, ALU.mult)
                else:
                    ins = nc.vector.scalar_tensor_tensor(acc[:, t, :], pp[m % 4][:, :], weights[:, t, e:e + 1],
                                                         acc[:, t, :], ALU.mult, ALU.add)
                ins.then_inc(s_x, 1)


def gelu_rows(nc, name, h):
    with Stage(nc, name) as st:
        block = st.block()

        @block.scalar
        def _(act):
            for t in range(0, NT, QT):
                nc.scalar.activation(h[:, t:t + QT, :], h[:, t:t + QT, :], ACT.Gelu)


def add_choice(nc, name, weights, b2, x, ident):
    E = b2.shape[0]
    with Stage(nc, name) as st:
        b2s = st.sb("b2s", [E, D])
        wT = st.sb("wT", [E, T])
        pt = [st.ps(f"pt{i}", [E, S]) for i in range(2)]
        pp = [st.ps(f"pp{i}", [P, D]) for i in range(2)]
        s_ld, s_t, s_te, s_p, s_x = (st.sem(n) for n in ("ld", "t", "te", "p", "x"))
        block = st.block()

        @block.sync
        def _(sp):
            sp.dma_start(b2s[:, :], b2).then_inc(s_ld, 16)

        @block.tensor
        def _(pe):
            pe.wait_ge(s_ld, 16)
            for b in range(B):
                if b >= 2:
                    pe.wait_ge(s_te, b - 1)
                for i in range(QT):
                    last = nc.tensor.transpose(pt[b % 2][:, i * P:(i + 1) * P], weights[:, b * QT + i, :], ident[:, :])
                last.then_inc(s_t, 1)
            for t in range(NT):
                pe.wait_ge(s_te, t // QT + 1)
                if t >= 2:
                    pe.wait_ge(s_x, t - 1)
                nc.tensor.matmul(pp[t % 2][:, :], wT[:, t * P:(t + 1) * P], b2s[:, :], start=True, stop=True
                                 ).then_inc(s_p, 1)

        @block.scalar
        def _(act):
            for b in range(B):
                act.wait_ge(s_t, b + 1)
                nc.scalar.activation(wT[:, b * S:(b + 1) * S], pt[b % 2][:, :], ACT.Identity).then_inc(s_te, 1)

        @block.vector
        def _(dve):
            for t in range(NT):
                dve.wait_ge(s_p, t + 1)
                nc.vector.tensor_tensor(x[:, t, :], x[:, t, :], pp[t % 2][:, :], ALU.add).then_inc(s_x, 1)


def sigmoid_column(nc, name, z, out):
    with Stage(nc, name) as st:
        s_e, s_own = st.sem("e"), st.sem("own")
        block = st.block()

        @block.scalar
        def _(act):
            nc.scalar.activation(out, z, ACT.Exp, scale=-1.0).then_inc(s_e, 1)

        @block.vector
        def _(dve):
            own = InOrder(dve, s_own)
            dve.wait_ge(s_e, 1)
            own.after(nc.vector.tensor_scalar(out, out, 1.0, None, ALU.add))
            own.after(nc.vector.reciprocal(out, out))



def load(nc, name, pairs):
    with Stage(nc, name) as st:
        s_ld = st.sem("ld")
        block = st.block()

        @block.sync
        def _(sp):
            for dst, src in pairs:
                sp.dma_start(dst, src).then_inc(s_ld, 16)
            sp.wait_ge(s_ld, 16 * len(pairs))


def rows(ap):
    return ap.rearrange("(t p) n -> p t n", p=P)


def cols(ap):
    return ap.rearrange("(c p) n -> p c n", p=P)




def network(nc, a, out):
    with ExitStack() as ctx:
        def sb(name, shape, dt=F32):
            return ctx.enter_context(nc.sbuf_tensor(name, shape, dt))

        s_stored = ctx.enter_context(nc.semaphore("stored"))
        x = sb("x", [P, NT, D])
        ident = sb("ident", [P, P])
        identb = sb("identb", [P, P], BF16)
        sel_sum = sb("sel_sum", [P, GH])
        tiny = sb("tiny", [P, 1])
        iota = sb("iota", [P, 16])
        tri = sb("tri", [P, P], BF16)
        ones = sb("ones", [P, P])
        onesb = sb("onesb", [P, P], BF16)
        sel_head = nc.dram_tensor("sel_head_bf", [MR, GH, S], BF16).ap()
        qp = nc.dram_tensor("q_parts", [NPART, D, T], BF16).ap()
        kp = nc.dram_tensor("k_parts", [NPART, D, T], BF16).ap()
        vp = nc.dram_tensor("v_padded", [T, H16 * 32], F32).ap()
        scratch = (qp, kp, vp)
        consts = (ident, identb, sel_head, sel_sum)

        with Stage(nc, "setup") as st:
            selh = st.sb("selh", [MR, GH, S])
            trif = st.sb("trif", [P, P])
            selb = st.sb("selb", [MR, GH, S], BF16)
            s_ld, s_cp, s_st = st.sem("ld"), st.sem("cp"), st.sem("st")
            block = st.block()

            @block.sync
            def _(sp):
                for dst, src in ((x[:, :, :], rows(a["x"])), (ident[:, :], a["c_ident"]),
                                 (sel_sum[:, :], a["c_selsum"]), (selh[:, :, :], a["c_selhead"]),
                                 (iota[:, :], a["c_iota"]), (trif[:, :], a["c_tri"])):
                    sp.dma_start(dst, src).then_inc(s_ld, 16)
                sp.wait_ge(s_cp, 2)
                sp.dma_start(sel_head, selb[:, :, :]).then_inc(s_st, 16)
                sp.wait_ge(s_st, 16)
                sp.wait_ge(s_ld, 96)

            @block.vector
            def _(dve):
                nc.vector.memset(tiny[:, :], 1e-11)
                nc.vector.memset(ones[:, :], 1.0)
                nc.vector.memset(onesb[:, :], 1.0)
                dve.wait_ge(s_ld, 96)
                nc.vector.tensor_copy(tri[:, :], trif[:, :])
                nc.vector.tensor_copy(identb[:, :], ident[:, :]).then_inc(s_cp, 1)
                nc.vector.tensor_copy(selb[:, :, :], selh[:, :, :]).then_inc(s_cp, 1)

        def xattn16(name, w, masked):
            with Stage(nc, name) as outer:
                with Stage(nc, name + "a") as st:
                    xn, xnT, cT = st.sb("xn", [P, NT, D]), st.sb("xnT", [P, DC, T]), st.sb("cT", [P, DC, T])
                    load(nc, name + "ld", [(cT[:, :, :], cols(a["ctxT"]))])
                    layernorm(nc, name + "ln", x, xn, xnT, ident)
                    project16(nc, name + "pj", xnT, cT, w, scratch)
                outT = outer.sb("outT", [P, B * NG, S])
                masks = None
                if masked:
                    masks = {"neg_q": outer.sb("neg_q", [P, NT, S], BF16), "neg_k": outer.sb("neg_k", [P, NT, S], BF16),
                             "any_masked": outer.sb("any_masked", [P, NT]),
                             "vmasked": outer.sb("vmasked", [P, B * NG, S])}
                    masks16(nc, name + "mk", a["mask"], a["maskT"], vp, masks["neg_q"], masks["neg_k"],
                            masks["any_masked"], masks["vmasked"])
                    masks["tiny"] = tiny
                attend16(nc, name + "at", scratch, consts, outT, masks)
                output16(nc, name + "wo", outT, w["wo"], w["bo"], x)

        def moe(st, name, xT, router, w1, w2, K, func, E=None, **kw):
            E = router.shape[1]
            logits, weights = st.sb("logits", [P, NT, E]), st.sb("weights", [P, NT, E])
            project_rows(nc, name + "r", xT, router,
                         lambda own, t, psum: nc.vector.tensor_copy(logits[:, t, :], psum))
            route(nc, name + "t", logits, K, weights[:, :, :], iota, tri=tri, ones=onesb, **kw)
            experts(nc, name + "e", xT, w1, w2, weights, x, func)

        xattn16("L0", {k: a["L0_" + k] for k in ("wq", "wk", "wv", "bq", "bk", "bv", "wo", "bo")}, True)
        with Stage(nc, "L0f") as st:
            xn, xnT = st.sb("xn", [P, NT, D]), st.sb("xnT", [P, DC, T])
            layernorm(nc, "L0f0", x, xn, xnT, ident)
            with Stage(nc, "L0g") as st2:
                xn1, att = st2.sb("xn1", [P, NT, D]), st2.sb("att", [P, NT, D])
                layernorm(nc, "L0f1", xn, xn1, xnT, ident, (a["L0_ln1w"], a["L0_ln1b"]))
                small_attention(nc, "L0f2", xnT, a["L0_wqkv"], att)
                transpose_rows(nc, "L0f3", att, xnT, ident)

            def residual(own, t, psum):
                own.after(nc.vector.tensor_tensor(xn[:, t, :], xn[:, t, :], psum, ALU.add))
                return nc.vector.tensor_tensor(x[:, t, :], x[:, t, :], xn[:, t, :], ALU.add)

            project_rows(nc, "L0f4", xnT, a["L0_proj"], residual)
            xn2 = st.sb("xn2", [P, NT, D])
            layernorm(nc, "L0f5", xn, xn2, xnT, ident, (a["L0_ln2w"], a["L0_ln2b"]))
            moe(st, "L0f", xnT, a["L0_router"], a["L0_w1"], a["L0_w2"], 2, ACT.Gelu_apprx_tanh, over_all=True)
        with Stage(nc, "L1x") as st:
            xnT, cT = st.sb("xnT", [P, DC, T]), st.sb("cT", [P, DC, T])
            with Stage(nc, "L1y") as st2:
                xn = st2.sb("xn", [P, NT, D])
                load(nc, "L1ld", [(cT[:, :, :], cols(a["ctxT"]))])
                layernorm(nc, "L1ln", x, xn, xnT, ident)
            masks = (st.sb("am", [P, NT, S]), st.sb("mk_col", [P, NT]), st.sb("uT", [P, B, QT * (QT + 1) // 2 * P]),
                     st.sb("sufmax", [P, NT]), st.sb("usum", [P, NT]))
            causal_masks(nc, "L1m", a, *masks, ident)
            attend64(nc, "L1a", a, xnT, cT, masks, x, ident, identb, ones)
        with Stage(nc, "L1f") as st:
            xnT = st.sb("xnT", [P, DC, T])
            with Stage(nc, "L1g") as st2:
                layernorm(nc, "L1f0", x, st2.sb("xn", [P, NT, D]), xnT, ident)
            moe(st, "L1f", xnT, a["L1_router"], a["L1_w1"], a["L1_w2"], 2, ACT.Gelu_apprx_tanh, over_all=True,
                capacity=T // 8)
            add_rows(nc, "L1fb", a["L1_bias"], x)
        with Stage(nc, "L2x") as st:
            xnT, cT = st.sb("xnT", [P, DC, T]), st.sb("cT", [P, DC, T])
            hqT, crow = st.sb("hqT", [P, DC, T]), st.sb("crow", [P, NT, D])
            mcol = st.sb("mcol", [P, NT])
            load(nc, "L2ld", [(cT[:, :, :], cols(a["ctxT"])), (crow[:, :, :], rows(a["ctx"]))])
            with Stage(nc, "L2y") as st2:
                layernorm(nc, "L2ln", x, st2.sb("xn", [P, NT, D]), xnT, ident)
            similarity(nc, "L2s", a, xnT, cT, crow, hqT, mcol, ident)
            xhT, xcT = st.sb("xhT", [P, DC, T]), st.sb("xcT", [P, DC, T])
            attended_row(nc, "L2r", xnT, hqT, mcol, xhT, xcT, ident, ones)
            project_parts(nc, "L2p", (xnT, hqT, xhT, xcT), a["L2_Wqv"], a["L2_bqv"], x)
        with Stage(nc, "L2f") as st:
            xnT = st.sb("xnT", [P, DC, T])
            with Stage(nc, "L2g") as st2:
                layernorm(nc, "L2f0", x, st2.sb("xn", [P, NT, D]), xnT, ident)
            logits, weights = st.sb("logits", [P, NT, 17]), st.sb("weights", [P, NT, 17])
            project_rows(nc, "L2fr", xnT, a["L2_router"],
                         lambda own, t, psum: nc.vector.tensor_copy(logits[:, t, :], psum))
            route(nc, "L2ft", logits[:, :, 0:16], 2, weights[:, :, 0:16], iota)
            sigmoid_column(nc, "L2fs", logits[:, :, 16:17], weights[:, :, 16:17])
            experts(nc, "L2fe", xnT, a["L2_wg"], a["L2_wd"], weights, x, ACT.Silu, a["L2_wu"],
                    w_of=lambda e: min(e, 16))
        xattn16("L3", {k: a["L3_" + k] for k in ("wq", "wk", "wv", "bq", "bk", "bv", "wo", "bo")}, False)
        with Stage(nc, "L3f") as st:
            xnT, h = st.sb("xnT", [P, DC, T]), st.sb("h", [P, NT, D])
            layernorm(nc, "L3f0", x, h, xnT, ident)
            z = st.sb("z", [P, NT, 36])
            wts = [st.sb(f"wt{i}", [P, NT, 12]) for i in range(3)]
            address_scores(nc, "L3fa", xnT, a["L3_P"], a["L3_U"], z)
            for i in range(3):
                route(nc, f"L3ft{i}", z[:, :, 12 * i:12 * i + 12], 3, wts[i][:, :, :], iota)
            mixture(nc, "L3fm", xnT, a["L3_W1"], wts[0], h, True)
            gelu_rows(nc, "L3fg", h)
            transpose_rows(nc, "L3fh", h, xnT, ident)
            mixture(nc, "L3fn", xnT, a["L3_W2"], wts[1], x, False)
            add_choice(nc, "L3fb", wts[2], a["L3_b2"], x, ident)

        with Stage(nc, "store") as st:
            block = st.block()

            @block.sync
            def _(sp):
                sp.dma_start(rows(out), x[:, :, :]).then_inc(s_stored, 16)
                sp.wait_ge(s_stored, 16)


def kernel(**inputs):
    import numpy as np
    import concourse.bacc as _bacc
    from concourse.bass_utils import run_bass_kernel_spmd as _run

    i = {k: np.asarray(v) for k, v in inputs.items()}
    c = np.ascontiguousarray
    f32 = np.float32

    def pad_heads(w):
        out = np.zeros((H16, 32, w.shape[1]), f32)
        out[:, :HD] = w.reshape(H16, HD, w.shape[1])
        return out.reshape(H16 * 32, w.shape[1])

    Stage.USED.clear()
    a = {"x": i["x"].reshape(T, D), "ctxT": c(i["ctx_1024"].reshape(T, D).T),
         "mask": i["mask_BxSxS2_ik1"], "maskT": c(i["mask_BxSxS2_ik1"].transpose(0, 2, 1)),
         "c_ident": np.eye(P, dtype=f32)}
    selsum = np.zeros((P, GH), f32)
    for h in range(GH):
        selsum[32 * h + HD, h] = 1.0
    a["c_selsum"] = selsum
    selhead = np.zeros((NPART, GH, GH, S), f32)
    for h in range(GH):
        selhead[:, h, h, :] = 1.0
    a["c_selhead"] = selhead.reshape(MR, GH, S)
    for k in ("wq", "wk", "wv"):
        a["L0_" + k] = c(i["L0_xattn_" + k].T)
    for k in ("bq", "bk", "bv", "bo"):
        a["L0_" + k] = i["L0_xattn_" + k]
    a["L0_wo"] = pad_heads(i["L0_xattn_wo"].T)
    a["c_iota"] = np.tile(np.arange(16, dtype=f32), (P, 1))
    a["c_tri"] = np.triu(np.ones((P, P), f32), 1)
    for k in ("ln1w", "ln1b", "ln2w", "ln2b"):
        a["L0_" + k] = i["L0_ffn_" + k[:3] + {"w": "_weight", "b": "_bias"}[k[3]]]
    a["L0_wqkv"] = c(i["L0_ffn_qkv_weight"].T)
    a["L0_proj"] = c(i["L0_ffn_proj_weight"].T)
    a["L0_router"] = c(i["L0_ffn_router_weight"].T)
    a["L0_w1"], a["L0_w2"] = i["L0_ffn_moe_w1"], i["L0_ffn_moe_w2"]
    for k in "QKV":
        a["L1_W" + k] = c(i["L1_xattn_W_" + k].transpose(1, 0, 2).reshape(D, H16 * HB))
    for k in "QK":
        a["L1_b" + k] = c(i["L1_xattn_b_" + k].reshape(NP, P).T)
    a["L1_bV"] = i["L1_xattn_b_V"].reshape(-1)
    a["L1_WO"], a["L1_bO"] = i["L1_xattn_W_O"].reshape(H16 * HB, D), i["L1_xattn_b_O"]
    a["addm"] = i["mask_Bx1x1xS2_ff0"].reshape(T)
    a["addm_col"] = c(a["addm"].reshape(NT, P).T)
    is_later = np.arange(S)[None, :] > np.arange(S)[:, None]
    a["c_later"] = c(np.where(is_later, f32(BIG), f32(0)).reshape(QT, P, S).transpose(1, 0, 2))
    a["c_fill"] = c(np.where(is_later, f32(-1e5), f32(BIG)).reshape(QT, P, S).transpose(1, 0, 2))
    selm = np.zeros((P, P), f32)
    selc = np.zeros((P, 2), f32)
    for h in range(2):
        selm[h * HB:h * HB + NPART] = 1.0
        selc[h * HB, h] = 1.0
    a["c_selm"], a["c_selc"] = selm, selc
    a["L1_router"] = i["L1_ffn_router_w"]
    a["L1_w1"], a["L1_w2"], a["L1_bias"] = i["L1_ffn_w1"], i["L1_ffn_w2"], i["L1_ffn_bias"].reshape(D)
    a["ctx"] = i["ctx_1024"].reshape(T, D)
    a["L2_wsim"] = c(i["L2_xattn_w_sim"].reshape(3, DC, P).transpose(2, 0, 1))
    a["L2_bsim"], a["L2_Wqv"], a["L2_bqv"] = i["L2_xattn_b_sim"], i["L2_xattn_W_qv"], i["L2_xattn_b_qv"]
    a["L2_router"] = c(np.concatenate([i["L2_ffn_Wg"], i["L2_ffn_Wsg"]]).T)
    for k, n in (("g", "gate"), ("u", "up")):
        shared = i["L2_ffn_Ws_" + n].reshape(4, P, D)
        a["L2_w" + k] = c(np.concatenate([i["L2_ffn_We_" + n], shared]).transpose(0, 2, 1))
    shared = i["L2_ffn_Ws_down"].T.reshape(4, P, D)
    a["L2_wd"] = c(np.concatenate([i["L2_ffn_We_down"].transpose(0, 2, 1), shared]))
    kv = i["L3_xattn_Wkv"].reshape(D, H16, 2, HD)
    bkv = i["L3_xattn_bkv"].reshape(H16, 2, HD)
    a["L3_wq"], a["L3_bq"] = i["L3_xattn_Wq"], i["L3_xattn_bq"]
    for j, k in enumerate("kv"):
        a["L3_w" + k], a["L3_b" + k] = c(kv[:, :, j].reshape(D, D)), c(bkv[:, j].reshape(D))
    a["L3_wo"], a["L3_bo"] = pad_heads(i["L3_xattn_Wp"]), i["L3_xattn_bp"]
    a["L3_P"] = c(i["L3_ffn_P_w"].T)
    a["L3_U"] = c(np.concatenate([i["L3_ffn_U1"], i["L3_ffn_U2"], i["L3_ffn_U3"]]).T)
    a["L3_W1"], a["L3_W2"] = c(i["L3_ffn_W1"].transpose(0, 2, 1)), c(i["L3_ffn_W2"].transpose(0, 2, 1))
    a["L3_b2"] = i["L3_ffn_b2"]

    nc = _bacc.Bacc("TRN2", target_bir_lowering=False, num_devices=1)
    arrays, aps = {}, {}
    for name, v in a.items():
        v = c(v)
        arrays[f"in_{name}"] = v
        aps[name] = nc.dram_tensor(f"in_{name}", v.shape, mybir.dt.from_np(v.dtype), kind="ExternalInput").ap()
    out = nc.dram_tensor("out_0", (T, D), F32, kind="ExternalOutput").ap()
    network(nc, aps, out)
    r = _run(nc, [arrays], core_ids=[0])
    return r.results[0]["out_0"].reshape(B, S, D)
```

```python
import concourse.bass as bass
from concourse import mybir
from contextlib import ExitStack

F32 = mybir.dt.float32
BF16 = mybir.dt.bfloat16
I32 = mybir.dt.int32
U32 = mybir.dt.uint32
ALU = mybir.AluOpType
ACT = mybir.ActivationFunctionType
AX = mybir.AxisListType

P = 128
D = 256
DC = D // P
B = 4
S = 512
T = B * S
NT = T // P
QT = S // P
BIG = -1.0e30
EPS = 1e-5

H16 = 16
HD = 16
GH = 4
NG = H16 // GH
NPART = 3
Q_PARTS = (0, 0, 1, 0, 2, 1)
K_PARTS = (0, 1, 0, 2, 0, 1)
KR = len(Q_PARTS) * HD
MR = NPART * GH


class Stage:

    USED = []

    def __init__(self, nc, name):
        self.nc, self.name, self.ctx, self.sems = nc, name, ExitStack(), []

    def __enter__(self):
        self.ctx.__enter__()
        return self

    def __exit__(self, *a):
        self.ctx.__exit__(*a)
        self.USED.extend(self.sems)
        if len(self.USED) > 100:
            self.nc.clear_and_free_semaphores(list(self.USED))
            self.nc.all_engine_barrier()
            self.USED.clear()

    def sb(self, name, shape, dt=F32):
        return self.ctx.enter_context(self.nc.sbuf_tensor(f"{self.name}_{name}", shape, dt))

    def ps(self, name, shape, dt=F32):
        return self.ctx.enter_context(self.nc.psum_tensor(f"{self.name}_{name}", shape, dt))

    def sem(self, name):
        self.sems.append(self.nc.alloc_semaphore(f"{self.name}_{name}"))
        return self.sems[-1]

    def block(self):
        return self.ctx.enter_context(self.nc.Block())


class InOrder:

    def __init__(self, eng, sem):
        self.eng, self.sem, self.n = eng, sem, 0

    def after(self, ins):
        self.n += 1
        ins.then_inc(self.sem, 1)
        self.eng.wait_ge(self.sem, self.n)


def layernorm(nc, name, x, xn, xnT, ident, affine=None):
    with Stage(nc, name) as st:
        stats = st.sb("stats", [P, NT, 6])
        mv = st.sb("mv", [P, NT, 2])
        ve = st.sb("ve", [P, NT])
        std = st.sb("std", [P, NT])
        rstd = st.sb("rstd", [P, NT])
        wb = st.sb("wb", [P, 2, DC])
        tp = [st.ps(f"tp{i}", [P, S]) for i in range(4)]
        s_own, s_var, s_std, s_norm, s_tr, s_ev, s_wb = (
            st.sem(n) for n in ("own", "var", "std", "norm", "tr", "ev", "wb"))
        block = st.block()

        @block.sync
        def _(sp):
            if affine is not None:
                for i in range(2):
                    for c in range(DC):
                        sp.dma_start(wb[:, i, c:c + 1], affine[i][c * P:(c + 1) * P].unsqueeze(1)).then_inc(s_wb, 16)

        @block.vector
        def _(dve):
            own = InOrder(dve, s_own)
            for t in range(NT):
                last = nc.vector.bn_stats(stats[:, t, :], x[:, t, :])
            own.after(last)
            for t in range(NT):
                last = nc.vector.bn_aggr(mv[:, t, :], stats[:, t, :])
            own.after(last)
            nc.vector.tensor_scalar(ve[:, :], mv[:, :, 1], EPS, None, ALU.add).then_inc(s_var, 1)
            dve.wait_ge(s_std, 1)
            own.after(nc.vector.reciprocal(rstd[:, :], std[:, :]))
            for t in range(NT):
                nc.vector.tensor_scalar(xn[:, t, :], x[:, t, :], mv[:, t, 0:1], rstd[:, t:t + 1],
                                        ALU.subtract, ALU.mult).then_inc(s_norm, 1)

        @block.tensor
        def _(pe):
            for n in range(B * DC):
                g, c = n // DC, n % DC
                pe.wait_ge(s_norm, QT * (g + 1))
                if n >= 4:
                    pe.wait_ge(s_ev, n - 3)
                for i in range(QT):
                    last = nc.tensor.transpose(tp[n % 4][:, i * P:(i + 1) * P],
                                               xn[:, g * QT + i, c * P:(c + 1) * P], ident[:, :])
                last.then_inc(s_tr, 1)

        @block.scalar
        def _(act):
            act.wait_ge(s_var, 1)
            nc.scalar.activation(std[:, :], ve[:, :], ACT.Sqrt).then_inc(s_std, 1)
            if affine is not None:
                act.wait_ge(s_wb, 16 * 2 * DC)
            for n in range(B * DC):
                g, c = n // DC, n % DC
                act.wait_ge(s_tr, n + 1)
                dst = xnT[:, c, g * S:(g + 1) * S]
                if affine is None:
                    nc.scalar.activation(dst, tp[n % 4][:, :], ACT.Identity).then_inc(s_ev, 1)
                else:
                    nc.scalar.activation(dst, tp[n % 4][:, :], ACT.Identity, bias=wb[:, 1, c:c + 1],
                                         scale=wb[:, 0, c:c + 1]).then_inc(s_ev, 1)


def project16(nc, name, srcT_q, srcT_kv, w, scratch):
    qp, kp, vp = scratch
    scale = HD ** -0.5
    with Stage(nc, name) as st:
        wsb = {k: st.sb("w" + k, [P, DC, D]) for k in "qkv"}
        bqk = st.sb("bqk", [P, 2, DC])
        bv = st.sb("bv", [P, D])
        full = st.sb("full", [P, 2, S])
        rest = st.sb("rest", [P, 2, S])
        parts = st.sb("parts", [P, 2, NPART, S], BF16)
        vt = st.sb("vt", [P, 2, H16, 32])
        pj = [st.ps(f"pj{i}", [P, S]) for i in range(4)]
        pv = [st.ps(f"pv{i}", [P, D]) for i in range(2)]
        s_w, s_pj, s_full, s_hi, s_rest, s_mid, s_low, s_pv, s_vt, s_own = (
            st.sem(n) for n in ("w", "pj", "full", "hi", "rest", "mid", "low", "pv", "vt", "own"))
        s_out = [st.sem(f"out{i}") for i in range(2)]
        s_vo = [st.sem(f"vo{i}") for i in range(2)]
        JOBS = [(k, hb, b) for b in range(B) for k in range(2) for hb in range(DC)]
        block = st.block()

        @block.sync
        def _(sp):
            for k in "qkv":
                sp.dma_start(wsb[k][:, :, :], w["w" + k].rearrange("(c p) n -> p c n", p=P)).then_inc(s_w, 16)
            for i, k in enumerate("qk"):
                for c in range(DC):
                    sp.dma_start(bqk[:, i, c:c + 1], w["b" + k][c * P:(c + 1) * P].unsqueeze(1)).then_inc(s_w, 16)
            sp.dma_start(bv[:, :], w["bv"].partition_broadcast(P)).then_inc(s_w, 16)
            for j, (k, hb, b) in enumerate(JOBS):
                sp.wait_ge(s_low, j + 1)
                dst = (qp, kp)[k][:, hb * P:(hb + 1) * P, b * S:(b + 1) * S].rearrange("a p n -> p a n")
                sp.dma_start(dst, parts[:, j % 2, :, :]).then_inc(s_out[j % 2], 16)
            for i in range(2):
                sp.wait_ge(s_out[i], 16 * (len(JOBS) // 2))
                sp.wait_ge(s_vo[i], 16 * (NT // 2))

        @block.tensor
        def _(pe):
            pe.wait_ge(s_w, 16 * 8)
            for j, (k, hb, b) in enumerate(JOBS):
                if j >= 4:
                    pe.wait_ge(s_full, j - 3)
                src = (srcT_q, srcT_kv)[k]
                for c in range(DC):
                    last = nc.tensor.matmul(pj[j % 4][:, :], wsb["qk"[k]][:, c, hb * P:(hb + 1) * P],
                                            src[:, c, b * S:(b + 1) * S], start=(c == 0), stop=(c == DC - 1))
                last.then_inc(s_pj, 1)
                t = j
                if t >= 2:
                    pe.wait_ge(s_vt, t - 1)
                for c in range(DC):
                    last = nc.tensor.matmul(pv[t % 2][:, :], srcT_kv[:, c, t * P:(t + 1) * P],
                                            wsb["v"][:, c, :], start=(c == 0), stop=(c == DC - 1))
                last.then_inc(s_pv, 1)

        @block.vector
        def _(dve):
            own = InOrder(dve, s_own)
            own.after(nc.vector.memset(vt[:, :, :, :], 0.0))
            own.after(nc.vector.memset(vt[:, :, :, HD:HD + 1], 1.0))
            dve.wait_ge(s_w, 16 * 8)
            for j, (k, hb, b) in enumerate(JOBS):
                dve.wait_ge(s_pj, j + 1)
                if j >= 2:
                    dve.wait_ge(s_low, j - 1)
                nc.vector.tensor_scalar(full[:, j % 2, :], pj[j % 4][:, :], bqk[:, k, hb:hb + 1],
                                        scale if k == 0 else 1.0, ALU.add, ALU.mult).then_inc(s_full, 1)
                dve.wait_ge(s_hi, j + 1)
                nc.vector.tensor_tensor(rest[:, j % 2, :], full[:, j % 2, :], parts[:, j % 2, 0, :],
                                        ALU.subtract).then_inc(s_rest, 1)
                dve.wait_ge(s_pv, j + 1)
                if j >= 2:
                    dve.wait_ge(s_vo[j % 2], 16 * (j // 2))
                nc.vector.tensor_tensor(vt[:, j % 2, :, 0:HD], pv[j % 2][:, :].rearrange("p (h d) -> p h d", h=H16),
                                        bv[:, :].rearrange("p (h d) -> p h d", h=H16), ALU.add).then_inc(s_vt, 1)

        @block.scalar
        def _(act):
            for j in range(len(JOBS)):
                act.wait_ge(s_full, j + 1)
                if j >= 2:
                    act.wait_ge(s_out[j % 2], 16 * (j // 2))
                nc.scalar.activation(parts[:, j % 2, 0, :], full[:, j % 2, :], ACT.Identity).then_inc(s_hi, 1)
                act.wait_ge(s_rest, j + 1)
                nc.scalar.activation(parts[:, j % 2, 1, :], rest[:, j % 2, :], ACT.Identity).then_inc(s_mid, 1)

        @block.gpsimd
        def _(pool):
            for j in range(len(JOBS)):
                pool.wait_ge(s_mid, j + 1)
                nc.gpsimd.tensor_tensor(parts[:, j % 2, 2, :], rest[:, j % 2, :], parts[:, j % 2, 1, :],
                                        ALU.subtract).then_inc(s_low, 1)
                pool.wait_ge(s_vt, j + 1)
                pool.dma_start(vp[j * P:(j + 1) * P, :], vt[:, j % 2, :, :].rearrange("p h d -> p (h d)")
                               ).then_inc(s_vo[j % 2], 16)


def masks16(nc, name, mask, maskT, vp, neg_q, neg_k, any_masked, vmasked):
    with Stage(nc, name) as st:
        mi = st.sb("mi", [P, 2, S], I32)
        mk = st.sb("mk", [P, QT, S], I32)
        zk = st.sb("zk", [P, QT, S])
        vs = st.sb("vs", [P, QT, H16 * 32])
        vm = [st.ps(f"vm{i}", [P, S]) for i in range(2)]
        s_mi = [st.sem(f"mi{i}") for i in range(2)]
        s_q, s_mk, s_vs, s_z, s_vm, s_own, s_vsum, s_row = (
            st.sem(n) for n in ("q", "mk", "vs", "z", "vm", "own", "vsum", "row"))
        block = st.block()

        @block.sync
        def _(sp):
            for t in range(NT):
                if t >= 2:
                    sp.wait_ge(s_row, t - 1)
                sp.dma_start(mi[:, t % 2, :], mask[t // QT, (t % QT) * P:(t % QT + 1) * P, :]).then_inc(s_mi[t % 2], 16)

        @block.scalar
        def _(act):
            for b in range(B):
                if b >= 1:
                    act.wait_ge(s_z, 2 * QT * b)
                    act.wait_ge(s_vm, NG * b)
                act.dma_start(mk[:, :, :], maskT[b].rearrange("(t p) q -> p t q", p=P)).then_inc(s_mk, 16)
                act.dma_start(vs[:, :, :], vp[b * S:(b + 1) * S, :].rearrange("(t p) n -> p t n", p=P)
                              ).then_inc(s_vs, 16)
                for g in range(NG):
                    n = b * NG + g
                    act.wait_ge(s_vm, n + 1)
                    nc.scalar.activation(vmasked[:, n, :], vm[n % 2][:, :], ACT.Identity).then_inc(s_vsum, 1)

        @block.vector
        def _(dve):
            for t in range(NT):
                dve.wait_ge(s_mi[t % 2], 16 * (t // 2 + 1))
                nc.vector.tensor_scalar(neg_q[:, t, :], mi[:, t % 2, :], 0.0, BIG, ALU.is_equal, ALU.mult
                                        ).then_inc(s_q, 1)
                dve.wait_ge(s_q, t + 1)
                nc.vector.tensor_reduce(any_masked[:, t:t + 1], neg_q[:, t, :], AX.X, ALU.min).then_inc(s_row, 1)
            dve.wait_ge(s_row, NT)
            own = InOrder(dve, s_own)
            own.after(nc.vector.tensor_scalar(any_masked[:, :], any_masked[:, :], 0.0, BIG, ALU.is_equal, ALU.mult))
            own.after(nc.vector.tensor_scalar(any_masked[:, :], any_masked[:, :], 1e-11, None, ALU.add))
            for b in range(B):
                dve.wait_ge(s_mk, 16 * (b + 1))
                if b >= 1:
                    dve.wait_ge(s_vm, NG * b)
                for t in range(QT):
                    nc.vector.tensor_scalar(neg_k[:, b * QT + t, :], mk[:, t, :], 0.0, BIG, ALU.is_equal, ALU.mult
                                            ).then_inc(s_z, 1)
                    nc.vector.tensor_scalar(zk[:, t, :], mk[:, t, :], 0.0, None, ALU.is_equal).then_inc(s_z, 1)

        @block.tensor
        def _(pe):
            for b in range(B):
                pe.wait_ge(s_z, 2 * QT * (b + 1))
                pe.wait_ge(s_vs, 16 * (b + 1))
                for g in range(NG):
                    n = b * NG + g
                    if n >= 2:
                        pe.wait_ge(s_vsum, n - 1)
                    for t in range(QT):
                        last = nc.tensor.matmul(vm[n % 2][:, :], vs[:, t, g * P:(g + 1) * P], zk[:, t, :],
                                                start=(t == 0), stop=(t == QT - 1))
                    last.then_inc(s_vm, 1)


def attend16(nc, name, scratch, consts, outT, masks=None):
    qp, kp, vp = scratch
    ident, identb, sel_head, sel_sum = consts
    N = B * NG
    R = 4
    with Stage(nc, name) as st:
        qs = st.sb("qs", [P, R, GH, S], BF16)
        ks = st.sb("ks", [P, R, GH, S], BF16)
        vs = st.sb("vs", [P, R, QT, P])
        junk = st.sb("junk", [P, 2, S], BF16)
        rowmax = st.sb("rowmax", [P, 2, QT, GH])
        neg = st.sb("neg", [P, R, QT, GH])
        negr = st.sb("negr", [P, QT, GH])
        negp = st.sb("negp", [P, QT, P], BF16)
        prob = st.sb("prob", [P, 2, GH, 2, S])
        expand = st.sb("expand", [P, QT, GH, 32])
        em = st.sb("em", [P, QT, GH])
        rec = st.sb("rec", [P, QT, GH])
        oT = st.sb("oT", [P, S])
        sq = [st.ps(f"sq{i}", [P, S]) for i in range(2)]
        sk = [st.ps(f"sk{i}", [P, 2, S]) for i in range(2)]
        acc = st.ps("acc", [P, S])
        misc = st.ps("misc", [P, S])
        miscb = misc[:, :].bitcast(BF16)[:, 0:S]
        s_q = [st.sem(f"q{i}") for i in range(R)]
        s_v = [st.sem(f"v{i}") for i in range(R)]
        (s_sq, s_max, s_negp, s_mt, s_qm, s_sk, s_exp, s_pv, s_em, s_ex, s_eb, s_o,
         s_sum, s_rec, s_rb, s_out, s_own, s_am, s_hd) = (
            st.sem(n) for n in ("sq", "max", "negp", "mt", "qm", "sk", "exp", "pv", "em",
                                "ex", "eb", "o", "sum", "rec", "rb", "out", "own", "am", "hd"))
        block = st.block()
        NB = 1 if masks is None else 2

        @block.sync
        def _(sp):
            for i in range(R):
                sp.dma_start(ks[KR:KR + MR, i, :, :], sel_head).then_inc(s_hd, 16)
            for n in range(N):
                b, g = n // NG, n % NG
                if n >= R:
                    sp.wait_ge(s_sk, 8 * (n - R + 1))
                for buf, src, order in ((qs, qp, Q_PARTS), (ks, kp, K_PARTS)):
                    for i, a in enumerate(order):
                        sp.dma_start(buf[i * HD:(i + 1) * HD, n % R, :, :],
                                     src[a, g * GH * HD:(g + 1) * GH * HD, b * S:(b + 1) * S]
                                     .rearrange("(h d) n -> d h n", h=GH)).then_inc(s_q[n % R], 16)
                if n >= R:
                    sp.wait_ge(s_pv, 2 * (n - R + 1))
                sp.dma_start(vs[:, n % R, :, :], vp[b * S:(b + 1) * S, g * P:(g + 1) * P]
                             .rearrange("(t p) n -> p t n", p=P)).then_inc(s_v[n % R], 16)

        @block.tensor
        def _(pe):
            def row_scores(n, i):
                h, t = i // QT, i % QT
                k = n * GH * QT + i
                if k >= 2:
                    pe.wait_ge(s_max, k - 1)
                nc.tensor.matmul(sq[k % 2][:, :], qs[0:KR, n % R, h, t * P:(t + 1) * P], ks[0:KR, n % R, h, :],
                                 start=True, stop=True).then_inc(s_sq, 1)

            def turn_max(n):
                pe.wait_ge(s_negp, n + 1)
                if n >= 1:
                    pe.wait_ge(s_qm, n)
                if n >= 3:
                    pe.wait_ge(s_out, n - 2)
                for t in range(QT):
                    last = nc.tensor.transpose(miscb[:, t * P:(t + 1) * P], negp[:, t, :], identb[:, :])
                last.then_inc(s_mt, 1)

            def key_scores(n, u):
                h, k = u % GH, n * 8 + u
                if k >= 2:
                    pe.wait_ge(s_exp, k - 1)
                for i in range(2):
                    t = 2 * (u // GH) + i
                    last = nc.tensor.matmul(sk[k % 2][:, i, :], ks[0:KR + MR, n % R, h, t * P:(t + 1) * P],
                                            qs[0:KR + MR, n % R, h, :], start=True, stop=(masks is None))
                    if masks is not None:
                        last = nc.tensor.matmul(sk[k % 2][:, i, :], identb[:, :],
                                                masks["neg_k"][:, (n // NG) * QT + t, :], start=False, stop=True)
                last.then_inc(s_sk, 1)

            def values(n, half):
                pe.wait_ge(s_exp, n * 8 + 4 * half + 4)
                if half == 0:
                    pe.wait_ge(s_v[n % R], 16 * (n // R + 1))
                    if n >= 1:
                        pe.wait_ge(s_o, n)
                for i in range(2):
                    for h in range(GH):
                        t = 2 * half + i
                        last = nc.tensor.matmul(acc[32 * h:32 * h + 32, :], vs[:, n % R, t, 32 * h:32 * h + 32],
                                                prob[:, half, h, i, :], start=(t == 0), stop=(t == QT - 1),
                                                tile_position=(0, 32 * h), skip_group_check=True)
                last.then_inc(s_pv, 1)

            def broadcast(n, which):
                pe.wait_ge(s_ex, NB * n + which + 1)
                if which == 0:
                    pe.wait_ge(s_qm, min(n + 3, N))
                for t in range(QT):
                    last = nc.tensor.transpose(misc[:, t * P:(t + 1) * P],
                                               expand[:, t, :, :].rearrange("p h d -> p (h d)"), ident[:, :])
                last.then_inc(s_rb if which == NB - 1 else s_eb, 1)

            def sums(n):
                pe.wait_ge(s_o, n + 1)
                pe.wait_ge(s_qm, min(n + 3, N))
                for t in range(QT):
                    last = nc.tensor.matmul(misc[:, t * GH:(t + 1) * GH], oT[:, t * P:(t + 1) * P], sel_sum[:, :],
                                            start=True, stop=True)
                last.then_inc(s_sum, 1)

            pe.wait_ge(s_hd, 16 * R)
            for s in range(N + 3):
                if s < N:
                    pe.wait_ge(s_q[s % R], 16 * 12 * (s // R + 1))
                keys, last_group = 2 <= s < N + 2, s >= 3
                for u in range(8):
                    if u == 0 and 1 <= s <= N:
                        turn_max(s - 1)
                    if keys:
                        if u == 0:
                            pe.wait_ge(s_qm, s - 1)
                        key_scores(s - 2, u)
                    if last_group:
                        if u == 1:
                            values(s - 3, 1)
                        if u == 3 and masks is not None:
                            broadcast(s - 3, 0)
                        if u == 5:
                            sums(s - 3)
                        if u == 7:
                            broadcast(s - 3, NB - 1)
                    if s < N:
                        row_scores(s, 2 * u)
                        row_scores(s, 2 * u + 1)
                    if keys and u == 6:
                        values(s - 2, 0)

        @block.vector
        def _(dve):
            own = InOrder(dve, s_own)
            own.after(nc.vector.memset(negp[:, :, :], 0.0))

            def row_max(n, i):
                h, t = i // QT, i % QT
                k = n * GH * QT + i
                dve.wait_ge(s_sq, k + 1)
                dst = rowmax[:, n % 2, t, h:h + 1]
                if masks is None:
                    ins = nc.vector.tensor_reduce(dst, sq[k % 2][:, :], AX.X, ALU.max)
                else:
                    if k >= 2:
                        dve.wait_ge(s_max, k - 1)
                    ins = nc.vector.tensor_tensor_reduce(junk[:, k % 2, :], sq[k % 2][:, :],
                                                         masks["neg_q"][:, (n // NG) * QT + t, :], 1.0, 3.0 * BIG,
                                                         ALU.add, ALU.max, dst)
                ins.then_inc(s_max, 1)

            def minus_max(n):
                dve.wait_ge(s_max, GH * QT * (n + 1))
                m, x = rowmax[:, n % 2, :, :], neg[:, n % R, :, :]
                if masks is not None:
                    for t in range(QT):
                        c = (n // NG) * QT + t
                        last = nc.vector.tensor_scalar(m[:, t, :], m[:, t, :], masks["any_masked"][:, c:c + 1], None,
                                                       ALU.max)
                    own.after(last)
                if n >= R and masks is not None:
                    dve.wait_ge(s_em, n - R + 1)
                own.after(nc.vector.tensor_scalar(x, m, -1.0, None, ALU.mult))
                if n >= 1:
                    dve.wait_ge(s_mt, n)
                part = [negp[:, :, KR + a * GH:KR + (a + 1) * GH] for a in range(NPART)]
                own.after(nc.vector.tensor_copy(part[0], x))
                own.after(nc.vector.tensor_tensor(negr[:, :, :], x, part[0], ALU.subtract))
                own.after(nc.vector.tensor_copy(part[1], negr[:, :, :]))
                nc.vector.tensor_tensor(part[2], negr[:, :, :], part[1], ALU.subtract).then_inc(s_negp, 1)

            def gather(n):
                if n >= 1:
                    dve.wait_ge(s_out, n)
                if masks is not None:
                    dve.wait_ge(s_eb, n + 1)
                    own.after(nc.vector.tensor_tensor(oT[:, :], misc[:, :], masks["vmasked"][:, n, :], ALU.mult))
                    dve.wait_ge(s_pv, 2 * (n + 1))
                    nc.vector.tensor_tensor(oT[:, :], acc[:, :], oT[:, :], ALU.add).then_inc(s_o, 1)
                else:
                    dve.wait_ge(s_pv, 2 * (n + 1))
                    nc.vector.tensor_copy(oT[:, :], acc[:, :]).then_inc(s_o, 1)

            def spread(n, what, k):
                if n >= 1 or k:
                    dve.wait_ge(s_rb if (masks is None or k == 0) else s_eb, n if (masks is None or k == 0) else n + 1)
                nc.vector.tensor_copy(expand[:, :, :, :], what[:, :, :].unsqueeze(3).to_broadcast([P, QT, GH, 32])
                                      ).then_inc(s_ex, 1)

            def invert(n):
                dve.wait_ge(s_sum, n + 1)
                own.after(nc.vector.reciprocal(rec[:, :, :], misc[:, 0:QT * GH].rearrange("p (t h) -> p t h", t=QT)))
                spread(n, rec, NB - 1)

            def finish(n):
                dve.wait_ge(s_rb, n + 1)
                nc.vector.tensor_tensor(outT[:, n, :], oT[:, :], misc[:, :], ALU.mult).then_inc(s_out, 1)

            for s in range(N + 3):
                for u in range(8):
                    if s >= 3:
                        if u == 1 and masks is not None:
                            dve.wait_ge(s_em, s - 2)
                            spread(s - 3, em, 0)
                        if u == 4:
                            gather(s - 3)
                        if u == 6:
                            invert(s - 3)
                    if s < N:
                        row_max(s, 2 * u)
                        row_max(s, 2 * u + 1)
                if s >= 3:
                    finish(s - 3)
                if s < N:
                    minus_max(s)

        @block.scalar
        def _(act):
            for s in range(N + 3):
                for u in range(8):
                    if 2 <= s < N + 2:
                        n = s - 2
                        k = n * 8 + u
                        act.wait_ge(s_sk, k + 1)
                        if n >= 1:
                            act.wait_ge(s_pv, 2 * (n - 1) + u // GH + 1)
                        nc.scalar.activation(prob[:, u // GH, u % GH, :, :], sk[k % 2][:, :, :], ACT.Exp
                                             ).then_inc(s_exp, 1)
                    if u == 0 and s >= 3 and masks is not None:
                        if s >= 4:
                            act.wait_ge(s_ex, NB * (s - 4) + 1)
                        act.wait_ge(s_negp, s - 2)
                        nc.scalar.activation(em[:, :, :], neg[:, (s - 3) % R, :, :], ACT.Exp, bias=masks["tiny"][:, 0:1]
                                             ).then_inc(s_em, 1)
                    if u == 0 and 1 <= s <= N:
                        act.wait_ge(s_mt, s)
                        nc.scalar.activation(qs[KR:KR + MR, (s - 1) % R, :, :],
                                             miscb[KR:KR + MR, :].unsqueeze(1).to_broadcast([MR, GH, S]), ACT.Identity
                                             ).then_inc(s_qm, 1)


def output16(nc, name, aT, wo, bo, x):
    with Stage(nc, name) as st:
        w = st.sb("w", [P, NG, D])
        bb = st.sb("bb", [P, D])
        pp = [st.ps(f"pp{i}", [P, D]) for i in range(4)]
        s_w, s_p, s_x, s_b = (st.sem(n) for n in ("w", "p", "x", "b"))
        block = st.block()

        @block.sync
        def _(sp):
            sp.dma_start(w[:, :, :], wo.rearrange("(g p) n -> p g n", p=P)).then_inc(s_w, 16)
            sp.dma_start(bb[:, :], bo.partition_broadcast(P)).then_inc(s_w, 16)

        @block.tensor
        def _(pe):
            pe.wait_ge(s_w, 32)
            for t in range(NT):
                if t >= 4:
                    pe.wait_ge(s_x, t - 3)
                for g in range(NG):
                    last = nc.tensor.matmul(pp[t % 4][:, :], aT[:, (t // QT) * NG + g, (t % QT) * P:(t % QT + 1) * P],
                                            w[:, g, :], start=(g == 0), stop=(g == NG - 1))
                last.then_inc(s_p, 1)

        @block.vector
        def _(dve):
            dve.wait_ge(s_w, 32)
            for t in range(NT):
                nc.vector.tensor_tensor(x[:, t, :], x[:, t, :], bb[:, :], ALU.add).then_inc(s_b, 1)
            for t in range(NT):
                dve.wait_ge(s_b, t + 1)
                dve.wait_ge(s_p, t + 1)
                nc.vector.tensor_tensor(x[:, t, :], x[:, t, :], pp[t % 4][:, :], ALU.add).then_inc(s_x, 1)


def transpose_rows(nc, name, src, dstT, ident):
    with Stage(nc, name) as st:
        tp = [st.ps(f"tp{i}", [P, S]) for i in range(4)]
        s_tr, s_ev = st.sem("tr"), st.sem("ev")
        block = st.block()

        @block.tensor
        def _(pe):
            for n in range(B * DC):
                g, c = n // DC, n % DC
                if n >= 4:
                    pe.wait_ge(s_ev, n - 3)
                for i in range(QT):
                    last = nc.tensor.transpose(tp[n % 4][:, i * P:(i + 1) * P],
                                               src[:, g * QT + i, c * P:(c + 1) * P], ident[:, :])
                last.then_inc(s_tr, 1)

        @block.scalar
        def _(act):
            for n in range(B * DC):
                g, c = n // DC, n % DC
                act.wait_ge(s_tr, n + 1)
                nc.scalar.activation(dstT[:, c, g * S:(g + 1) * S], tp[n % 4][:, :], ACT.Identity).then_inc(s_ev, 1)


def small_attention(nc, name, srcT, wqkv, att):
    HK = 4
    R = H16 // HK
    SL = B
    NB = NT // SL
    W = (H16 + 2 * HK) * HD
    PAIRS = [(s, t) for s in range(SL) for t in range(s + 1)]
    with Stage(nc, name) as st:
        w = st.sb("w", [P, DC, W])
        qkv = st.sb("qkv", [P, NT, W])
        prod = st.sb("prod", [P, 2, NB, H16 * HD])
        sc = st.sb("sc", [P, len(PAIRS), NB * H16])
        mx = st.sb("mx", [P, SL, NB * H16])
        pp = [st.ps(f"pp{i}", [P, W]) for i in range(4)]
        s_w, s_p, s_ev, s_own, s_sc, s_ex = (st.sem(n) for n in ("w", "p", "ev", "own", "sc", "ex"))
        block = st.block()

        def q(s, b):
            return qkv[:, s * NB + b, 0:H16 * HD].rearrange("p (g r d) -> p g r d", g=HK, r=R)

        def kv(s, b, which):
            lo = (H16 + which * HK) * HD
            v = qkv[:, s * NB + b, lo:lo + HK * HD].rearrange("p (g d) -> p g d", g=HK)
            return v.unsqueeze(2).to_broadcast([P, HK, R, HD])

        @block.sync
        def _(sp):
            sp.dma_start(w[:, :, :], cols(wqkv)).then_inc(s_w, 16)

        @block.tensor
        def _(pe):
            pe.wait_ge(s_w, 16)
            for t in range(NT):
                if t >= 4:
                    pe.wait_ge(s_ev, t - 3)
                for c in range(DC):
                    last = nc.tensor.matmul(pp[t % 4][:, :], srcT[:, c, t * P:(t + 1) * P], w[:, c, :],
                                            start=(c == 0), stop=(c == DC - 1))
                last.then_inc(s_p, 1)

        @block.scalar
        def _(act):
            for t in range(NT):
                act.wait_ge(s_p, t + 1)
                nc.scalar.activation(qkv[:, t, :], pp[t % 4][:, :], ACT.Identity).then_inc(s_ev, 1)
            act.wait_ge(s_sc, 1)
            nc.scalar.activation(sc[:, :, :], sc[:, :, :], ACT.Exp, scale=HD ** -0.5).then_inc(s_ex, 1)

        @block.vector
        def _(dve):
            own = InOrder(dve, s_own)
            dve.wait_ge(s_ev, NT)
            for i, (s, t) in enumerate(PAIRS):
                for b in range(NB):
                    last = nc.vector.tensor_tensor(prod[:, i % 2, b, :].rearrange("p (g r d) -> p g r d", g=HK, r=R),
                                                   q(s, b), kv(t, b, 0), ALU.mult)
                own.after(last)
                last = nc.vector.tensor_reduce(sc[:, i, :], prod[:, i % 2, :, :].rearrange("p b (h d) -> p (b h) d", h=H16),
                                        AX.X, ALU.add)
            own.after(last)
            first = [s * (s + 1) // 2 for s in range(SL + 1)]
            for s in range(SL):
                last = nc.vector.tensor_reduce(mx[:, s, :], sc[:, first[s]:first[s + 1], :].rearrange("p t n -> p n t"),
                                               AX.X, ALU.max)
            own.after(last)
            for s in range(SL):
                v = sc[:, first[s]:first[s + 1], :]
                last = nc.vector.tensor_tensor(v, v, mx[:, s, :].unsqueeze(1).to_broadcast([P, s + 1, NB * H16]),
                                               ALU.subtract)
            last.then_inc(s_sc, 1)
            dve.wait_ge(s_ex, 1)
            for s in range(SL):
                last = nc.vector.tensor_reduce(mx[:, s, :], sc[:, first[s]:first[s + 1], :].rearrange("p t n -> p n t"),
                                               AX.X, ALU.add)
            own.after(last)
            own.after(nc.vector.reciprocal(mx[:, :, :], mx[:, :, :]))
            for s in range(SL):
                v = sc[:, first[s]:first[s + 1], :]
                last = nc.vector.tensor_tensor(v, v, mx[:, s, :].unsqueeze(1).to_broadcast([P, s + 1, NB * H16]),
                                               ALU.mult)
            own.after(last)
            for i, (s, t) in enumerate(PAIRS):
                prob = sc[:, i, :].rearrange("p (b g r) -> p b g r", b=NB, g=HK)
                for b in range(NB):
                    dst = att[:, s * NB + b, :] if t == 0 else prod[:, i % 2, b, :]
                    last = nc.vector.tensor_tensor(dst.rearrange("p (g r d) -> p g r d", g=HK, r=R), kv(t, b, 1),
                                                   prob[:, b].unsqueeze(3).to_broadcast([P, HK, R, HD]), ALU.mult)
                own.after(last)
                if t > 0:
                    a = att[:, s * NB:(s + 1) * NB, :]
                    last = nc.vector.tensor_tensor(a, a, prod[:, i % 2, :, :], ALU.add)
            own.after(last)


def project_rows(nc, name, srcT, w_dram, tiles_out):
    with Stage(nc, name) as st:
        K = w_dram.shape[0] // P
        w = st.sb("w", [P, K, w_dram.shape[1]])
        pp = [st.ps(f"pp{i}", [P, w_dram.shape[1]]) for i in range(4)]
        s_w, s_p, s_ev, s_own = (st.sem(n) for n in ("w", "p", "ev", "own"))
        block = st.block()

        @block.sync
        def _(sp):
            sp.dma_start(w[:, :, :], cols(w_dram)).then_inc(s_w, 16)

        @block.tensor
        def _(pe):
            pe.wait_ge(s_w, 16)
            for t in range(NT):
                if t >= 4:
                    pe.wait_ge(s_ev, t - 3)
                for c in range(K):
                    last = nc.tensor.matmul(pp[t % 4][:, :], srcT[:, c, t * P:(t + 1) * P], w[:, c, :],
                                            start=(c == 0), stop=(c == K - 1))
                last.then_inc(s_p, 1)

        @block.vector
        def _(dve):
            own = InOrder(dve, s_own)
            for t in range(NT):
                dve.wait_ge(s_p, t + 1)
                tiles_out(own, t, pp[t % 4][:, :]).then_inc(s_ev, 1)


def route(nc, name, logits, K, weights, iota, over_all=False, capacity=None, tri=None, ones=None, spare=None,
          slots=None):
    E = logits.shape[2]
    with Stage(nc, name) as st:
        top = st.sb("top", [P, NT, 8])
        idx = st.sb("idx", [P, NT, 8], U32)
        idf = st.sb("idf", [P, NT, K])
        et = st.sb("et", [P, NT, 8])
        ea = st.sb("ea", [P, NT, E])
        den = st.sb("den", [P, NT])
        hot = st.sb("hot", [P, K, NT, E])
        s_own, s_sub, s_exp, s_hot, s_rank = (st.sem(n) for n in ("own", "sub", "exp", "hot", "rank"))
        if capacity:
            rs = st.sb("rs", [P, K, NT])
            keep = st.sb("keep", [P, K, NT])
            sl = st.sb("sl", [P, K, NT])
            sp_ = st.sb("spare", [P, K, NT])
            s_sp = st.sem("sp")
            hotb = st.sb("hotb", [P, K, NT, E], BF16)
            seen = st.sb("seen", [P, K, NT, E], BF16)
            rank = st.ps("rank", [P, K, NT, E])
        block = st.block()

        if capacity:
            @block.sync
            def _(sp):
                sp.dma_start(sp_[:, :, :], spare).then_inc(s_sp, 16)

        @block.vector
        def _(dve):
            own = InOrder(dve, s_own)
            for t in range(NT):
                last = nc.vector.max(top[:, t, :], logits[:, t, :])
            own.after(last)
            for t in range(NT):
                nc.vector.max_index(idx[:, t, :], top[:, t, :], logits[:, t, :])
            best = top[:, :, 0:1]
            if over_all:
                nc.vector.tensor_tensor(ea[:, :, :], logits[:, :, :], best.to_broadcast([P, NT, E]), ALU.subtract)
            nc.vector.tensor_tensor(et[:, :, :], top[:, :, :], best.to_broadcast([P, NT, 8]), ALU.subtract
                                    ).then_inc(s_sub, 1)
            dve.wait_ge(s_sub, 1)
            own.after(nc.vector.tensor_copy(idf[:, :, :], idx[:, :, 0:K]))
            for k in range(K):
                last = nc.vector.tensor_tensor(hot[:, k, :, :], iota[:, 0:E].unsqueeze(1).to_broadcast([P, NT, E]),
                                        idf[:, :, k:k + 1].to_broadcast([P, NT, E]), ALU.is_equal)
            own.after(last)
            if capacity:
                own.after(nc.vector.tensor_copy(hotb[:, :, :, :], hot[:, :, :, :]))
                own.after(nc.vector.memset(seen[:, :, 0, :], 0.0))
                for t in range(1, NT):
                    own.after(nc.vector.tensor_tensor(seen[:, :, t, :], seen[:, :, t - 1, :], hotb[:, :, t - 1, :],
                                                      ALU.add))
                nc.vector.memset(den[:, :], 0.0).then_inc(s_hot, 1)
                dve.wait_ge(s_rank, 1)
                own.after(nc.vector.tensor_tensor(hot[:, :, :, :], rank[:, :, :, :], hot[:, :, :, :], ALU.mult))
                own.after(nc.vector.tensor_reduce(rs[:, :, :], hot[:, :, :, :], AX.X, ALU.add))
                own.after(nc.vector.tensor_scalar(keep[:, :, :], rs[:, :, :], float(capacity), None, ALU.is_lt))
                for k in range(K):
                    last = nc.vector.scalar_tensor_tensor(sl[:, k, :], idf[:, :, k], float(K * capacity), rs[:, k, :],
                                                          ALU.mult, ALU.add)
                own.after(last)
                for k in range(1, K):
                    own.after(nc.vector.tensor_scalar(sl[:, k, :], sl[:, k, :], float(k * capacity), None, ALU.add))
                own.after(nc.vector.tensor_tensor(sl[:, :, :], sl[:, :, :], keep[:, :, :], ALU.mult))
                nc.vector.tensor_copy(slots[1][:, :, :], sl[:, :, :])
                dve.wait_ge(s_sp, 16)
                own.after(nc.vector.tensor_scalar(rs[:, :, :], keep[:, :, :], 0.0, None, ALU.is_equal))
                own.after(nc.vector.tensor_tensor(rs[:, :, :], rs[:, :, :], sp_[:, :, :], ALU.mult))
                own.after(nc.vector.tensor_tensor(sl[:, :, :], sl[:, :, :], rs[:, :, :], ALU.add))
                nc.vector.tensor_copy(slots[0][:, :, :], sl[:, :, :])
            dve.wait_ge(s_exp, 1)
            own.after(nc.vector.tensor_reduce(den[:, :], ea[:, :, :] if over_all else et[:, :, 0:K], AX.X, ALU.add))
            own.after(nc.vector.reciprocal(den[:, :], den[:, :]))
            own.after(nc.vector.tensor_tensor(et[:, :, 0:K], et[:, :, 0:K],
                                              den[:, :].unsqueeze(2).to_broadcast([P, NT, K]), ALU.mult))
            if capacity:
                for k in range(K):
                    nc.vector.tensor_tensor(weights[:, :, k], et[:, :, k], keep[:, k, :], ALU.mult)
                return
            for k in range(K):
                last = nc.vector.tensor_tensor(hot[:, k, :, :], hot[:, k, :, :],
                                               et[:, :, k:k + 1].to_broadcast([P, NT, E]), ALU.mult)
            own.after(last)
            own.after(nc.vector.tensor_tensor(weights, hot[:, 0, :, :], hot[:, 1, :, :], ALU.add))
            for k in range(2, K):
                own.after(nc.vector.tensor_tensor(weights, weights, hot[:, k, :, :], ALU.add))

        @block.scalar
        def _(act):
            act.wait_ge(s_sub, 1)
            if over_all:
                nc.scalar.activation(ea[:, :, :], ea[:, :, :], ACT.Exp)
            nc.scalar.activation(et[:, :, :], et[:, :, :], ACT.Exp).then_inc(s_exp, 1)

        if capacity:
            @block.tensor
            def _(pe):
                pe.wait_ge(s_hot, 1)
                for k in range(K):
                    for t in range(NT):
                        nc.tensor.matmul(rank[:, k, t, :], tri[:, :], hotb[:, k, t, :], start=True, stop=False)
                        last = nc.tensor.matmul(rank[:, k, t, :], ones[:, :], seen[:, k, t, :], start=False, stop=True)
                last.then_inc(s_rank, 1)


def experts(nc, name, xT, w1, w2, weights, x, func, w1u=None, w_of=None):
    E, _, F = w1.shape
    FT = F // P
    NS = E * B
    w_of = w_of or (lambda e: e)
    with Stage(nc, name) as st:
        wa = st.sb("wa", [P, 2, DC, F])
        wu = st.sb("wu", [P, 2, DC, F]) if w1u is not None else None
        wd = st.sb("wd", [P, 2, FT, D])
        hT = st.sb("hT", [P, 2, FT, S])
        NU = 4 if w1u is None else 2
        up = [st.ps(f"up{i}", [P, 4 // NU, S]) for i in range(NU)]
        down = [st.ps(f"down{i}", [P, D]) for i in range(4)]
        sg = st.sb("sg", [P, 2, S]) if w1u is not None else None
        s_w = [st.sem(f"w{i}") for i in range(2)]
        s_up, s_h, s_dn, s_x, s_sg = (st.sem(n) for n in ("up", "h", "dn", "x", "sg"))
        NW = 2 if w1u is None else 3
        block = st.block()

        @block.sync
        def _(sp):
            for e in range(E):
                if e >= 2:
                    sp.wait_ge(s_dn, NT * (e - 1))
                sp.dma_start(wa[:, e % 2, :, :], cols(w1[e])).then_inc(s_w[e % 2], 16)
                if w1u is not None:
                    sp.dma_start(wu[:, e % 2, :, :], cols(w1u[e])).then_inc(s_w[e % 2], 16)
                sp.dma_start(wd[:, e % 2, :, :], cols(w2[e])).then_inc(s_w[e % 2], 16)

        @block.tensor
        def _(pe):
            def go_up(n):
                e, g = n // B, n % B
                if g == 0:
                    pe.wait_ge(s_w[e % 2], 16 * NW * (e // 2 + 1))
                for f in range(FT):
                    k = n * FT + f
                    if k >= NU:
                        pe.wait_ge(s_h, k - NU + 1)
                    for j, w in enumerate([wa] if w1u is None else [wa, wu]):
                        for c in range(DC):
                            last = nc.tensor.matmul(up[k % NU][:, j, :], w[:, e % 2, c, f * P:(f + 1) * P],
                                                    xT[:, c, g * S:(g + 1) * S], start=(c == 0), stop=(c == DC - 1))
                    last.then_inc(s_up, 1)

            def go_down(n):
                e = n // B
                pe.wait_ge(s_h, FT * (n + 1))
                for i in range(QT):
                    m = n * QT + i
                    if m >= 4:
                        pe.wait_ge(s_x, m - 3)
                    for f in range(FT):
                        last = nc.tensor.matmul(down[m % 4][:, :], hT[:, n % 2, f, i * P:(i + 1) * P],
                                                wd[:, e % 2, f, :], start=(f == 0), stop=(f == FT - 1))
                    last.then_inc(s_dn, 1)

            for n in range(NS + 1):
                if n < NS:
                    go_up(n)
                if n >= 1:
                    go_down(n - 1)

        @block.scalar
        def _(act):
            for k in range(NS * FT):
                n, f = k // FT, k % FT
                act.wait_ge(s_up, k + 1)
                if w1u is None:
                    if n >= 2:
                        act.wait_ge(s_dn, QT * (n - 1))
                    nc.scalar.activation(hT[:, n % 2, f, :], up[k % NU][:, 0, :], func).then_inc(s_h, 1)
                else:
                    if k >= 2:
                        act.wait_ge(s_h, k - 1)
                    nc.scalar.activation(sg[:, k % 2, :], up[k % NU][:, 0, :], func).then_inc(s_sg, 1)

        @block.vector
        def _(dve):
            def gate(n):
                for f in range(FT):
                    k = n * FT + f
                    dve.wait_ge(s_sg, k + 1)
                    if n >= 2:
                        dve.wait_ge(s_dn, QT * (n - 1))
                    nc.vector.tensor_tensor(hT[:, n % 2, f, :], sg[:, k % 2, :], up[k % NU][:, 1, :], ALU.mult
                                            ).then_inc(s_h, 1)

            for n in range(NS + 1):
                if w1u is not None and n < NS:
                    gate(n)
                if n == 0:
                    continue
                for i in range(QT):
                    m = (n - 1) * QT + i
                    t, e = m % NT, m // NT
                    dve.wait_ge(s_dn, m + 1)
                    if m >= NT:
                        dve.wait_ge(s_x, m - NT + 1)
                    nc.vector.scalar_tensor_tensor(x[:, t, :], down[m % 4][:, :], weights[:, t, w_of(e):w_of(e) + 1],
                                                   x[:, t, :], ALU.mult, ALU.add).then_inc(s_x, 1)


def dispatch(nc, name, xn, slots, xs):
    K = slots.shape[1]
    with Stage(nc, name) as st:
        s_out = st.sem("out")
        block = st.block()

        @block.gpsimd
        def _(pool):
            for t in range(NT):
                for k in range(K):
                    pool.indirect_dma_start(xs[:, :], bass.IndirectOffsetOnAxis(slots[:, k, t:t + 1], 0),
                                            xn[:, t, :], None).then_inc(s_out, 16)
            pool.wait_ge(s_out, 16 * NT * K)


def combine(nc, name, ys, slots, wk, x, vec):
    K = slots.shape[1]
    R = 4
    with Stage(nc, name) as st:
        vb = st.sb("vb", [P, D])
        y = st.sb("y", [P, R, K, D])
        s_vb, s_b, s_x = (st.sem(n) for n in ("vb", "b", "x"))
        s_y = [st.sem(f"y{i}") for i in range(R)]
        block = st.block()

        @block.sync
        def _(sp):
            sp.dma_start(vb[:, :], vec.partition_broadcast(P)).then_inc(s_vb, 16)

        @block.gpsimd
        def _(pool):
            for t in range(NT):
                if t >= R:
                    pool.wait_ge(s_x, K * (t - R + 1))
                for k in range(K):
                    pool.indirect_dma_start(y[:, t % R, k, :], None, ys[:, :],
                                            bass.IndirectOffsetOnAxis(slots[:, k, t:t + 1], 0)).then_inc(s_y[t % R], 16)

        @block.vector
        def _(dve):
            dve.wait_ge(s_vb, 16)
            for t in range(NT):
                nc.vector.tensor_tensor(x[:, t, :], x[:, t, :], vb[:, :], ALU.add).then_inc(s_b, 1)
            for t in range(NT):
                dve.wait_ge(s_y[t % R], 16 * K * (t // R + 1))
                dve.wait_ge(s_b, t + 1)
                for k in range(K):
                    if k:
                        dve.wait_ge(s_x, K * t + k)
                    nc.vector.scalar_tensor_tensor(x[:, t, :], y[:, t % R, k, :], wk[:, t, k:k + 1], x[:, t, :],
                                                   ALU.mult, ALU.add).then_inc(s_x, 1)


def slot_experts(nc, name, xs, ys, w1, w2, func, ident):
    E, _, F = w1.shape
    FT = F // P
    with Stage(nc, name) as st:
        wa = st.sb("wa", [P, 2, DC, F])
        wd = st.sb("wd", [P, 2, FT, D])
        xr = st.sb("xr", [P, 2, QT, D])
        xT = st.sb("xT", [P, 2, DC, S])
        hT = st.sb("hT", [P, 2, FT, S])
        y = st.sb("y", [P, 2, QT, D])
        NU = 3
        up = [st.ps(f"up{i}", [P, S]) for i in range(NU)]
        tp = st.ps("tp", [P, S])
        down = [st.ps(f"down{i}", [P, D]) for i in range(4)]
        s_w = [st.sem(f"w{i}") for i in range(2)]
        s_xr = [st.sem(f"xr{i}") for i in range(2)]
        s_st = [st.sem(f"st{i}") for i in range(2)]
        s_tr, s_xt, s_up, s_h, s_dn, s_y = (st.sem(n) for n in ("tr", "xt", "up", "h", "dn", "y"))
        block = st.block()

        @block.sync
        def _(sp):
            for e in range(E):
                if e >= 2:
                    sp.wait_ge(s_tr, DC * (e - 1))
                sp.dma_start(xr[:, e % 2, :, :], rows(xs[e * S:(e + 1) * S, :])).then_inc(s_xr[e % 2], 16)
                if e >= 2:
                    sp.wait_ge(s_dn, QT * (e - 1))
                sp.dma_start(wa[:, e % 2, :, :], cols(w1[e])).then_inc(s_w[e % 2], 16)
                sp.dma_start(wd[:, e % 2, :, :], cols(w2[e])).then_inc(s_w[e % 2], 16)

        @block.gpsimd
        def _(pool):
            for e in range(E):
                pool.wait_ge(s_y, QT * (e + 1))
                pool.dma_start(rows(ys[e * S:(e + 1) * S, :]), y[:, e % 2, :, :]).then_inc(s_st[e % 2], 16)
            for i in range(2):
                pool.wait_ge(s_st[i], 16 * (E // 2))

        @block.tensor
        def _(pe):
            def turn(e):
                pe.wait_ge(s_xr[e % 2], 16 * (e // 2 + 1))
                for c in range(DC):
                    k = e * DC + c
                    if k >= 1:
                        pe.wait_ge(s_xt, k)
                    for i in range(QT):
                        last = nc.tensor.transpose(tp[:, i * P:(i + 1) * P], xr[:, e % 2, i, c * P:(c + 1) * P],
                                                   ident[:, :])
                    last.then_inc(s_tr, 1)

            def go_up(e):
                pe.wait_ge(s_w[e % 2], 32 * (e // 2 + 1))
                pe.wait_ge(s_xt, DC * (e + 1))
                for f in range(FT):
                    k = e * FT + f
                    if k >= NU:
                        pe.wait_ge(s_h, k - NU + 1)
                    for c in range(DC):
                        last = nc.tensor.matmul(up[k % NU][:, :], wa[:, e % 2, c, f * P:(f + 1) * P],
                                                xT[:, e % 2, c, :], start=(c == 0), stop=(c == DC - 1))
                    last.then_inc(s_up, 1)

            def go_down(e):
                pe.wait_ge(s_h, FT * (e + 1))
                for i in range(QT):
                    m = e * QT + i
                    if m >= 4:
                        pe.wait_ge(s_y, m - 3)
                    for f in range(FT):
                        last = nc.tensor.matmul(down[m % 4][:, :], hT[:, e % 2, f, i * P:(i + 1) * P],
                                                wd[:, e % 2, f, :], start=(f == 0), stop=(f == FT - 1))
                    last.then_inc(s_dn, 1)

            turn(0)
            for e in range(E):
                go_up(e)
                if e + 1 < E:
                    turn(e + 1)
                if e >= 1:
                    go_down(e - 1)
            go_down(E - 1)

        @block.scalar
        def _(act):
            for k in range(E * FT):
                e, f = k // FT, k % FT
                act.wait_ge(s_up, k + 1)
                if e >= 2:
                    act.wait_ge(s_dn, QT * (e - 1))
                nc.scalar.activation(hT[:, e % 2, f, :], up[k % NU][:, :], func).then_inc(s_h, 1)

        @block.vector
        def _(dve):
            def turned(e):
                for c in range(DC):
                    dve.wait_ge(s_tr, e * DC + c + 1)
                    if e >= 2:
                        dve.wait_ge(s_up, FT * (e - 1))
                    nc.vector.tensor_copy(xT[:, e % 2, c, :], tp[:, :]).then_inc(s_xt, 1)

            def done(e):
                for i in range(QT):
                    m = e * QT + i
                    dve.wait_ge(s_dn, m + 1)
                    if e >= 2:
                        dve.wait_ge(s_st[e % 2], 16 * (e // 2))
                    nc.vector.tensor_copy(y[:, e % 2, i, :], down[m % 4][:, :]).then_inc(s_y, 1)

            turned(0)
            for e in range(E):
                if e + 1 < E:
                    turned(e + 1)
                if e >= 1:
                    done(e - 1)
            done(E - 1)


def add_rows(nc, name, vec, x):
    with Stage(nc, name) as st:
        vb = st.sb("vb", [P, D])
        s_ld = st.sem("ld")
        block = st.block()

        @block.sync
        def _(sp):
            sp.dma_start(vb[:, :], vec.partition_broadcast(P)).then_inc(s_ld, 16)

        @block.vector
        def _(dve):
            dve.wait_ge(s_ld, 16)
            for t in range(NT):
                nc.vector.tensor_tensor(x[:, t, :], x[:, t, :], vb[:, :], ALU.add)


HB = 64
NP = H16 * HB // P


def tri_at(k):
    return slice(k * (k + 1) // 2 * P, (k + 1) * (k + 2) // 2 * P)


def causal_masks(nc, name, a, am, uT, sufmax, usum, ident):
    with Stage(nc, name) as st:
        later = st.sb("later", [P, QT, S])
        zero = st.sb("zero", [P, 8 * D])
        s_z, s_zs = st.sem("z"), st.sem("zs")
        fill = st.sb("fill", [P, QT, S])
        mb = st.sb("mb", [P, B, S])
        sc = st.sb("sc", [P, 2, S])
        u = st.sb("u", [P, QT, S])
        ns = st.sb("ns", [P, NT])
        tp = [st.ps(f"tp{i}", [P, S]) for i in range(2)]
        s_ld, s_sc, s_mx, s_ns, s_u, s_tr, s_ev, s_am = (
            st.sem(n) for n in ("ld", "sc", "mx", "ns", "u", "tr", "ev", "am"))
        block = st.block()

        @block.sync
        def _(sp):
            sp.dma_start(later[:, :, :], a["c_later"]).then_inc(s_ld, 16)
            sp.dma_start(fill[:, :, :], a["c_fill"]).then_inc(s_ld, 16)
            sp.dma_start(mb[:, :, :].rearrange("p b n -> p (b n)"), a["addm"].partition_broadcast(P)
                         ).then_inc(s_ld, 16)
            sp.wait_ge(s_ld, 48)
            sp.wait_ge(s_z, 1)
            for i in range(4):
                sp.dma_start(a["slot_rows"][i * 8 * P:(i + 1) * 8 * P, :].rearrange("(p r) n -> p (r n)", p=P),
                             zero[:, :]).then_inc(s_zs, 16)
            sp.wait_ge(s_zs, 64)

        @block.vector
        def _(dve):
            nc.vector.memset(zero[:, :], 0.0).then_inc(s_z, 1)
            dve.wait_ge(s_ld, 48)
            for m in range(NT):
                b, t = m // QT, m % QT
                nc.vector.tensor_tensor(am[:, b, tri_at(t)], mb[:, b, 0:(t + 1) * P], later[:, t, 0:(t + 1) * P], ALU.add
                                        ).then_inc(s_am, 1)
                if m >= 2:
                    dve.wait_ge(s_u, m - 1)
                nc.vector.tensor_tensor(sc[:, m % 2, :], mb[:, b, :], fill[:, t, :], ALU.add).then_inc(s_sc, 1)
                dve.wait_ge(s_sc, m + 1)
                nc.vector.tensor_reduce(sufmax[:, m:m + 1], sc[:, m % 2, :], AX.X, ALU.max).then_inc(s_mx, 1)
                dve.wait_ge(s_mx, m + 1)
                nc.vector.tensor_scalar(ns[:, m:m + 1], sufmax[:, m:m + 1], -1.0, None, ALU.mult).then_inc(s_ns, 1)

        @block.scalar
        def _(act):
            j = 0
            for m in range(NT):
                b, t = m // QT, m % QT
                act.wait_ge(s_ns, m + 1)
                if b >= 1:
                    act.wait_ge(s_tr, QT * b)
                nc.scalar.activation(u[:, t, :], sc[:, m % 2, :], ACT.Exp, bias=ns[:, m:m + 1],
                                     accum_out=usum[:, m:m + 1]).then_inc(s_u, 1)
                if t == QT - 1:
                    for k in range(QT):
                        act.wait_ge(s_tr, j + 1)
                        nc.scalar.activation(uT[:, b, tri_at(k)], tp[j % 2][:, 0:(k + 1) * P], ACT.Identity
                                             ).then_inc(s_ev, 1)
                        j += 1

        @block.tensor
        def _(pe):
            for j in range(B * QT):
                b, k = j // QT, j % QT
                pe.wait_ge(s_u, QT * (b + 1))
                if j >= 2:
                    pe.wait_ge(s_ev, j - 1)
                for t in range(k + 1):
                    last = nc.tensor.transpose(tp[j % 2][:, t * P:(t + 1) * P], u[:, t, k * P:(k + 1) * P], ident[:, :])
                last.then_inc(s_tr, 1)


def attend64(nc, name, a, xT, cT, masks, x, ident):
    am, uT, sufmax, usum = masks
    N = B * NP
    scale = HB ** -0.5
    TRI = QT * (QT + 1) // 2 * P
    with Stage(nc, name) as st:
        w = [st.sb("w" + k, [P, DC, H16 * HB]) for k in "qkv"]
        wo = st.sb("wo", [P, NP, D])
        bqk = st.sb("bqk", [P, 2, NP])
        bv = st.sb("bv", [P, H16 * HB])
        bo = st.sb("bo", [P, D])
        qT = st.sb("qT", [P, 2, S])
        kT = st.sb("kT", [P, 2, S])
        v = st.sb("v", [P, 2, QT, P])
        wmT = st.sb("wmT", [P, 2, S])
        prob = st.sb("prob", [P, 2, 2, TRI])
        probT = st.sb("probT", [P, 2, QT, S])
        rowmax = st.sb("rowmax", [P, 2, 2, QT])
        neg = st.sb("neg", [P, 2, 2, QT])
        en = st.sb("en", [P, 2, 2, QT])
        em = st.sb("em", [P, 2, 2, QT])
        tot = st.sb("tot", [P, 2, 2, QT])
        den = st.sb("den", [P, QT])
        rec = st.sb("rec", [P, QT])
        share = st.sb("share", [P, 2, QT])
        expand = st.sb("expand", [P, QT, 2, HB])
        t2 = st.sb("t2", [P, S])
        oT = st.sb("oT", [P, NP, S])
        pj = [st.ps(f"pj{i}", [P, S]) for i in range(2)]
        sq = [st.ps(f"sq{i}", [P, S]) for i in range(2)]
        tp = [st.ps(f"tp{i}", [P, S]) for i in range(2)]
        acc = st.ps("acc", [P, S])
        misc = st.ps("misc", [P, S])
        names = "w pj qkv wm sq max neg exp em p tr ta td pv ex fb t2 out op x own".split()
        (s_w, s_pj, s_qkv, s_wm, s_sq, s_max, s_neg, s_exp, s_em, s_p, s_tr, s_ta, s_td, s_pv, s_ex, s_fb, s_t2,
         s_out, s_op, s_x, s_own) = (st.sem(n) for n in names)
        block = st.block()

        @block.sync
        def _(sp):
            for i, k in enumerate(("WQ", "WK", "WV")):
                sp.dma_start(w[i][:, :, :], cols(a["L1_" + k])).then_inc(s_w, 16)
            sp.dma_start(wo[:, :, :], cols(a["L1_WO"])).then_inc(s_w, 16)
            for i, k in enumerate(("bQ", "bK")):
                sp.dma_start(bqk[:, i, :], a["L1_" + k]).then_inc(s_w, 16)
            sp.dma_start(bv[:, :], a["L1_bV"].partition_broadcast(P)).then_inc(s_w, 16)
            sp.dma_start(bo[:, :], a["L1_bO"].partition_broadcast(P)).then_inc(s_w, 16)
            sp.wait_ge(s_w, 16 * 8)

        @block.tensor
        def _(pe):
            def project(n, which):
                b, p = n // NP, n % NP
                bank = pj[which % 2]
                if which == 0 and n >= 1:
                    pe.wait_ge(s_qkv, 3 * n)
                    if p == 2 and b >= 1:
                        pe.wait_ge(s_x, QT * b)
                if which == 1 and n >= 1:
                    pe.wait_ge(s_wm, n)
                if which == 2:
                    pe.wait_ge(s_qkv, 3 * n + 1)
                if which == 3:
                    pe.wait_ge(s_qkv, 3 * n + 3)
                if which < 2:
                    src = (xT, cT)[which]
                    for c in range(DC):
                        last = nc.tensor.matmul(bank[:, :], w[which][:, c, p * P:(p + 1) * P], src[:, c, b * S:(b + 1) * S],
                                                start=(c == 0), stop=(c == DC - 1))
                elif which == 2:
                    for t in range(QT):
                        for c in range(DC):
                            last = nc.tensor.matmul(bank[:, t * P:(t + 1) * P], cT[:, c, b * S + t * P:b * S + (t + 1) * P],
                                                    w[2][:, c, p * P:(p + 1) * P], start=(c == 0), stop=(c == DC - 1))
                else:
                    for t in reversed(range(QT)):
                        last = nc.tensor.matmul(bank[:, 0:(t + 1) * P], v[:, n % 2, t, :], uT[:, b, tri_at(t)],
                                                start=(t == QT - 1), stop=(t == 0), skip_group_check=True)
                last.then_inc(s_pj, 1)

            def row_scores(n, i):
                h, t = i // QT, i % QT
                k = n * 8 + i
                if k >= 2:
                    pe.wait_ge(s_max, k - 1)
                if i == 0:
                    pe.wait_ge(s_qkv, 3 * n + 2)
                r = slice(h * HB, (h + 1) * HB)
                nc.tensor.matmul(sq[k % 2][:, 0:(t + 1) * P], qT[r, n % 2, t * P:(t + 1) * P],
                                 kT[r, n % 2, 0:(t + 1) * P], start=True, stop=True).then_inc(s_sq, 1)

            def turn(n, i):
                h, t = i // QT, i % QT
                j = n * 8 + i
                pe.wait_ge(s_p, 2 * n + h + 1)
                if j >= 2:
                    jn, jh, jt = (j - 2) // 8, (j - 2) % 8 // QT, (j - 2) % QT
                    pe.wait_ge((s_ta, s_td)[jh], QT * jn + jt + 1)
                for r in range(t, QT):
                    at = tri_at(r).start + t * P
                    last = nc.tensor.transpose(tp[j % 2][:, r * P:(r + 1) * P], prob[:, n % 2, h, at:at + P], ident[:, :])
                last.then_inc(s_tr, 1)

            def values(n):
                pe.wait_ge(s_ta, QT * (n + 1))
                pe.wait_ge(s_td, QT * (n + 1))
                if n >= 1:
                    pe.wait_ge(s_out, n)
                for t in reversed(range(QT)):
                    for h in range(2):
                        last = nc.tensor.matmul(acc[h * HB:(h + 1) * HB, t * P:S], v[:, n % 2, t, h * HB:(h + 1) * HB],
                                                probT[:, h, t, t * P:S], start=(t == QT - 1), stop=(t == 0),
                                                tile_position=(0, h * HB), skip_group_check=True)
                last.then_inc(s_pv, 1)

            def shares(n):
                pe.wait_ge(s_ex, n + 1)
                if n >= 1:
                    pe.wait_ge(s_t2, n)
                for t in range(QT):
                    last = nc.tensor.transpose(misc[:, t * P:(t + 1) * P],
                                               expand[:, t, :, :].rearrange("p h d -> p (h d)"), ident[:, :])
                last.then_inc(s_fb, 1)

            def output(b):
                pe.wait_ge(s_out, NP * (b + 1))
                pe.wait_ge(s_qkv, 3 * min(NP * (b + 1) + 2, N))
                pe.wait_ge(s_wm, min(NP * (b + 1) + 2, N))
                for i in range(QT):
                    if i >= 2:
                        pe.wait_ge(s_x, QT * b + i - 1)
                    for p in range(NP):
                        last = nc.tensor.matmul(pj[i % 2][:, 0:D], oT[:, p, i * P:(i + 1) * P],
                                                wo[:, p, :], start=(p == 0), stop=(p == NP - 1))
                    last.then_inc(s_op, 1)

            pe.wait_ge(s_w, 16 * 8)
            for n in range(-1, N):
                now, nxt = n >= 0, n + 1 < N
                if nxt:
                    project(n + 1, 0)
                if now:
                    turn(n, 0)
                    turn(n, 1)
                if nxt:
                    project(n + 1, 1)
                if now:
                    turn(n, 2)
                    turn(n, 3)
                if nxt:
                    project(n + 1, 2)
                for i in range(QT):
                    if nxt:
                        row_scores(n + 1, i)
                    if now:
                        turn(n, QT + i)
                if now:
                    shares(n)
                if nxt:
                    project(n + 1, 3)
                    for i in range(QT, 2 * QT):
                        row_scores(n + 1, i)
                if now:
                    values(n)
                    if n % NP == 0 and n >= NP:
                        output(n // NP - 1)
            output(B - 1)

        @block.vector
        def _(dve):
            own = InOrder(dve, s_own)
            dve.wait_ge(s_w, 16 * 8)
            for t in range(NT):
                last = nc.vector.tensor_tensor(x[:, t, :], x[:, t, :], bo[:, :], ALU.add)
            own.after(last)

            def evacuate(n, i):
                p = n % NP
                dve.wait_ge(s_pj, 4 * n + i + 1)
                if i < 2:
                    if n >= 2:
                        dve.wait_ge(s_sq, 8 * (n - 1))
                    nc.vector.tensor_scalar((qT, kT)[i][:, n % 2, :], pj[i][:, :], bqk[:, i, p:p + 1],
                                            scale if i == 0 else 1.0, ALU.add, ALU.mult).then_inc(s_qkv, 1)
                else:
                    if n >= 2:
                        dve.wait_ge(s_pv, n - 1)
                    nc.vector.tensor_tensor(v[:, n % 2, :, :], pj[0][:, :].rearrange("p (t n) -> p t n", t=QT),
                                            bv[:, p * P:(p + 1) * P].unsqueeze(1).to_broadcast([P, QT, P]), ALU.add
                                            ).then_inc(s_qkv, 1)

            def row_max(n, i):
                h, t = i // QT, i % QT
                k = n * 8 + i
                dve.wait_ge(s_sq, k + 1)
                if n >= 2 and i == 0:
                    dve.wait_ge(s_tr, 8 * (n - 1))
                nc.vector.tensor_tensor_reduce(prob[:, n % 2, h, tri_at(t)], sq[k % 2][:, 0:(t + 1) * P],
                                               am[:, n // NP, tri_at(t)], 1.0, 3.0 * BIG,
                                               ALU.add, ALU.max, rowmax[:, n % 2, h, t:t + 1]).then_inc(s_max, 1)

            def minus_max(n, h):
                suf = sufmax[:, (n // NP) * QT:(n // NP + 1) * QT]
                m, g = rowmax[:, n % 2, h, :], neg[:, n % 2, h, :]
                dve.wait_ge(s_max, 8 * n + QT * (h + 1))
                own.after(nc.vector.tensor_tensor(m, m, suf, ALU.max))
                own.after(nc.vector.tensor_scalar(g, m, -1.0, None, ALU.mult))
                nc.vector.tensor_tensor(en[:, n % 2, h, :], g, suf, ALU.add).then_inc(s_neg, 1)

            def normalize(n, h):
                e = em[:, n % 2, h, :]
                dve.wait_ge(s_em, 2 * n + h + 1)
                own.after(nc.vector.tensor_tensor(den[:, :], e, usum[:, (n // NP) * QT:(n // NP + 1) * QT], ALU.mult))
                own.after(nc.vector.tensor_tensor(den[:, :], den[:, :], tot[:, n % 2, h, :], ALU.add))
                own.after(nc.vector.reciprocal(rec[:, :], den[:, :]))
                if n >= 1:
                    dve.wait_ge(s_ex, n)
                own.after(nc.vector.tensor_tensor(share[:, h, :], e, rec[:, :], ALU.mult))
                for t in range(QT):
                    u = prob[:, n % 2, h, tri_at(t)]
                    last = nc.vector.tensor_scalar(u, u, rec[:, t:t + 1], None, ALU.mult)
                last.then_inc(s_p, 1)
                dve.wait_ge(s_p, 2 * n + h + 1)
                if h == 1:
                    if n >= 1:
                        dve.wait_ge(s_fb, n)
                    nc.vector.tensor_copy(expand[:, :, :, :], share[:, :, :].rearrange("p h t -> p t h").unsqueeze(3)
                                          .to_broadcast([P, QT, 2, HB])).then_inc(s_ex, 1)

            def turned(n, t):
                dve.wait_ge(s_tr, n * 8 + QT + t + 1)
                if n >= 1:
                    dve.wait_ge(s_pv, n)
                nc.vector.tensor_copy(probT[:, 1, t, t * P:S], tp[(QT + t) % 2][:, t * P:S]).then_inc(s_td, 1)

            def finish(n):
                b, p = n // NP, n % NP
                dve.wait_ge(s_fb, n + 1)
                dve.wait_ge(s_wm, n + 1)
                nc.vector.tensor_tensor(t2[:, :], wmT[:, n % 2, :], misc[:, :], ALU.mult).then_inc(s_t2, 1)
                dve.wait_ge(s_t2, n + 1)
                dve.wait_ge(s_pv, n + 1)
                if b >= 1:
                    dve.wait_ge(s_op, QT * b)
                nc.vector.tensor_tensor(oT[:, p, :], acc[:, :], t2[:, :], ALU.add).then_inc(s_out, 1)

            def outputs(b):
                for i in range(QT):
                    m = b * QT + i
                    dve.wait_ge(s_op, m + 1)
                    nc.vector.tensor_tensor(x[:, m, :], x[:, m, :], pj[i % 2][:, 0:D], ALU.add
                                            ).then_inc(s_x, 1)

            for n in range(-1, N):
                now, nxt = n >= 0, n + 1 < N
                if nxt:
                    for i in range(3):
                        evacuate(n + 1, i)
                for i in range(QT):
                    if nxt:
                        row_max(n + 1, i)
                    if now:
                        turned(n, i)
                if nxt:
                    minus_max(n + 1, 0)
                    for i in range(QT, 2 * QT):
                        row_max(n + 1, i)
                    minus_max(n + 1, 1)
                    normalize(n + 1, 0)
                    normalize(n + 1, 1)
                if now:
                    if n % NP == 0 and n >= NP:
                        outputs(n // NP - 1)
                    finish(n)
            outputs(B - 1)

        @block.scalar
        def _(act):
            def exps(n, h):
                act.wait_ge(s_neg, 2 * n + h + 1)
                for t in range(QT):
                    u = prob[:, n % 2, h, tri_at(t)]
                    nc.scalar.activation(u, u, ACT.Exp, bias=neg[:, n % 2, h, t:t + 1],
                                         accum_out=tot[:, n % 2, h, t:t + 1])
                nc.scalar.activation(em[:, n % 2, h, :], en[:, n % 2, h, :], ACT.Exp).then_inc(s_em, 1)

            for n in range(-1, N):
                now, nxt = n >= 0, n + 1 < N
                if now:
                    for t in range(QT):
                        act.wait_ge(s_tr, n * 8 + t + 1)
                        if n >= 1:
                            act.wait_ge(s_pv, n)
                        nc.scalar.activation(probT[:, 0, t, t * P:S], tp[t % 2][:, t * P:S], ACT.Identity).then_inc(s_ta, 1)
                if nxt:
                    exps(n + 1, 0)
                    act.wait_ge(s_pj, 4 * (n + 2))
                    if n >= 1:
                        act.wait_ge(s_t2, n)
                    nc.scalar.activation(wmT[:, (n + 1) % 2, :], pj[1][:, :], ACT.Identity).then_inc(s_wm, 1)
                    exps(n + 1, 1)


def similarity(nc, name, a, xnT, cT, crow, hqT, mcol, ident):
    with Stage(nc, name) as st:
        w3 = st.sb("w3", [P, 3, DC])
        bsim = st.sb("bsim", [P, 1])
        e3T = st.sb("e3T", [P, DC, T])
        A = st.sb("A", [P, 2, QT, S])
        AT = st.sb("AT", [P, QT, S])
        neg = st.sb("neg", [P, NT])
        tot = st.sb("tot", [P, NT])
        sc = [st.ps(f"sc{i}", [P, S]) for i in range(2)]
        tp = [st.ps(f"tp{i}", [P, S]) for i in range(2)]
        hq = [st.ps(f"hq{i}", [P, S]) for i in range(2)]
        e1 = st.ps("e1", [P, NT])
        s_w, s_e3, s_sc, s_neg, s_exp, s_A, s_tr, s_at, s_hq, s_ev, s_e1, s_own, s_tot = (
            st.sem(n) for n in ("w", "e3", "sc", "neg", "exp", "A", "tr", "at", "hq", "ev", "e1", "own", "tot"))
        block = st.block()

        @block.sync
        def _(sp):
            sp.dma_start(w3[:, :, :], a["L2_wsim"]).then_inc(s_w, 16)
            sp.dma_start(bsim[:, :], a["L2_bsim"].partition_broadcast(P)).then_inc(s_w, 16)
            sp.wait_ge(s_w, 32)

        @block.tensor
        def _(pe):
            pe.wait_ge(s_w, 32)
            for t in range(NT):
                for c in range(DC):
                    last = nc.tensor.matmul(e1[:, t:t + 1], xnT[:, c, t * P:(t + 1) * P], w3[:, 0, c:c + 1],
                                            start=(c == 0), stop=(c == DC - 1))
            last.then_inc(s_e1, 1)

            def scores(b):
                for t in range(QT):
                    m = b * QT + t
                    pe.wait_ge(s_e3, DC * (b + 1))
                    if m >= 2:
                        pe.wait_ge(s_exp, m - 1)
                    for c in range(DC):
                        last = nc.tensor.matmul(sc[m % 2][:, :], e3T[:, c, m * P:(m + 1) * P], cT[:, c, b * S:(b + 1) * S],
                                                start=(c == 0), stop=(c == DC - 1))
                    last.then_inc(s_sc, 1)

            scores(0)
            for b in range(B):
                if b + 1 < B:
                    scores(b + 1)
                pe.wait_ge(s_A, QT * (b + 1))
                for j in range(QT):
                    k = b * QT + j
                    if k >= 2:
                        pe.wait_ge(s_at, k - 1)
                    for t in range(QT):
                        last = nc.tensor.transpose(tp[k % 2][:, t * P:(t + 1) * P], A[:, b % 2, t, j * P:(j + 1) * P],
                                                   ident[:, :])
                    last.then_inc(s_tr, 1)
                pe.wait_ge(s_at, QT * (b + 1))
                for c in range(DC):
                    if b >= 1:
                        pe.wait_ge(s_ev, DC * (b - 1) + c + 1)
                    for j in range(QT):
                        last = nc.tensor.matmul(hq[c][:, :], crow[:, b * QT + j, c * P:(c + 1) * P], AT[:, j, :],
                                                start=(j == 0), stop=(j == QT - 1))
                    last.then_inc(s_hq, 1)

        @block.vector
        def _(dve):
            own = InOrder(dve, s_own)
            dve.wait_ge(s_w, 32)
            for b in range(B):
                for c in range(DC):
                    nc.vector.tensor_scalar(e3T[:, c, b * S:(b + 1) * S], xnT[:, c, b * S:(b + 1) * S],
                                            w3[:, 2, c:c + 1], w3[:, 1, c:c + 1], ALU.mult, ALU.add).then_inc(s_e3, 1)
            for m in range(NT):
                b, t = m // QT, m % QT
                dve.wait_ge(s_sc, m + 1)
                own.after(nc.vector.tensor_reduce(mcol[:, m:m + 1], sc[m % 2][:, :], AX.X, ALU.max))
                nc.vector.tensor_scalar(neg[:, m:m + 1], mcol[:, m:m + 1], -1.0, None, ALU.mult).then_inc(s_neg, 1)
                dve.wait_ge(s_exp, m + 1)
                own.after(nc.vector.reciprocal(tot[:, m:m + 1], tot[:, m:m + 1]))
                nc.vector.tensor_scalar(A[:, b % 2, t, :], A[:, b % 2, t, :], tot[:, m:m + 1], None, ALU.mult
                                        ).then_inc(s_A, 1)
            dve.wait_ge(s_e1, 1)
            own.after(nc.vector.tensor_tensor(mcol[:, :], mcol[:, :], e1[:, :], ALU.add))
            own.after(nc.vector.tensor_scalar(mcol[:, :], mcol[:, :], bsim[:, 0:1], None, ALU.add))

        @block.scalar
        def _(act):
            def exps(b):
                for t in range(QT):
                    m = b * QT + t
                    act.wait_ge(s_neg, m + 1)
                    if b >= 2:
                        act.wait_ge(s_tr, QT * (b - 1))
                    nc.scalar.activation(A[:, b % 2, t, :], sc[m % 2][:, :], ACT.Exp, bias=neg[:, m:m + 1],
                                         accum_out=tot[:, m:m + 1]).then_inc(s_exp, 1)

            exps(0)
            for b in range(B):
                if b + 1 < B:
                    exps(b + 1)
                for j in range(QT):
                    k = b * QT + j
                    act.wait_ge(s_tr, k + 1)
                    if b >= 1:
                        act.wait_ge(s_hq, DC * b)
                    nc.scalar.activation(AT[:, j, :], tp[k % 2][:, :], ACT.Identity).then_inc(s_at, 1)
                for c in range(DC):
                    act.wait_ge(s_hq, DC * b + c + 1)
                    nc.scalar.activation(hqT[:, c, b * S:(b + 1) * S], hq[c][:, :], ACT.Identity).then_inc(s_ev, 1)


def attended_row(nc, name, xnT, hqT, mcol, xhT, xcT, ident, ones):
    with Stage(nc, name) as st:
        row = st.sb("row", [1, B, S])
        mx = st.sb("mx", [1, B])
        junk = st.sb("junk", [P, 2, S])
        hc = st.sb("hc", [P, B, DC])
        r = st.ps("r", [1, B, S])
        rb = [st.ps(f"rb{i}", [P, S]) for i in range(2)]
        s_r, s_sub, s_exp, s_row, s_rb, s_hc, s_own, s_xh = (
            st.sem(n) for n in ("r", "sub", "exp", "row", "rb", "hc", "own", "xh"))
        block = st.block()

        @block.tensor
        def _(pe):
            for t in range(NT):
                last = nc.tensor.matmul(r[:, t // QT, (t % QT) * P:(t % QT + 1) * P], mcol[:, t:t + 1], ident[:, :],
                                        start=True, stop=True)
            last.then_inc(s_r, 1)
            pe.wait_ge(s_row, 1)
            for b in range(B):
                if b >= 2:
                    pe.wait_ge(s_hc, DC * (b - 1))
                nc.tensor.matmul(rb[b % 2][:, :], ones[0:1, :], row[:, b, :], start=True, stop=True).then_inc(s_rb, 1)

        @block.scalar
        def _(act):
            act.wait_ge(s_sub, 1)
            nc.scalar.activation(row[:, :, :], row[:, :, :], ACT.Exp).then_inc(s_exp, 1)

        @block.vector
        def _(dve):
            own = InOrder(dve, s_own)
            dve.wait_ge(s_r, 1)
            own.after(nc.vector.tensor_reduce(mx[:, :], r[:, :, :], AX.X, ALU.max))
            nc.vector.tensor_tensor(row[:, :, :], r[:, :, :], mx[:, :].unsqueeze(2).to_broadcast([1, B, S]),
                                    ALU.subtract).then_inc(s_sub, 1)
            for c in range(DC):
                nc.vector.tensor_tensor(xhT[:, c, :], xnT[:, c, :], hqT[:, c, :], ALU.mult)
            dve.wait_ge(s_exp, 1)
            own.after(nc.vector.tensor_reduce(mx[:, :], row[:, :, :], AX.X, ALU.add))
            own.after(nc.vector.reciprocal(mx[:, :], mx[:, :]))
            nc.vector.tensor_tensor(row[:, :, :], row[:, :, :], mx[:, :].unsqueeze(2).to_broadcast([1, B, S]), ALU.mult
                                    ).then_inc(s_row, 1)
            for b in range(B):
                dve.wait_ge(s_rb, b + 1)
                for c in range(DC):
                    k = b * DC + c
                    if k >= 2:
                        dve.wait_ge(s_hc, k - 1)
                    nc.vector.tensor_tensor_reduce(junk[:, k % 2, :], xnT[:, c, b * S:(b + 1) * S], rb[b % 2][:, :],
                                                   1.0, 0.0, ALU.mult, ALU.add, hc[:, b, c:c + 1]).then_inc(s_hc, 1)
            dve.wait_ge(s_hc, B * DC)
            for b in range(B):
                for c in range(DC):
                    nc.vector.tensor_scalar(xcT[:, c, b * S:(b + 1) * S], xnT[:, c, b * S:(b + 1) * S],
                                            hc[:, b, c:c + 1], None, ALU.mult)


def project_parts(nc, name, parts, w_dram, b_dram, x):
    with Stage(nc, name) as st:
        K = len(parts) * DC
        w = st.sb("w", [P, K, D])
        bb = st.sb("bb", [P, D])
        pp = [st.ps(f"pp{i}", [P, D]) for i in range(4)]
        s_w, s_p, s_ev, s_b = (st.sem(n) for n in ("w", "p", "ev", "b"))
        block = st.block()

        @block.sync
        def _(sp):
            sp.dma_start(w[:, :, :], cols(w_dram)).then_inc(s_w, 16)
            sp.dma_start(bb[:, :], b_dram.partition_broadcast(P)).then_inc(s_w, 16)

        @block.tensor
        def _(pe):
            pe.wait_ge(s_w, 32)
            for t in range(NT):
                if t >= 4:
                    pe.wait_ge(s_ev, t - 3)
                for k in range(K):
                    last = nc.tensor.matmul(pp[t % 4][:, :], parts[k // DC][:, k % DC, t * P:(t + 1) * P], w[:, k, :],
                                            start=(k == 0), stop=(k == K - 1))
                last.then_inc(s_p, 1)

        @block.vector
        def _(dve):
            dve.wait_ge(s_w, 32)
            for t in range(NT):
                nc.vector.tensor_tensor(x[:, t, :], x[:, t, :], bb[:, :], ALU.add).then_inc(s_b, 1)
            for t in range(NT):
                dve.wait_ge(s_b, t + 1)
                dve.wait_ge(s_p, t + 1)
                nc.vector.tensor_tensor(x[:, t, :], x[:, t, :], pp[t % 4][:, :], ALU.add).then_inc(s_ev, 1)


def address_scores(nc, name, xT, pw, u, z):
    R = pw.shape[1]
    with Stage(nc, name) as st:
        w = st.sb("w", [P, DC, R])
        us = st.sb("us", [R, u.shape[1]])
        aT = st.sb("aT", [R, T])
        pa = [st.ps(f"pa{i}", [R, S]) for i in range(2)]
        pz = [st.ps(f"pz{i}", [P, u.shape[1]]) for i in range(2)]
        s_w, s_a, s_ae, s_z, s_ze = (st.sem(n) for n in ("w", "a", "ae", "z", "ze"))
        block = st.block()

        @block.sync
        def _(sp):
            sp.dma_start(w[:, :, :], cols(pw)).then_inc(s_w, 16)
            sp.dma_start(us[:, :], u).then_inc(s_w, 16)

        @block.tensor
        def _(pe):
            pe.wait_ge(s_w, 32)
            for b in range(B):
                if b >= 2:
                    pe.wait_ge(s_ae, b - 1)
                for c in range(DC):
                    last = nc.tensor.matmul(pa[b % 2][:, :], w[:, c, :], xT[:, c, b * S:(b + 1) * S],
                                            start=(c == 0), stop=(c == DC - 1))
                last.then_inc(s_a, 1)
            for t in range(NT):
                pe.wait_ge(s_ae, t // QT + 1)
                if t >= 2:
                    pe.wait_ge(s_ze, t - 1)
                nc.tensor.matmul(pz[t % 2][:, :], aT[:, t * P:(t + 1) * P], us[:, :], start=True, stop=True
                                 ).then_inc(s_z, 1)

        @block.scalar
        def _(act):
            for b in range(B):
                act.wait_ge(s_a, b + 1)
                nc.scalar.activation(aT[:, b * S:(b + 1) * S], pa[b % 2][:, :], ACT.Identity).then_inc(s_ae, 1)

        @block.vector
        def _(dve):
            for t in range(NT):
                dve.wait_ge(s_z, t + 1)
                nc.vector.tensor_copy(z[:, t, :], pz[t % 2][:, :]).then_inc(s_ze, 1)


def mixture(nc, name, xT, w_dram, weights, acc, fresh):
    E = w_dram.shape[0]
    with Stage(nc, name) as st:
        w = st.sb("w", [P, 2, DC, D])
        pp = [st.ps(f"pp{i}", [P, D]) for i in range(4)]
        s_w = [st.sem(f"w{i}") for i in range(2)]
        s_p, s_x = st.sem("p"), st.sem("x")
        block = st.block()

        @block.sync
        def _(sp):
            for e in range(E):
                if e >= 2:
                    sp.wait_ge(s_p, NT * (e - 1))
                sp.dma_start(w[:, e % 2, :, :], cols(w_dram[e])).then_inc(s_w[e % 2], 16)

        @block.tensor
        def _(pe):
            for m in range(E * NT):
                e, t = m // NT, m % NT
                if t == 0:
                    pe.wait_ge(s_w[e % 2], 16 * (e // 2 + 1))
                if m >= 4:
                    pe.wait_ge(s_x, m - 3)
                for c in range(DC):
                    last = nc.tensor.matmul(pp[m % 4][:, :], xT[:, c, t * P:(t + 1) * P], w[:, e % 2, c, :],
                                            start=(c == 0), stop=(c == DC - 1))
                last.then_inc(s_p, 1)

        @block.vector
        def _(dve):
            for m in range(E * NT):
                e, t = m // NT, m % NT
                dve.wait_ge(s_p, m + 1)
                if m >= NT:
                    dve.wait_ge(s_x, m - NT + 1)
                if fresh and e == 0:
                    ins = nc.vector.tensor_scalar(acc[:, t, :], pp[m % 4][:, :], weights[:, t, 0:1], None, ALU.mult)
                else:
                    ins = nc.vector.scalar_tensor_tensor(acc[:, t, :], pp[m % 4][:, :], weights[:, t, e:e + 1],
                                                         acc[:, t, :], ALU.mult, ALU.add)
                ins.then_inc(s_x, 1)


def gelu_rows(nc, name, h):
    with Stage(nc, name) as st:
        block = st.block()

        @block.scalar
        def _(act):
            for t in range(0, NT, QT):
                nc.scalar.activation(h[:, t:t + QT, :], h[:, t:t + QT, :], ACT.Gelu)


def add_choice(nc, name, weights, b2, x, ident):
    E = b2.shape[0]
    with Stage(nc, name) as st:
        b2s = st.sb("b2s", [E, D])
        wT = st.sb("wT", [E, T])
        pt = [st.ps(f"pt{i}", [E, S]) for i in range(2)]
        pp = [st.ps(f"pp{i}", [P, D]) for i in range(2)]
        s_ld, s_t, s_te, s_p, s_x = (st.sem(n) for n in ("ld", "t", "te", "p", "x"))
        block = st.block()

        @block.sync
        def _(sp):
            sp.dma_start(b2s[:, :], b2).then_inc(s_ld, 16)

        @block.tensor
        def _(pe):
            pe.wait_ge(s_ld, 16)
            for b in range(B):
                if b >= 2:
                    pe.wait_ge(s_te, b - 1)
                for i in range(QT):
                    last = nc.tensor.transpose(pt[b % 2][:, i * P:(i + 1) * P], weights[:, b * QT + i, :], ident[:, :])
                last.then_inc(s_t, 1)
            for t in range(NT):
                pe.wait_ge(s_te, t // QT + 1)
                if t >= 2:
                    pe.wait_ge(s_x, t - 1)
                nc.tensor.matmul(pp[t % 2][:, :], wT[:, t * P:(t + 1) * P], b2s[:, :], start=True, stop=True
                                 ).then_inc(s_p, 1)

        @block.scalar
        def _(act):
            for b in range(B):
                act.wait_ge(s_t, b + 1)
                nc.scalar.activation(wT[:, b * S:(b + 1) * S], pt[b % 2][:, :], ACT.Identity).then_inc(s_te, 1)

        @block.vector
        def _(dve):
            for t in range(NT):
                dve.wait_ge(s_p, t + 1)
                nc.vector.tensor_tensor(x[:, t, :], x[:, t, :], pp[t % 2][:, :], ALU.add).then_inc(s_x, 1)


def sigmoid_column(nc, name, z, out):
    with Stage(nc, name) as st:
        s_e, s_own = st.sem("e"), st.sem("own")
        block = st.block()

        @block.scalar
        def _(act):
            nc.scalar.activation(out, z, ACT.Exp, scale=-1.0).then_inc(s_e, 1)

        @block.vector
        def _(dve):
            own = InOrder(dve, s_own)
            dve.wait_ge(s_e, 1)
            own.after(nc.vector.tensor_scalar(out, out, 1.0, None, ALU.add))
            own.after(nc.vector.reciprocal(out, out))



def load(nc, name, pairs):
    with Stage(nc, name) as st:
        s_ld = st.sem("ld")
        block = st.block()

        @block.sync
        def _(sp):
            for dst, src in pairs:
                sp.dma_start(dst, src).then_inc(s_ld, 16)
            sp.wait_ge(s_ld, 16 * len(pairs))


def rows(ap):
    return ap.rearrange("(t p) n -> p t n", p=P)


def cols(ap):
    return ap.rearrange("(c p) n -> p c n", p=P)




def network(nc, a, out):
    with ExitStack() as ctx:
        def sb(name, shape, dt=F32):
            return ctx.enter_context(nc.sbuf_tensor(name, shape, dt))

        s_stored = ctx.enter_context(nc.semaphore("stored"))
        x = sb("x", [P, NT, D])
        ident = sb("ident", [P, P])
        identb = sb("identb", [P, P], BF16)
        sel_sum = sb("sel_sum", [P, GH])
        tiny = sb("tiny", [P, 1])
        iota = sb("iota", [P, 16])
        tri = sb("tri", [P, P], BF16)
        ones = sb("ones", [P, P])
        onesb = sb("onesb", [P, P], BF16)
        sel_head = nc.dram_tensor("sel_head_bf", [MR, GH, S], BF16).ap()
        qp = nc.dram_tensor("q_parts", [NPART, D, T], BF16).ap()
        kp = nc.dram_tensor("k_parts", [NPART, D, T], BF16).ap()
        vp = nc.dram_tensor("v_padded", [T, H16 * 32], F32).ap()
        scratch = (qp, kp, vp)
        xs = nc.dram_tensor("slot_rows", [4 * T, D], F32).ap()
        ys = nc.dram_tensor("slot_results", [2 * T, D], F32).ap()
        consts = (ident, identb, sel_head, sel_sum)

        with Stage(nc, "setup") as st:
            selh = st.sb("selh", [MR, GH, S])
            trif = st.sb("trif", [P, P])
            selb = st.sb("selb", [MR, GH, S], BF16)
            s_ld, s_cp, s_st = st.sem("ld"), st.sem("cp"), st.sem("st")
            block = st.block()

            @block.sync
            def _(sp):
                for dst, src in ((x[:, :, :], rows(a["x"])), (ident[:, :], a["c_ident"]),
                                 (sel_sum[:, :], a["c_selsum"]), (selh[:, :, :], a["c_selhead"]),
                                 (iota[:, :], a["c_iota"]), (trif[:, :], a["c_tri"])):
                    sp.dma_start(dst, src).then_inc(s_ld, 16)
                sp.wait_ge(s_cp, 2)
                sp.dma_start(sel_head, selb[:, :, :]).then_inc(s_st, 16)
                sp.wait_ge(s_st, 16)
                sp.wait_ge(s_ld, 96)

            @block.vector
            def _(dve):
                nc.vector.memset(tiny[:, :], 1e-11)
                nc.vector.memset(ones[:, :], 1.0)
                nc.vector.memset(onesb[:, :], 1.0)
                dve.wait_ge(s_ld, 96)
                nc.vector.tensor_copy(tri[:, :], trif[:, :])
                nc.vector.tensor_copy(identb[:, :], ident[:, :]).then_inc(s_cp, 1)
                nc.vector.tensor_copy(selb[:, :, :], selh[:, :, :]).then_inc(s_cp, 1)

        def xattn16(name, w, masked):
            with Stage(nc, name) as outer:
                with Stage(nc, name + "a") as st:
                    xn, xnT, cT = st.sb("xn", [P, NT, D]), st.sb("xnT", [P, DC, T]), st.sb("cT", [P, DC, T])
                    load(nc, name + "ld", [(cT[:, :, :], cols(a["ctxT"]))])
                    layernorm(nc, name + "ln", x, xn, xnT, ident)
                    project16(nc, name + "pj", xnT, cT, w, scratch)
                outT = outer.sb("outT", [P, B * NG, S])
                masks = None
                if masked:
                    masks = {"neg_q": outer.sb("neg_q", [P, NT, S], BF16), "neg_k": outer.sb("neg_k", [P, NT, S], BF16),
                             "any_masked": outer.sb("any_masked", [P, NT]),
                             "vmasked": outer.sb("vmasked", [P, B * NG, S])}
                    masks16(nc, name + "mk", a["mask"], a["maskT"], vp, masks["neg_q"], masks["neg_k"],
                            masks["any_masked"], masks["vmasked"])
                    masks["tiny"] = tiny
                attend16(nc, name + "at", scratch, consts, outT, masks)
                output16(nc, name + "wo", outT, w["wo"], w["bo"], x)

        a = dict(a, slot_rows=xs)

        def moe(st, name, xT, router, w1, w2, K, func, E=None, **kw):
            E = router.shape[1]
            logits, weights = st.sb("logits", [P, NT, E]), st.sb("weights", [P, NT, E])
            project_rows(nc, name + "r", xT, router,
                         lambda own, t, psum: nc.vector.tensor_copy(logits[:, t, :], psum))
            route(nc, name + "t", logits, K, weights[:, :, :], iota, tri=tri, ones=onesb, **kw)
            experts(nc, name + "e", xT, w1, w2, weights, x, func)

        xattn16("L0", {k: a["L0_" + k] for k in ("wq", "wk", "wv", "bq", "bk", "bv", "wo", "bo")}, True)
        with Stage(nc, "L0f") as st:
            xn, xnT = st.sb("xn", [P, NT, D]), st.sb("xnT", [P, DC, T])
            layernorm(nc, "L0f0", x, xn, xnT, ident)
            with Stage(nc, "L0g") as st2:
                xn1, att = st2.sb("xn1", [P, NT, D]), st2.sb("att", [P, NT, D])
                layernorm(nc, "L0f1", xn, xn1, xnT, ident, (a["L0_ln1w"], a["L0_ln1b"]))
                small_attention(nc, "L0f2", xnT, a["L0_wqkv"], att)
                transpose_rows(nc, "L0f3", att, xnT, ident)

            def residual(own, t, psum):
                own.after(nc.vector.tensor_tensor(xn[:, t, :], xn[:, t, :], psum, ALU.add))
                return nc.vector.tensor_tensor(x[:, t, :], x[:, t, :], xn[:, t, :], ALU.add)

            project_rows(nc, "L0f4", xnT, a["L0_proj"], residual)
            xn2 = st.sb("xn2", [P, NT, D])
            layernorm(nc, "L0f5", xn, xn2, xnT, ident, (a["L0_ln2w"], a["L0_ln2b"]))
            moe(st, "L0f", xnT, a["L0_router"], a["L0_w1"], a["L0_w2"], 2, ACT.Gelu_apprx_tanh, over_all=True)
        with Stage(nc, "L1x") as st:
            xnT, cT = st.sb("xnT", [P, DC, T]), st.sb("cT", [P, DC, T])
            with Stage(nc, "L1y") as st2:
                xn = st2.sb("xn", [P, NT, D])
                load(nc, "L1ld", [(cT[:, :, :], cols(a["ctxT"]))])
                layernorm(nc, "L1ln", x, xn, xnT, ident)
            masks = (st.sb("am", [P, B, QT * (QT + 1) // 2 * P]), st.sb("uT", [P, B, QT * (QT + 1) // 2 * P]),
                     st.sb("sufmax", [P, NT]), st.sb("usum", [P, NT]))
            causal_masks(nc, "L1m", a, *masks, ident)
            attend64(nc, "L1a", a, xnT, cT, masks, x, ident)
        with Stage(nc, "L1f") as st:
            xn, xnT = st.sb("xn", [P, NT, D]), st.sb("xnT", [P, DC, T])
            layernorm(nc, "L1f0", x, xn, xnT, ident)
            E, K, cap = 8, 2, T // 8
            logits, wk = st.sb("logits", [P, NT, E]), st.sb("wk", [P, NT, K])
            slots = (st.sb("slot_to", [P, K, NT], I32), st.sb("slot_from", [P, K, NT], I32))
            project_rows(nc, "L1fr", xnT, a["L1_router"],
                         lambda own, t, psum: nc.vector.tensor_copy(logits[:, t, :], psum))
            route(nc, "L1ft", logits, K, wk, iota, over_all=True, capacity=cap, tri=tri, ones=onesb,
                  spare=a["c_spare"], slots=slots)
            dispatch(nc, "L1fd", xn, slots[0], xs)
            slot_experts(nc, "L1fe", xs, ys, a["L1_w1"], a["L1_w2"], ACT.Gelu_apprx_tanh, ident)
            combine(nc, "L1fc", ys, slots[1], wk, x, a["L1_bias"])
        with Stage(nc, "L2x") as st:
            xnT, cT = st.sb("xnT", [P, DC, T]), st.sb("cT", [P, DC, T])
            hqT, crow = st.sb("hqT", [P, DC, T]), st.sb("crow", [P, NT, D])
            mcol = st.sb("mcol", [P, NT])
            load(nc, "L2ld", [(cT[:, :, :], cols(a["ctxT"])), (crow[:, :, :], rows(a["ctx"]))])
            with Stage(nc, "L2y") as st2:
                layernorm(nc, "L2ln", x, st2.sb("xn", [P, NT, D]), xnT, ident)
            similarity(nc, "L2s", a, xnT, cT, crow, hqT, mcol, ident)
            xhT, xcT = st.sb("xhT", [P, DC, T]), st.sb("xcT", [P, DC, T])
            attended_row(nc, "L2r", xnT, hqT, mcol, xhT, xcT, ident, ones)
            project_parts(nc, "L2p", (xnT, hqT, xhT, xcT), a["L2_Wqv"], a["L2_bqv"], x)
        with Stage(nc, "L2f") as st:
            xnT = st.sb("xnT", [P, DC, T])
            with Stage(nc, "L2g") as st2:
                layernorm(nc, "L2f0", x, st2.sb("xn", [P, NT, D]), xnT, ident)
            logits, weights = st.sb("logits", [P, NT, 17]), st.sb("weights", [P, NT, 17])
            project_rows(nc, "L2fr", xnT, a["L2_router"],
                         lambda own, t, psum: nc.vector.tensor_copy(logits[:, t, :], psum))
            route(nc, "L2ft", logits[:, :, 0:16], 2, weights[:, :, 0:16], iota)
            sigmoid_column(nc, "L2fs", logits[:, :, 16:17], weights[:, :, 16:17])
            experts(nc, "L2fe", xnT, a["L2_wg"], a["L2_wd"], weights, x, ACT.Silu, a["L2_wu"],
                    w_of=lambda e: min(e, 16))
        xattn16("L3", {k: a["L3_" + k] for k in ("wq", "wk", "wv", "bq", "bk", "bv", "wo", "bo")}, False)
        with Stage(nc, "L3f") as st:
            xnT, h = st.sb("xnT", [P, DC, T]), st.sb("h", [P, NT, D])
            layernorm(nc, "L3f0", x, h, xnT, ident)
            z = st.sb("z", [P, NT, 36])
            wts = [st.sb(f"wt{i}", [P, NT, 12]) for i in range(3)]
            address_scores(nc, "L3fa", xnT, a["L3_P"], a["L3_U"], z)
            for i in range(3):
                route(nc, f"L3ft{i}", z[:, :, 12 * i:12 * i + 12], 3, wts[i][:, :, :], iota)
            mixture(nc, "L3fm", xnT, a["L3_W1"], wts[0], h, True)
            gelu_rows(nc, "L3fg", h)
            transpose_rows(nc, "L3fh", h, xnT, ident)
            mixture(nc, "L3fn", xnT, a["L3_W2"], wts[1], x, False)
            add_choice(nc, "L3fb", wts[2], a["L3_b2"], x, ident)

        with Stage(nc, "store") as st:
            block = st.block()

            @block.sync
            def _(sp):
                sp.dma_start(rows(out), x[:, :, :]).then_inc(s_stored, 16)
                sp.wait_ge(s_stored, 16)


def kernel(**inputs):
    import numpy as np
    import concourse.bacc as _bacc
    from concourse.bass_utils import run_bass_kernel_spmd as _run

    i = {k: np.asarray(v) for k, v in inputs.items()}
    c = np.ascontiguousarray
    f32 = np.float32

    def pad_heads(w):
        out = np.zeros((H16, 32, w.shape[1]), f32)
        out[:, :HD] = w.reshape(H16, HD, w.shape[1])
        return out.reshape(H16 * 32, w.shape[1])

    Stage.USED.clear()
    a = {"x": i["x"].reshape(T, D), "ctxT": c(i["ctx_1024"].reshape(T, D).T),
         "mask": i["mask_BxSxS2_ik1"], "maskT": c(i["mask_BxSxS2_ik1"].transpose(0, 2, 1)),
         "c_ident": np.eye(P, dtype=f32)}
    selsum = np.zeros((P, GH), f32)
    for h in range(GH):
        selsum[32 * h + HD, h] = 1.0
    a["c_selsum"] = selsum
    selhead = np.zeros((NPART, GH, GH, S), f32)
    for h in range(GH):
        selhead[:, h, h, :] = 1.0
    a["c_selhead"] = selhead.reshape(MR, GH, S)
    for k in ("wq", "wk", "wv"):
        a["L0_" + k] = c(i["L0_xattn_" + k].T)
    for k in ("bq", "bk", "bv", "bo"):
        a["L0_" + k] = i["L0_xattn_" + k]
    a["L0_wo"] = pad_heads(i["L0_xattn_wo"].T)
    a["c_iota"] = np.tile(np.arange(16, dtype=f32), (P, 1))
    a["c_tri"] = np.triu(np.ones((P, P), f32), 1)
    for k in ("ln1w", "ln1b", "ln2w", "ln2b"):
        a["L0_" + k] = i["L0_ffn_" + k[:3] + {"w": "_weight", "b": "_bias"}[k[3]]]
    a["L0_wqkv"] = c(i["L0_ffn_qkv_weight"].T)
    a["L0_proj"] = c(i["L0_ffn_proj_weight"].T)
    a["L0_router"] = c(i["L0_ffn_router_weight"].T)
    a["L0_w1"], a["L0_w2"] = i["L0_ffn_moe_w1"], i["L0_ffn_moe_w2"]
    for k in "QKV":
        a["L1_W" + k] = c(i["L1_xattn_W_" + k].transpose(1, 0, 2).reshape(D, H16 * HB))
    for k in "QK":
        a["L1_b" + k] = c(i["L1_xattn_b_" + k].reshape(NP, P).T)
    a["L1_bV"] = i["L1_xattn_b_V"].reshape(-1)
    a["L1_WO"], a["L1_bO"] = i["L1_xattn_W_O"].reshape(H16 * HB, D), i["L1_xattn_b_O"]
    a["addm"] = i["mask_Bx1x1xS2_ff0"].reshape(T)
    is_later = np.arange(S)[None, :] > np.arange(S)[:, None]
    a["c_later"] = c(np.where(is_later, f32(BIG), f32(0)).reshape(QT, P, S).transpose(1, 0, 2))
    a["c_fill"] = c(np.where(is_later, f32(-1e5), f32(BIG)).reshape(QT, P, S).transpose(1, 0, 2))
    a["L1_router"] = i["L1_ffn_router_w"]
    a["L1_w1"], a["L1_w2"], a["L1_bias"] = i["L1_ffn_w1"], i["L1_ffn_w2"], i["L1_ffn_bias"].reshape(D)
    a["c_spare"] = c((2 * T + np.arange(2 * T, dtype=f32)).reshape(2, NT, P).transpose(2, 0, 1))
    a["ctx"] = i["ctx_1024"].reshape(T, D)
    a["L2_wsim"] = c(i["L2_xattn_w_sim"].reshape(3, DC, P).transpose(2, 0, 1))
    a["L2_bsim"], a["L2_Wqv"], a["L2_bqv"] = i["L2_xattn_b_sim"], i["L2_xattn_W_qv"], i["L2_xattn_b_qv"]
    a["L2_router"] = c(np.concatenate([i["L2_ffn_Wg"], i["L2_ffn_Wsg"]]).T)
    for k, n in (("g", "gate"), ("u", "up")):
        shared = i["L2_ffn_Ws_" + n].reshape(4, P, D)
        a["L2_w" + k] = c(np.concatenate([i["L2_ffn_We_" + n], shared]).transpose(0, 2, 1))
    shared = i["L2_ffn_Ws_down"].T.reshape(4, P, D)
    a["L2_wd"] = c(np.concatenate([i["L2_ffn_We_down"].transpose(0, 2, 1), shared]))
    kv = i["L3_xattn_Wkv"].reshape(D, H16, 2, HD)
    bkv = i["L3_xattn_bkv"].reshape(H16, 2, HD)
    a["L3_wq"], a["L3_bq"] = i["L3_xattn_Wq"], i["L3_xattn_bq"]
    for j, k in enumerate("kv"):
        a["L3_w" + k], a["L3_b" + k] = c(kv[:, :, j].reshape(D, D)), c(bkv[:, j].reshape(D))
    a["L3_wo"], a["L3_bo"] = pad_heads(i["L3_xattn_Wp"]), i["L3_xattn_bp"]
    a["L3_P"] = c(i["L3_ffn_P_w"].T)
    a["L3_U"] = c(np.concatenate([i["L3_ffn_U1"], i["L3_ffn_U2"], i["L3_ffn_U3"]]).T)
    a["L3_W1"], a["L3_W2"] = c(i["L3_ffn_W1"].transpose(0, 2, 1)), c(i["L3_ffn_W2"].transpose(0, 2, 1))
    a["L3_b2"] = i["L3_ffn_b2"]

    nc = _bacc.Bacc("TRN2", target_bir_lowering=False, num_devices=1)
    arrays, aps = {}, {}
    for name, v in a.items():
        v = c(v)
        arrays[f"in_{name}"] = v
        aps[name] = nc.dram_tensor(f"in_{name}", v.shape, mybir.dt.from_np(v.dtype), kind="ExternalInput").ap()
    out = nc.dram_tensor("out_0", (T, D), F32, kind="ExternalOutput").ap()
    network(nc, aps, out)
    r = _run(nc, [arrays], core_ids=[0])
    return r.results[0]["out_0"].reshape(B, S, D)
```

```python
import concourse.bass as bass
from concourse import mybir
from contextlib import ExitStack

F32 = mybir.dt.float32
BF16 = mybir.dt.bfloat16
I32 = mybir.dt.int32
U32 = mybir.dt.uint32
ALU = mybir.AluOpType
ACT = mybir.ActivationFunctionType
AX = mybir.AxisListType

P = 128
D = 256
DC = D // P
B = 4
S = 512
T = B * S
NT = T // P
QT = S // P
BIG = -1.0e30
EPS = 1e-5

H16 = 16
HD = 16
GH = 4
NG = H16 // GH
NPART = 3
Q_PARTS = (0, 0, 1, 0, 2, 1)
K_PARTS = (0, 1, 0, 2, 0, 1)
KR = len(Q_PARTS) * HD
MR = NPART * GH


class Stage:

    USED = []

    def __init__(self, nc, name):
        self.nc, self.name, self.ctx, self.sems = nc, name, ExitStack(), []

    def __enter__(self):
        self.ctx.__enter__()
        return self

    def __exit__(self, *a):
        self.ctx.__exit__(*a)
        self.USED.extend(self.sems)
        if len(self.USED) > 100:
            self.nc.clear_and_free_semaphores(list(self.USED))
            self.nc.all_engine_barrier()
            self.USED.clear()

    def sb(self, name, shape, dt=F32):
        return self.ctx.enter_context(self.nc.sbuf_tensor(f"{self.name}_{name}", shape, dt))

    def ps(self, name, shape, dt=F32):
        return self.ctx.enter_context(self.nc.psum_tensor(f"{self.name}_{name}", shape, dt))

    def sem(self, name):
        self.sems.append(self.nc.alloc_semaphore(f"{self.name}_{name}"))
        return self.sems[-1]

    def block(self):
        return self.ctx.enter_context(self.nc.Block())


class InOrder:

    def __init__(self, eng, sem):
        self.eng, self.sem, self.n = eng, sem, 0

    def after(self, ins):
        self.n += 1
        ins.then_inc(self.sem, 1)
        self.eng.wait_ge(self.sem, self.n)


def layernorm(nc, name, x, xn, xnT, ident, affine=None):
    with Stage(nc, name) as st:
        stats = st.sb("stats", [P, NT, 6])
        mv = st.sb("mv", [P, NT, 2])
        ve = st.sb("ve", [P, NT])
        std = st.sb("std", [P, NT])
        rstd = st.sb("rstd", [P, NT])
        wb = st.sb("wb", [P, 2, DC])
        tp = [st.ps(f"tp{i}", [P, S]) for i in range(4)]
        s_own, s_var, s_std, s_norm, s_tr, s_ev, s_wb = (
            st.sem(n) for n in ("own", "var", "std", "norm", "tr", "ev", "wb"))
        block = st.block()

        @block.sync
        def _(sp):
            if affine is not None:
                for i in range(2):
                    for c in range(DC):
                        sp.dma_start(wb[:, i, c:c + 1], affine[i][c * P:(c + 1) * P].unsqueeze(1)).then_inc(s_wb, 16)

        @block.vector
        def _(dve):
            own = InOrder(dve, s_own)
            for t in range(NT):
                last = nc.vector.bn_stats(stats[:, t, :], x[:, t, :])
            own.after(last)
            for t in range(NT):
                last = nc.vector.bn_aggr(mv[:, t, :], stats[:, t, :])
            own.after(last)
            nc.vector.tensor_scalar(ve[:, :], mv[:, :, 1], EPS, None, ALU.add).then_inc(s_var, 1)
            dve.wait_ge(s_std, 1)
            own.after(nc.vector.reciprocal(rstd[:, :], std[:, :]))
            for t in range(NT):
                nc.vector.tensor_scalar(xn[:, t, :], x[:, t, :], mv[:, t, 0:1], rstd[:, t:t + 1],
                                        ALU.subtract, ALU.mult).then_inc(s_norm, 1)

        @block.tensor
        def _(pe):
            for n in range(B * DC):
                g, c = n // DC, n % DC
                pe.wait_ge(s_norm, QT * (g + 1))
                if n >= 4:
                    pe.wait_ge(s_ev, n - 3)
                for i in range(QT):
                    last = nc.tensor.transpose(tp[n % 4][:, i * P:(i + 1) * P],
                                               xn[:, g * QT + i, c * P:(c + 1) * P], ident[:, :])
                last.then_inc(s_tr, 1)

        @block.scalar
        def _(act):
            act.wait_ge(s_var, 1)
            nc.scalar.activation(std[:, :], ve[:, :], ACT.Sqrt).then_inc(s_std, 1)
            if affine is not None:
                act.wait_ge(s_wb, 16 * 2 * DC)
            for n in range(B * DC):
                g, c = n // DC, n % DC
                act.wait_ge(s_tr, n + 1)
                dst = xnT[:, c, g * S:(g + 1) * S]
                if affine is None:
                    nc.scalar.activation(dst, tp[n % 4][:, :], ACT.Identity).then_inc(s_ev, 1)
                else:
                    nc.scalar.activation(dst, tp[n % 4][:, :], ACT.Identity, bias=wb[:, 1, c:c + 1],
                                         scale=wb[:, 0, c:c + 1]).then_inc(s_ev, 1)


def project16(nc, name, srcT_q, srcT_kv, w, scratch):
    qp, kp, vp = scratch
    scale = HD ** -0.5
    with Stage(nc, name) as st:
        wsb = {k: st.sb("w" + k, [P, DC, D]) for k in "qkv"}
        bqk = st.sb("bqk", [P, 2, DC])
        bv = st.sb("bv", [P, D])
        full = st.sb("full", [P, 2, S])
        rest = st.sb("rest", [P, 2, S])
        parts = st.sb("parts", [P, 2, NPART, S], BF16)
        vt = st.sb("vt", [P, 2, H16, 32])
        pj = [st.ps(f"pj{i}", [P, S]) for i in range(4)]
        pv = [st.ps(f"pv{i}", [P, D]) for i in range(2)]
        s_w, s_pj, s_full, s_hi, s_rest, s_mid, s_low, s_pv, s_vt, s_own = (
            st.sem(n) for n in ("w", "pj", "full", "hi", "rest", "mid", "low", "pv", "vt", "own"))
        s_out = [st.sem(f"out{i}") for i in range(2)]
        s_vo = [st.sem(f"vo{i}") for i in range(2)]
        JOBS = [(k, hb, b) for b in range(B) for k in range(2) for hb in range(DC)]
        block = st.block()

        @block.sync
        def _(sp):
            for k in "qkv":
                sp.dma_start(wsb[k][:, :, :], w["w" + k].rearrange("(c p) n -> p c n", p=P)).then_inc(s_w, 16)
            for i, k in enumerate("qk"):
                for c in range(DC):
                    sp.dma_start(bqk[:, i, c:c + 1], w["b" + k][c * P:(c + 1) * P].unsqueeze(1)).then_inc(s_w, 16)
            sp.dma_start(bv[:, :], w["bv"].partition_broadcast(P)).then_inc(s_w, 16)
            for j, (k, hb, b) in enumerate(JOBS):
                sp.wait_ge(s_low, j + 1)
                dst = (qp, kp)[k][:, hb * P:(hb + 1) * P, b * S:(b + 1) * S].rearrange("a p n -> p a n")
                sp.dma_start(dst, parts[:, j % 2, :, :]).then_inc(s_out[j % 2], 16)
            for i in range(2):
                sp.wait_ge(s_out[i], 16 * (len(JOBS) // 2))
                sp.wait_ge(s_vo[i], 16 * (NT // 2))

        @block.tensor
        def _(pe):
            pe.wait_ge(s_w, 16 * 8)
            for j, (k, hb, b) in enumerate(JOBS):
                if j >= 4:
                    pe.wait_ge(s_full, j - 3)
                src = (srcT_q, srcT_kv)[k]
                for c in range(DC):
                    last = nc.tensor.matmul(pj[j % 4][:, :], wsb["qk"[k]][:, c, hb * P:(hb + 1) * P],
                                            src[:, c, b * S:(b + 1) * S], start=(c == 0), stop=(c == DC - 1))
                last.then_inc(s_pj, 1)
                t = j
                if t >= 2:
                    pe.wait_ge(s_vt, t - 1)
                for c in range(DC):
                    last = nc.tensor.matmul(pv[t % 2][:, :], srcT_kv[:, c, t * P:(t + 1) * P],
                                            wsb["v"][:, c, :], start=(c == 0), stop=(c == DC - 1))
                last.then_inc(s_pv, 1)

        @block.vector
        def _(dve):
            own = InOrder(dve, s_own)
            own.after(nc.vector.memset(vt[:, :, :, :], 0.0))
            own.after(nc.vector.memset(vt[:, :, :, HD:HD + 1], 1.0))
            dve.wait_ge(s_w, 16 * 8)
            for j, (k, hb, b) in enumerate(JOBS):
                dve.wait_ge(s_pj, j + 1)
                if j >= 2:
                    dve.wait_ge(s_low, j - 1)
                nc.vector.tensor_scalar(full[:, j % 2, :], pj[j % 4][:, :], bqk[:, k, hb:hb + 1],
                                        scale if k == 0 else 1.0, ALU.add, ALU.mult).then_inc(s_full, 1)
                dve.wait_ge(s_hi, j + 1)
                nc.vector.tensor_tensor(rest[:, j % 2, :], full[:, j % 2, :], parts[:, j % 2, 0, :],
                                        ALU.subtract).then_inc(s_rest, 1)
                dve.wait_ge(s_pv, j + 1)
                if j >= 2:
                    dve.wait_ge(s_vo[j % 2], 16 * (j // 2))
                nc.vector.tensor_tensor(vt[:, j % 2, :, 0:HD], pv[j % 2][:, :].rearrange("p (h d) -> p h d", h=H16),
                                        bv[:, :].rearrange("p (h d) -> p h d", h=H16), ALU.add).then_inc(s_vt, 1)

        @block.scalar
        def _(act):
            for j in range(len(JOBS)):
                act.wait_ge(s_full, j + 1)
                if j >= 2:
                    act.wait_ge(s_out[j % 2], 16 * (j // 2))
                nc.scalar.activation(parts[:, j % 2, 0, :], full[:, j % 2, :], ACT.Identity).then_inc(s_hi, 1)
                act.wait_ge(s_rest, j + 1)
                nc.scalar.activation(parts[:, j % 2, 1, :], rest[:, j % 2, :], ACT.Identity).then_inc(s_mid, 1)

        @block.gpsimd
        def _(pool):
            for j in range(len(JOBS)):
                pool.wait_ge(s_mid, j + 1)
                nc.gpsimd.tensor_tensor(parts[:, j % 2, 2, :], rest[:, j % 2, :], parts[:, j % 2, 1, :],
                                        ALU.subtract).then_inc(s_low, 1)
                pool.wait_ge(s_vt, j + 1)
                pool.dma_start(vp[j * P:(j + 1) * P, :], vt[:, j % 2, :, :].rearrange("p h d -> p (h d)")
                               ).then_inc(s_vo[j % 2], 16)


def masks16(nc, name, mask, maskT, vp, neg_q, neg_k, any_masked, vmasked):
    with Stage(nc, name) as st:
        mq = st.sb("mq", [P, QT, S], I32)
        mk = st.sb("mk", [P, 2, QT, S], I32)
        zk = st.sb("zk", [P, 2, QT, S])
        vs = st.sb("vs", [P, 2, QT, H16 * 32])
        vm = [st.ps(f"vm{i}", [P, S]) for i in range(4)]
        s_mk = [st.sem(f"mk{i}") for i in range(2)]
        s_vs = [st.sem(f"vs{i}") for i in range(2)]
        s_mq, s_q, s_z, s_nk, s_vm, s_own, s_vsum, s_row = (
            st.sem(n) for n in ("mq", "q", "z", "nk", "vm", "own", "vsum", "row"))
        block = st.block()

        @block.sync
        def _(sp):
            for b in range(B):
                if b >= 2:
                    sp.wait_ge(s_z, b - 1)
                sp.dma_start(mk[:, b % 2, :, :], maskT[b].rearrange("(t p) q -> p t q", p=P)).then_inc(s_mk[b % 2], 16)
                if b >= 2:
                    sp.wait_ge(s_vm, NG * (b - 1))
                sp.dma_start(vs[:, b % 2, :, :], vp[b * S:(b + 1) * S, :].rearrange("(t p) n -> p t n", p=P)
                             ).then_inc(s_vs[b % 2], 16)
                if b >= 1:
                    sp.wait_ge(s_q, b)
                sp.dma_start(mq[:, :, :], mask[b].rearrange("(t p) k -> p t k", p=P)).then_inc(s_mq, 16)

        @block.vector
        def _(dve):
            for b in range(B):
                t4 = slice(b * QT, (b + 1) * QT)
                dve.wait_ge(s_mk[b % 2], 16 * (b // 2 + 1))
                if b >= 2:
                    dve.wait_ge(s_vm, NG * (b - 1))
                    dve.wait_ge(s_nk, b - 1)
                nc.vector.tensor_scalar(zk[:, b % 2, :, :], mk[:, b % 2, :, :], 0.0, None, ALU.is_equal).then_inc(s_z, 1)
                dve.wait_ge(s_mq, 16 * (b + 1))
                nc.vector.tensor_scalar(neg_q[:, t4, :], mq[:, :, :], 0.0, BIG, ALU.is_equal, ALU.mult
                                        ).then_inc(s_q, 1)
                dve.wait_ge(s_q, b + 1)
                nc.vector.tensor_reduce(any_masked[:, t4], neg_q[:, t4, :], AX.X, ALU.min).then_inc(s_row, 1)
            dve.wait_ge(s_row, B)
            own = InOrder(dve, s_own)
            own.after(nc.vector.tensor_scalar(any_masked[:, :], any_masked[:, :], 0.0, BIG, ALU.is_equal, ALU.mult))
            own.after(nc.vector.tensor_scalar(any_masked[:, :], any_masked[:, :], 1e-11, None, ALU.add))

        @block.tensor
        def _(pe):
            for b in range(B):
                pe.wait_ge(s_z, b + 1)
                pe.wait_ge(s_vs[b % 2], 16 * (b // 2 + 1))
                for g in range(NG):
                    n = b * NG + g
                    if n >= 4:
                        pe.wait_ge(s_vsum, n - 3)
                    for t in range(QT):
                        last = nc.tensor.matmul(vm[n % 4][:, :], vs[:, b % 2, t, g * P:(g + 1) * P], zk[:, b % 2, t, :],
                                                start=(t == 0), stop=(t == QT - 1))
                    last.then_inc(s_vm, 1)

        @block.scalar
        def _(act):
            for b in range(B):
                act.wait_ge(s_z, b + 1)
                nc.scalar.activation(neg_k[:, b * QT:(b + 1) * QT, :], zk[:, b % 2, :, :], ACT.Identity, scale=BIG
                                     ).then_inc(s_nk, 1)
                for g in range(NG):
                    n = b * NG + g
                    act.wait_ge(s_vm, n + 1)
                    nc.scalar.activation(vmasked[:, n, :], vm[n % 4][:, :], ACT.Identity).then_inc(s_vsum, 1)


def attend16(nc, name, scratch, consts, outT, masks=None):
    qp, kp, vp = scratch
    ident, identb, sel_head, sel_sum = consts
    N = B * NG
    R = 4
    with Stage(nc, name) as st:
        qs = st.sb("qs", [P, R, GH, S], BF16)
        ks = st.sb("ks", [P, R, GH, S], BF16)
        vs = st.sb("vs", [P, R, QT, P])
        junk = st.sb("junk", [P, 2, S], BF16)
        rowmax = st.sb("rowmax", [P, 2, QT, GH])
        neg = st.sb("neg", [P, R, QT, GH])
        negr = st.sb("negr", [P, QT, GH])
        negp = st.sb("negp", [P, QT, P], BF16)
        prob = st.sb("prob", [P, 2, GH, 2, S])
        expand = st.sb("expand", [P, QT, GH, 32])
        em = st.sb("em", [P, QT, GH])
        rec = st.sb("rec", [P, QT, GH])
        oT = st.sb("oT", [P, S])
        sq = [st.ps(f"sq{i}", [P, S]) for i in range(2)]
        sk = [st.ps(f"sk{i}", [P, 2, S]) for i in range(2)]
        acc = st.ps("acc", [P, S])
        misc = st.ps("misc", [P, S])
        miscb = misc[:, :].bitcast(BF16)[:, 0:S]
        s_q = [st.sem(f"q{i}") for i in range(R)]
        s_v = [st.sem(f"v{i}") for i in range(R)]
        (s_sq, s_max, s_negp, s_mt, s_qm, s_sk, s_exp, s_pv, s_em, s_ex, s_eb, s_o,
         s_sum, s_rb, s_out, s_own, s_hd, s_qh) = (
            st.sem(n) for n in ("sq", "max", "negp", "mt", "qm", "sk", "exp", "pv", "em",
                                "ex", "eb", "o", "sum", "rb", "out", "own", "hd", "qh"))
        block = st.block()
        NB = 1 if masks is None else 2

        @block.sync
        def _(sp):
            for i in range(R):
                sp.dma_start(ks[KR:KR + MR, i, :, :], sel_head).then_inc(s_hd, 16)
            for n in range(N):
                b, g = n // NG, n % NG
                if n >= R:
                    sp.wait_ge(s_sk, 8 * (n - R + 1))
                for buf, src, order in ((qs, qp, Q_PARTS), (ks, kp, K_PARTS)):
                    for i, a in enumerate(order):
                        sp.dma_start(buf[i * HD:(i + 1) * HD, n % R, :, :],
                                     src[a, g * GH * HD:(g + 1) * GH * HD, b * S:(b + 1) * S]
                                     .rearrange("(h d) n -> d h n", h=GH)).then_inc(s_q[n % R], 16)
                if n >= R:
                    sp.wait_ge(s_pv, 2 * (n - R + 1))
                sp.dma_start(vs[:, n % R, :, :], vp[b * S:(b + 1) * S, g * P:(g + 1) * P]
                             .rearrange("(t p) n -> p t n", p=P)).then_inc(s_v[n % R], 16)

        @block.tensor
        def _(pe):
            def row_scores(n, i):
                h, t = i // QT, i % QT
                k = n * GH * QT + i
                if k >= 2:
                    pe.wait_ge(s_max, k - 1)
                nc.tensor.matmul(sq[k % 2][:, :], qs[0:KR, n % R, h, t * P:(t + 1) * P], ks[0:KR, n % R, h, :],
                                 start=True, stop=True).then_inc(s_sq, 1)

            def turn_max(n):
                pe.wait_ge(s_negp, n + 1)
                if n >= 1:
                    pe.wait_ge(s_qm, n)
                if n >= 3:
                    pe.wait_ge(s_out, n - 2)
                for t in range(QT):
                    last = nc.tensor.transpose(miscb[:, t * P:(t + 1) * P], negp[:, t, :], identb[:, :])
                last.then_inc(s_mt, 1)

            def key_scores(n, u):
                h, k = u % GH, n * 8 + u
                if k >= 2:
                    pe.wait_ge(s_exp, k - 1)
                for i in range(2):
                    t = 2 * (u // GH) + i
                    last = nc.tensor.matmul(sk[k % 2][:, i, :], ks[0:KR + MR, n % R, h, t * P:(t + 1) * P],
                                            qs[0:KR + MR, n % R, h, :], start=True, stop=(masks is None))
                    if masks is not None:
                        last = nc.tensor.matmul(sk[k % 2][:, i, :], identb[:, :],
                                                masks["neg_k"][:, (n // NG) * QT + t, :], start=False, stop=True)
                last.then_inc(s_sk, 1)

            def values(n, half):
                pe.wait_ge(s_exp, n * 8 + 4 * half + 4)
                if half == 0:
                    pe.wait_ge(s_v[n % R], 16 * (n // R + 1))
                    if n >= 1:
                        pe.wait_ge(s_o, n)
                for i in range(2):
                    for h in range(GH):
                        t = 2 * half + i
                        last = nc.tensor.matmul(acc[32 * h:32 * h + 32, :], vs[:, n % R, t, 32 * h:32 * h + 32],
                                                prob[:, half, h, i, :], start=(t == 0), stop=(t == QT - 1),
                                                tile_position=(0, 32 * h), skip_group_check=True)
                last.then_inc(s_pv, 1)

            def broadcast(n, which):
                pe.wait_ge(s_ex, NB * n + which + 1)
                if which == 0:
                    pe.wait_ge(s_qm, min(n + 3, N))
                for t in range(QT):
                    last = nc.tensor.transpose(misc[:, t * P:(t + 1) * P],
                                               expand[:, t, :, :].rearrange("p h d -> p (h d)"), ident[:, :])
                last.then_inc(s_rb if which == NB - 1 else s_eb, 1)

            def sums(n):
                pe.wait_ge(s_o, n + 1)
                pe.wait_ge(s_qm, min(n + 3, N))
                for t in range(QT):
                    last = nc.tensor.matmul(misc[:, t * GH:(t + 1) * GH], oT[:, t * P:(t + 1) * P], sel_sum[:, :],
                                            start=True, stop=True)
                last.then_inc(s_sum, 1)

            pe.wait_ge(s_hd, 16 * R)
            for s in range(N + 4):
                if s < N:
                    pe.wait_ge(s_q[s % R], 16 * 12 * (s // R + 1))
                keys, last_group = 2 <= s < N + 2, 3 <= s < N + 3
                for u in range(8):
                    if u == 2 and 1 <= s <= N:
                        turn_max(s - 1)
                    if keys:
                        if u == 0:
                            pe.wait_ge(s_qh, s - 1)
                        key_scores(s - 2, u)
                    if last_group:
                        if u == 1:
                            values(s - 3, 1)
                        if u == 4 and masks is not None:
                            broadcast(s - 3, 0)
                        if u == 6:
                            sums(s - 3)
                    if s < N:
                        row_scores(s, 2 * u)
                        row_scores(s, 2 * u + 1)
                    if u == 0 and s >= 4:
                        broadcast(s - 4, NB - 1)
                    if keys and u == 6:
                        values(s - 2, 0)

        @block.vector
        def _(dve):
            own = InOrder(dve, s_own)
            own.after(nc.vector.memset(negp[:, :, :], 0.0))

            def row_max(n, i):
                h, t = i // QT, i % QT
                k = n * GH * QT + i
                dve.wait_ge(s_sq, k + 1)
                dst = rowmax[:, n % 2, t, h:h + 1]
                if masks is None:
                    ins = nc.vector.tensor_reduce(dst, sq[k % 2][:, :], AX.X, ALU.max)
                else:
                    if k >= 2:
                        dve.wait_ge(s_max, k - 1)
                    ins = nc.vector.tensor_tensor_reduce(junk[:, k % 2, :], sq[k % 2][:, :],
                                                         masks["neg_q"][:, (n // NG) * QT + t, :], 1.0, 3.0 * BIG,
                                                         ALU.add, ALU.max, dst)
                ins.then_inc(s_max, 1)

            def minus_max(n):
                dve.wait_ge(s_max, GH * QT * (n + 1))
                m, x = rowmax[:, n % 2, :, :], neg[:, n % R, :, :]
                if masks is not None:
                    for t in range(QT):
                        c = (n // NG) * QT + t
                        last = nc.vector.tensor_scalar(m[:, t, :], m[:, t, :], masks["any_masked"][:, c:c + 1], None,
                                                       ALU.max)
                    own.after(last)
                if n >= R and masks is not None:
                    dve.wait_ge(s_em, n - R + 1)
                own.after(nc.vector.tensor_scalar(x, m, -1.0, None, ALU.mult))
                if n >= 1:
                    dve.wait_ge(s_mt, n)
                part = [negp[:, :, KR + a * GH:KR + (a + 1) * GH] for a in range(NPART)]
                own.after(nc.vector.tensor_copy(part[0], x))
                own.after(nc.vector.tensor_tensor(negr[:, :, :], x, part[0], ALU.subtract))
                own.after(nc.vector.tensor_copy(part[1], negr[:, :, :]))
                nc.vector.tensor_tensor(part[2], negr[:, :, :], part[1], ALU.subtract).then_inc(s_negp, 1)

            def gather(n):
                if n >= 1:
                    dve.wait_ge(s_out, n)
                if masks is not None:
                    dve.wait_ge(s_eb, n + 1)
                    own.after(nc.vector.tensor_tensor(oT[:, :], misc[:, :], masks["vmasked"][:, n, :], ALU.mult))
                    dve.wait_ge(s_pv, 2 * (n + 1))
                    nc.vector.tensor_tensor(oT[:, :], acc[:, :], oT[:, :], ALU.add).then_inc(s_o, 1)
                else:
                    dve.wait_ge(s_pv, 2 * (n + 1))
                    nc.vector.tensor_copy(oT[:, :], acc[:, :]).then_inc(s_o, 1)

            def spread(n, what, k):
                if n >= 1 or k:
                    dve.wait_ge(s_rb if (masks is None or k == 0) else s_eb, n if (masks is None or k == 0) else n + 1)
                nc.vector.tensor_copy(expand[:, :, :, :], what[:, :, :].unsqueeze(3).to_broadcast([P, QT, GH, 32])
                                      ).then_inc(s_ex, 1)

            def invert(n):
                dve.wait_ge(s_sum, n + 1)
                own.after(nc.vector.reciprocal(rec[:, :, :], misc[:, 0:QT * GH].rearrange("p (t h) -> p t h", t=QT)))
                spread(n, rec, NB - 1)

            def finish(n):
                dve.wait_ge(s_rb, n + 1)
                nc.vector.tensor_tensor(outT[:, n, :], oT[:, :], misc[:, :], ALU.mult).then_inc(s_out, 1)

            for s in range(N + 4):
                for u in range(8):
                    if u == 1:
                        if s >= 4:
                            finish(s - 4)
                        if 1 <= s <= N:
                            minus_max(s - 1)
                    if 3 <= s < N + 3:
                        if u == 2 and masks is not None:
                            dve.wait_ge(s_em, s - 2)
                            spread(s - 3, em, 0)
                        if u == 5:
                            gather(s - 3)
                        if u == 7:
                            invert(s - 3)
                    if s < N:
                        row_max(s, 2 * u)
                        row_max(s, 2 * u + 1)

        @block.scalar
        def _(act):
            for s in range(N + 3):
                for u in range(8):
                    if 2 <= s < N + 2:
                        n = s - 2
                        k = n * 8 + u
                        act.wait_ge(s_sk, k + 1)
                        if n >= 1:
                            act.wait_ge(s_pv, 2 * (n - 1) + u // GH + 1)
                        nc.scalar.activation(prob[:, u // GH, u % GH, :, :], sk[k % 2][:, :, :], ACT.Exp
                                             ).then_inc(s_exp, 1)
                    if u == 0 and s >= 3 and masks is not None:
                        if s >= 4:
                            act.wait_ge(s_ex, NB * (s - 4) + 1)
                        act.wait_ge(s_negp, s - 2)
                        nc.scalar.activation(em[:, :, :], neg[:, (s - 3) % R, :, :], ACT.Exp, bias=masks["tiny"][:, 0:1]
                                             ).then_inc(s_em, 1)
                    if u == 3 and 1 <= s <= N:
                        act.wait_ge(s_mt, s)
                        nc.scalar.activation(qs[KR:KR + MR, (s - 1) % R, 0, :], miscb[KR:KR + MR, :], ACT.Identity
                                             ).then_inc(s_qm, 1)

        @block.gpsimd
        def _(pool):
            for n in range(N):
                pool.wait_ge(s_qm, n + 1)
                nc.gpsimd.tensor_copy(qs[KR:KR + MR, n % R, 1:GH, :],
                                      qs[KR:KR + MR, n % R, 0:1, :].to_broadcast([MR, GH - 1, S])).then_inc(s_qh, 1)


def output16(nc, name, aT, wo, bo, x):
    with Stage(nc, name) as st:
        w = st.sb("w", [P, NG, D])
        bb = st.sb("bb", [P, D])
        pp = [st.ps(f"pp{i}", [P, D]) for i in range(4)]
        s_w, s_p, s_x, s_b = (st.sem(n) for n in ("w", "p", "x", "b"))
        block = st.block()

        @block.sync
        def _(sp):
            sp.dma_start(w[:, :, :], wo.rearrange("(g p) n -> p g n", p=P)).then_inc(s_w, 16)
            sp.dma_start(bb[:, :], bo.partition_broadcast(P)).then_inc(s_w, 16)

        @block.tensor
        def _(pe):
            pe.wait_ge(s_w, 32)
            for t in range(NT):
                if t >= 4:
                    pe.wait_ge(s_x, t - 3)
                for g in range(NG):
                    last = nc.tensor.matmul(pp[t % 4][:, :], aT[:, (t // QT) * NG + g, (t % QT) * P:(t % QT + 1) * P],
                                            w[:, g, :], start=(g == 0), stop=(g == NG - 1))
                last.then_inc(s_p, 1)

        @block.vector
        def _(dve):
            dve.wait_ge(s_w, 32)
            for t in range(NT):
                nc.vector.tensor_tensor(x[:, t, :], x[:, t, :], bb[:, :], ALU.add).then_inc(s_b, 1)
            for t in range(NT):
                dve.wait_ge(s_b, t + 1)
                dve.wait_ge(s_p, t + 1)
                nc.vector.tensor_tensor(x[:, t, :], x[:, t, :], pp[t % 4][:, :], ALU.add).then_inc(s_x, 1)


def transpose_rows(nc, name, src, dstT, ident):
    with Stage(nc, name) as st:
        tp = [st.ps(f"tp{i}", [P, S]) for i in range(4)]
        s_tr, s_ev = st.sem("tr"), st.sem("ev")
        block = st.block()

        @block.tensor
        def _(pe):
            for n in range(B * DC):
                g, c = n // DC, n % DC
                if n >= 4:
                    pe.wait_ge(s_ev, n - 3)
                for i in range(QT):
                    last = nc.tensor.transpose(tp[n % 4][:, i * P:(i + 1) * P],
                                               src[:, g * QT + i, c * P:(c + 1) * P], ident[:, :])
                last.then_inc(s_tr, 1)

        @block.scalar
        def _(act):
            for n in range(B * DC):
                g, c = n // DC, n % DC
                act.wait_ge(s_tr, n + 1)
                nc.scalar.activation(dstT[:, c, g * S:(g + 1) * S], tp[n % 4][:, :], ACT.Identity).then_inc(s_ev, 1)


def small_attention(nc, name, srcT, wqkv, att):
    HK = 4
    R = H16 // HK
    SL = B
    NB = NT // SL
    W = (H16 + 2 * HK) * HD
    PAIRS = [(s, t) for s in range(SL) for t in range(s + 1)]
    with Stage(nc, name) as st:
        w = st.sb("w", [P, DC, W])
        qkv = st.sb("qkv", [P, NT, W])
        prod = st.sb("prod", [P, 2, NB, H16 * HD])
        sc = st.sb("sc", [P, len(PAIRS), NB * H16])
        mx = st.sb("mx", [P, SL, NB * H16])
        pp = [st.ps(f"pp{i}", [P, W]) for i in range(4)]
        s_w, s_p, s_ev, s_own, s_sc, s_ex = (st.sem(n) for n in ("w", "p", "ev", "own", "sc", "ex"))
        block = st.block()

        def q(s, b):
            return qkv[:, s * NB + b, 0:H16 * HD].rearrange("p (g r d) -> p g r d", g=HK, r=R)

        def kv(s, b, which):
            lo = (H16 + which * HK) * HD
            v = qkv[:, s * NB + b, lo:lo + HK * HD].rearrange("p (g d) -> p g d", g=HK)
            return v.unsqueeze(2).to_broadcast([P, HK, R, HD])

        @block.sync
        def _(sp):
            sp.dma_start(w[:, :, :], cols(wqkv)).then_inc(s_w, 16)

        @block.tensor
        def _(pe):
            pe.wait_ge(s_w, 16)
            for t in range(NT):
                if t >= 4:
                    pe.wait_ge(s_ev, t - 3)
                for c in range(DC):
                    last = nc.tensor.matmul(pp[t % 4][:, :], srcT[:, c, t * P:(t + 1) * P], w[:, c, :],
                                            start=(c == 0), stop=(c == DC - 1))
                last.then_inc(s_p, 1)

        @block.scalar
        def _(act):
            for t in range(NT):
                act.wait_ge(s_p, t + 1)
                nc.scalar.activation(qkv[:, t, :], pp[t % 4][:, :], ACT.Identity).then_inc(s_ev, 1)
            act.wait_ge(s_sc, 1)
            nc.scalar.activation(sc[:, :, :], sc[:, :, :], ACT.Exp, scale=HD ** -0.5).then_inc(s_ex, 1)

        @block.vector
        def _(dve):
            own = InOrder(dve, s_own)
            dve.wait_ge(s_ev, NT)
            for i, (s, t) in enumerate(PAIRS):
                for b in range(NB):
                    last = nc.vector.tensor_tensor(prod[:, i % 2, b, :].rearrange("p (g r d) -> p g r d", g=HK, r=R),
                                                   q(s, b), kv(t, b, 0), ALU.mult)
                own.after(last)
                last = nc.vector.tensor_reduce(sc[:, i, :], prod[:, i % 2, :, :].rearrange("p b (h d) -> p (b h) d", h=H16),
                                        AX.X, ALU.add)
            own.after(last)
            first = [s * (s + 1) // 2 for s in range(SL + 1)]
            for s in range(SL):
                last = nc.vector.tensor_reduce(mx[:, s, :], sc[:, first[s]:first[s + 1], :].rearrange("p t n -> p n t"),
                                               AX.X, ALU.max)
            own.after(last)
            for s in range(SL):
                v = sc[:, first[s]:first[s + 1], :]
                last = nc.vector.tensor_tensor(v, v, mx[:, s, :].unsqueeze(1).to_broadcast([P, s + 1, NB * H16]),
                                               ALU.subtract)
            last.then_inc(s_sc, 1)
            dve.wait_ge(s_ex, 1)
            for s in range(SL):
                last = nc.vector.tensor_reduce(mx[:, s, :], sc[:, first[s]:first[s + 1], :].rearrange("p t n -> p n t"),
                                               AX.X, ALU.add)
            own.after(last)
            own.after(nc.vector.reciprocal(mx[:, :, :], mx[:, :, :]))
            for s in range(SL):
                v = sc[:, first[s]:first[s + 1], :]
                last = nc.vector.tensor_tensor(v, v, mx[:, s, :].unsqueeze(1).to_broadcast([P, s + 1, NB * H16]),
                                               ALU.mult)
            own.after(last)
            for i, (s, t) in enumerate(PAIRS):
                prob = sc[:, i, :].rearrange("p (b g r) -> p b g r", b=NB, g=HK)
                for b in range(NB):
                    dst = att[:, s * NB + b, :] if t == 0 else prod[:, i % 2, b, :]
                    last = nc.vector.tensor_tensor(dst.rearrange("p (g r d) -> p g r d", g=HK, r=R), kv(t, b, 1),
                                                   prob[:, b].unsqueeze(3).to_broadcast([P, HK, R, HD]), ALU.mult)
                own.after(last)
                if t > 0:
                    a = att[:, s * NB:(s + 1) * NB, :]
                    last = nc.vector.tensor_tensor(a, a, prod[:, i % 2, :, :], ALU.add)
            own.after(last)


def project_rows(nc, name, srcT, w_dram, tiles_out):
    with Stage(nc, name) as st:
        K = w_dram.shape[0] // P
        w = st.sb("w", [P, K, w_dram.shape[1]])
        pp = [st.ps(f"pp{i}", [P, w_dram.shape[1]]) for i in range(4)]
        s_w, s_p, s_ev, s_own = (st.sem(n) for n in ("w", "p", "ev", "own"))
        block = st.block()

        @block.sync
        def _(sp):
            sp.dma_start(w[:, :, :], cols(w_dram)).then_inc(s_w, 16)

        @block.tensor
        def _(pe):
            pe.wait_ge(s_w, 16)
            for t in range(NT):
                if t >= 4:
                    pe.wait_ge(s_ev, t - 3)
                for c in range(K):
                    last = nc.tensor.matmul(pp[t % 4][:, :], srcT[:, c, t * P:(t + 1) * P], w[:, c, :],
                                            start=(c == 0), stop=(c == K - 1))
                last.then_inc(s_p, 1)

        @block.vector
        def _(dve):
            own = InOrder(dve, s_own)
            for t in range(NT):
                dve.wait_ge(s_p, t + 1)
                tiles_out(own, t, pp[t % 4][:, :]).then_inc(s_ev, 1)


def route(nc, name, logits, K, weights, iota, over_all=False, capacity=None, tri=None, ones=None, spare=None,
          slots=None):
    E = logits.shape[2]
    with Stage(nc, name) as st:
        top = st.sb("top", [P, NT, 8])
        idx = st.sb("idx", [P, NT, 8], U32)
        idf = st.sb("idf", [P, NT, K])
        et = st.sb("et", [P, NT, 8])
        ea = st.sb("ea", [P, NT, E])
        den = st.sb("den", [P, NT])
        hot = st.sb("hot", [P, K, NT, E])
        s_own, s_sub, s_exp, s_hot, s_rank = (st.sem(n) for n in ("own", "sub", "exp", "hot", "rank"))
        if capacity:
            rs = st.sb("rs", [P, K, NT])
            keep = st.sb("keep", [P, K, NT])
            sl = st.sb("sl", [P, K, NT])
            sp_ = st.sb("spare", [P, K, NT])
            s_sp = st.sem("sp")
            hotb = st.sb("hotb", [P, K, NT, E], BF16)
            seen = st.sb("seen", [P, K, NT, E], BF16)
            rank = st.ps("rank", [P, K, NT, E])
        block = st.block()

        if capacity:
            @block.sync
            def _(sp):
                sp.dma_start(sp_[:, :, :], spare).then_inc(s_sp, 16)

        @block.vector
        def _(dve):
            own = InOrder(dve, s_own)
            for t in range(NT):
                last = nc.vector.max(top[:, t, :], logits[:, t, :])
            own.after(last)
            for t in range(NT):
                nc.vector.max_index(idx[:, t, :], top[:, t, :], logits[:, t, :])
            best = top[:, :, 0:1]
            if over_all:
                nc.vector.tensor_tensor(ea[:, :, :], logits[:, :, :], best.to_broadcast([P, NT, E]), ALU.subtract)
            nc.vector.tensor_tensor(et[:, :, :], top[:, :, :], best.to_broadcast([P, NT, 8]), ALU.subtract
                                    ).then_inc(s_sub, 1)
            dve.wait_ge(s_sub, 1)
            own.after(nc.vector.tensor_copy(idf[:, :, :], idx[:, :, 0:K]))
            for k in range(K):
                last = nc.vector.tensor_tensor(hot[:, k, :, :], iota[:, 0:E].unsqueeze(1).to_broadcast([P, NT, E]),
                                        idf[:, :, k:k + 1].to_broadcast([P, NT, E]), ALU.is_equal)
            own.after(last)
            if capacity:
                own.after(nc.vector.tensor_copy(hotb[:, :, :, :], hot[:, :, :, :]))
                own.after(nc.vector.memset(seen[:, :, 0, :], 0.0))
                for t in range(1, NT):
                    own.after(nc.vector.tensor_tensor(seen[:, :, t, :], seen[:, :, t - 1, :], hotb[:, :, t - 1, :],
                                                      ALU.add))
                nc.vector.memset(den[:, :], 0.0).then_inc(s_hot, 1)
                dve.wait_ge(s_rank, 1)
                own.after(nc.vector.tensor_tensor(hot[:, :, :, :], rank[:, :, :, :], hot[:, :, :, :], ALU.mult))
                own.after(nc.vector.tensor_reduce(rs[:, :, :], hot[:, :, :, :], AX.X, ALU.add))
                own.after(nc.vector.tensor_scalar(keep[:, :, :], rs[:, :, :], float(capacity), None, ALU.is_lt))
                for k in range(K):
                    last = nc.vector.scalar_tensor_tensor(sl[:, k, :], idf[:, :, k], float(K * capacity), rs[:, k, :],
                                                          ALU.mult, ALU.add)
                own.after(last)
                for k in range(1, K):
                    own.after(nc.vector.tensor_scalar(sl[:, k, :], sl[:, k, :], float(k * capacity), None, ALU.add))
                own.after(nc.vector.tensor_tensor(sl[:, :, :], sl[:, :, :], keep[:, :, :], ALU.mult))
                nc.vector.tensor_copy(slots[1][:, :, :], sl[:, :, :])
                dve.wait_ge(s_sp, 16)
                own.after(nc.vector.tensor_scalar(rs[:, :, :], keep[:, :, :], 0.0, None, ALU.is_equal))
                own.after(nc.vector.tensor_tensor(rs[:, :, :], rs[:, :, :], sp_[:, :, :], ALU.mult))
                own.after(nc.vector.tensor_tensor(sl[:, :, :], sl[:, :, :], rs[:, :, :], ALU.add))
                nc.vector.tensor_copy(slots[0][:, :, :], sl[:, :, :])
            dve.wait_ge(s_exp, 1)
            own.after(nc.vector.tensor_reduce(den[:, :], ea[:, :, :] if over_all else et[:, :, 0:K], AX.X, ALU.add))
            own.after(nc.vector.reciprocal(den[:, :], den[:, :]))
            own.after(nc.vector.tensor_tensor(et[:, :, 0:K], et[:, :, 0:K],
                                              den[:, :].unsqueeze(2).to_broadcast([P, NT, K]), ALU.mult))
            if capacity:
                for k in range(K):
                    nc.vector.tensor_tensor(weights[:, :, k], et[:, :, k], keep[:, k, :], ALU.mult)
                return
            for k in range(K):
                last = nc.vector.tensor_tensor(hot[:, k, :, :], hot[:, k, :, :],
                                               et[:, :, k:k + 1].to_broadcast([P, NT, E]), ALU.mult)
            own.after(last)
            own.after(nc.vector.tensor_tensor(weights, hot[:, 0, :, :], hot[:, 1, :, :], ALU.add))
            for k in range(2, K):
                own.after(nc.vector.tensor_tensor(weights, weights, hot[:, k, :, :], ALU.add))

        @block.scalar
        def _(act):
            act.wait_ge(s_sub, 1)
            if over_all:
                nc.scalar.activation(ea[:, :, :], ea[:, :, :], ACT.Exp)
            nc.scalar.activation(et[:, :, :], et[:, :, :], ACT.Exp).then_inc(s_exp, 1)

        if capacity:
            @block.tensor
            def _(pe):
                pe.wait_ge(s_hot, 1)
                for k in range(K):
                    for t in range(NT):
                        nc.tensor.matmul(rank[:, k, t, :], tri[:, :], hotb[:, k, t, :], start=True, stop=False)
                        last = nc.tensor.matmul(rank[:, k, t, :], ones[:, :], seen[:, k, t, :], start=False, stop=True)
                last.then_inc(s_rank, 1)


def experts(nc, name, xT, w1, w2, weights, x, func, w1u=None, w_of=None, beside=None):
    E, _, F = w1.shape
    FT = F // P
    NS = E * B
    w_of = w_of or (lambda e: e)
    with Stage(nc, name) as st:
        wa = st.sb("wa", [P, 2, DC, F])
        wu = st.sb("wu", [P, 2, DC, F]) if w1u is not None else None
        wd = st.sb("wd", [P, 2, FT, D])
        hT = st.sb("hT", [P, 2, FT, S])
        NU = 4 if w1u is None else 2
        up = [st.ps(f"up{i}", [P, 4 // NU, S]) for i in range(NU)]
        down = [st.ps(f"down{i}", [P, D]) for i in range(4)]
        sg = st.sb("sg", [P, 2, S]) if w1u is not None else None
        s_w = [st.sem(f"w{i}") for i in range(2)]
        s_up, s_h, s_dn, s_x, s_sg, s_ld, s_out = (st.sem(n) for n in ("up", "h", "dn", "x", "sg", "ld", "out"))
        NW = 2 if w1u is None else 3
        block = st.block()

        @block.sync
        def _(sp):
            for e in range(E):
                if e >= 2:
                    sp.wait_ge(s_dn, NT * (e - 1))
                sp.dma_start(wa[:, e % 2, :, :], cols(w1[e])).then_inc(s_w[e % 2], 16)
                if w1u is not None:
                    sp.dma_start(wu[:, e % 2, :, :], cols(w1u[e])).then_inc(s_w[e % 2], 16)
                sp.dma_start(wd[:, e % 2, :, :], cols(w2[e])).then_inc(s_w[e % 2], 16)
            if beside is not None:
                for dst, src in beside[3]:
                    sp.dma_start(dst, src).then_inc(s_ld, 16)
                sp.wait_ge(s_ld, 16 * len(beside[3]))

        if beside is not None:
            @block.gpsimd
            def _(pool):
                scatter_rows(pool, s_out, *beside[:3])

        @block.tensor
        def _(pe):
            def go_up(n):
                e, g = n // B, n % B
                if g == 0:
                    pe.wait_ge(s_w[e % 2], 16 * NW * (e // 2 + 1))
                for f in range(FT):
                    k = n * FT + f
                    if k >= NU:
                        pe.wait_ge(s_h, k - NU + 1)
                    for j, w in enumerate([wa] if w1u is None else [wa, wu]):
                        for c in range(DC):
                            last = nc.tensor.matmul(up[k % NU][:, j, :], w[:, e % 2, c, f * P:(f + 1) * P],
                                                    xT[:, c, g * S:(g + 1) * S], start=(c == 0), stop=(c == DC - 1))
                    last.then_inc(s_up, 1)

            def go_down(n):
                e = n // B
                pe.wait_ge(s_h, FT * (n + 1))
                for i in range(QT):
                    m = n * QT + i
                    if m >= 4:
                        pe.wait_ge(s_x, m - 3)
                    for f in range(FT):
                        last = nc.tensor.matmul(down[m % 4][:, :], hT[:, n % 2, f, i * P:(i + 1) * P],
                                                wd[:, e % 2, f, :], start=(f == 0), stop=(f == FT - 1))
                    last.then_inc(s_dn, 1)

            for n in range(NS + 1):
                if n < NS:
                    go_up(n)
                if n >= 1:
                    go_down(n - 1)

        @block.scalar
        def _(act):
            for k in range(NS * FT):
                n, f = k // FT, k % FT
                act.wait_ge(s_up, k + 1)
                if w1u is None:
                    if n >= 2:
                        act.wait_ge(s_dn, QT * (n - 1))
                    nc.scalar.activation(hT[:, n % 2, f, :], up[k % NU][:, 0, :], func).then_inc(s_h, 1)
                else:
                    if k >= 2:
                        act.wait_ge(s_h, k - 1)
                    nc.scalar.activation(sg[:, k % 2, :], up[k % NU][:, 0, :], func).then_inc(s_sg, 1)

        @block.vector
        def _(dve):
            def gate(n):
                for f in range(FT):
                    k = n * FT + f
                    dve.wait_ge(s_sg, k + 1)
                    if n >= 2:
                        dve.wait_ge(s_dn, QT * (n - 1))
                    nc.vector.tensor_tensor(hT[:, n % 2, f, :], sg[:, k % 2, :], up[k % NU][:, 1, :], ALU.mult
                                            ).then_inc(s_h, 1)

            for n in range(NS + 1):
                if w1u is not None and n < NS:
                    gate(n)
                if n == 0:
                    continue
                for i in range(QT):
                    m = (n - 1) * QT + i
                    t, e = m % NT, m // NT
                    dve.wait_ge(s_dn, m + 1)
                    if m >= NT:
                        dve.wait_ge(s_x, m - NT + 1)
                    nc.vector.scalar_tensor_tensor(x[:, t, :], down[m % 4][:, :], weights[:, t, w_of(e):w_of(e) + 1],
                                                   x[:, t, :], ALU.mult, ALU.add).then_inc(s_x, 1)


def route_tiles(nc, name, logits, wk, slots, expert_of, iota, tri, ones, over_all):
    E, K = logits.shape[2], wk.shape[2]
    NTILE = expert_of.shape[1]
    with Stage(nc, name) as st:
        top = st.sb("top", [P, NT, 8])
        idx = st.sb("idx", [P, NT, 8], U32)
        idf = st.sb("idf", [P, NT, K])
        et = st.sb("et", [P, NT, 8])
        ea = st.sb("ea", [P, NT, E])
        den = st.sb("den", [P, NT])
        hot = st.sb("hot", [P, K * NT, E])
        hotb = st.sb("hotb", [P, K * NT, E], BF16)
        seen = st.sb("seen", [P, K * NT, E], BF16)
        count = st.sb("count", [P, E])
        fills = st.sb("fills", [P, E, NT])
        tiles = st.sb("tiles", [P, E])
        start = st.sb("start", [P, E])
        begun = st.sb("begun", [P, NTILE, E - 1])
        last_begun = st.sb("last_begun", [P, NTILE])
        place = st.sb("place", [P, K * NT, E])
        sl = st.sb("sl", [P, K * NT])
        rank = st.ps("rank", [P, K * NT, E])
        total = st.ps("total", [P, E])
        s_own, s_sub, s_exp, s_hot, s_rank, s_total = (
            st.sem(n) for n in ("own", "sub", "exp", "hot", "rank", "total"))
        block = st.block()

        @block.vector
        def _(dve):
            own = InOrder(dve, s_own)
            for t in range(NT):
                last = nc.vector.max(top[:, t, :], logits[:, t, :])
            own.after(last)
            for t in range(NT):
                last = nc.vector.max_index(idx[:, t, :], top[:, t, :], logits[:, t, :])
            best = top[:, :, 0:1]
            if over_all:
                nc.vector.tensor_tensor(ea[:, :, :], logits[:, :, :], best.to_broadcast([P, NT, E]), ALU.subtract)
            nc.vector.tensor_tensor(et[:, :, :], top[:, :, :], best.to_broadcast([P, NT, 8]), ALU.subtract
                                    ).then_inc(s_sub, 1)
            dve.wait_ge(s_sub, 1)
            own.after(nc.vector.tensor_copy(idf[:, :, :], idx[:, :, 0:K]))
            for k in range(K):
                last = nc.vector.tensor_tensor(hot[:, k * NT:(k + 1) * NT, :],
                                               iota[:, 0:E].unsqueeze(1).to_broadcast([P, NT, E]),
                                               idf[:, :, k:k + 1].to_broadcast([P, NT, E]), ALU.is_equal)
            own.after(last)
            own.after(nc.vector.tensor_copy(hotb[:, :, :], hot[:, :, :]))
            own.after(nc.vector.memset(seen[:, 0, :], 0.0))
            for i in range(1, K * NT):
                own.after(nc.vector.tensor_tensor(seen[:, i, :], seen[:, i - 1, :], hotb[:, i - 1, :], ALU.add))
            nc.vector.memset(start[:, :], 0.0).then_inc(s_hot, 1)
            dve.wait_ge(s_total, 1)
            own.after(nc.vector.tensor_scalar(count[:, :], total[:, :], 1.0 / P, None, ALU.mult))
            own.after(nc.vector.tensor_tensor(fills[:, :, :], count[:, :].unsqueeze(2).to_broadcast([P, E, NT]),
                                              iota[:, 0:NT].unsqueeze(1).to_broadcast([P, E, NT]), ALU.is_gt))
            own.after(nc.vector.tensor_reduce(tiles[:, :], fills[:, :, :], AX.X, ALU.add))
            for e in range(1, E):
                own.after(nc.vector.tensor_tensor(start[:, e:e + 1], start[:, e - 1:e], tiles[:, e - 1:e], ALU.add))
            own.after(nc.vector.tensor_tensor(begun[:, :, :], start[:, 1:E].unsqueeze(1).to_broadcast([P, NTILE, E - 1]),
                                              iota[:, 0:NTILE].unsqueeze(2).to_broadcast([P, NTILE, E - 1]), ALU.is_le))
            own.after(nc.vector.tensor_reduce(last_begun[:, :], begun[:, :, :], AX.X, ALU.add))
            nc.vector.tensor_copy(expert_of[:, :], last_begun[:, :])
            own.after(nc.vector.tensor_scalar(count[:, :], start[:, :], float(P), None, ALU.mult))
            dve.wait_ge(s_rank, 1)
            own.after(nc.vector.tensor_tensor(place[:, :, :], rank[:, :, :],
                                              count[:, :].unsqueeze(1).to_broadcast([P, K * NT, E]), ALU.add))
            own.after(nc.vector.tensor_tensor(place[:, :, :], place[:, :, :], hot[:, :, :], ALU.mult))
            own.after(nc.vector.tensor_reduce(sl[:, :], place[:, :, :], AX.X, ALU.add))
            nc.vector.tensor_copy(slots[:, :, :].rearrange("p k t -> p (k t)"), sl[:, :])
            dve.wait_ge(s_exp, 1)
            own.after(nc.vector.tensor_reduce(den[:, :], ea[:, :, :] if over_all else et[:, :, 0:K], AX.X, ALU.add))
            own.after(nc.vector.reciprocal(den[:, :], den[:, :]))
            nc.vector.tensor_tensor(wk[:, :, :], et[:, :, 0:K], den[:, :].unsqueeze(2).to_broadcast([P, NT, K]), ALU.mult)

        @block.scalar
        def _(act):
            act.wait_ge(s_sub, 1)
            if over_all:
                nc.scalar.activation(ea[:, :, :], ea[:, :, :], ACT.Exp)
            nc.scalar.activation(et[:, :, :], et[:, :, :], ACT.Exp).then_inc(s_exp, 1)

        @block.tensor
        def _(pe):
            pe.wait_ge(s_hot, 1)
            n = K * NT - 1
            nc.tensor.matmul(total[:, :], ones[:, :], seen[:, n, :], start=True, stop=False)
            nc.tensor.matmul(total[:, :], ones[:, :], hotb[:, n, :], start=False, stop=True).then_inc(s_total, 1)
            for i in range(K * NT):
                nc.tensor.matmul(rank[:, i, :], tri[:, :], hotb[:, i, :], start=True, stop=False)
                last = nc.tensor.matmul(rank[:, i, :], ones[:, :], seen[:, i, :], start=False, stop=True)
            last.then_inc(s_rank, 1)


def tile_experts(nc, name, xs, ys, expert_of, wa, wd, func, gated, ident, affine=None):
    F = wa.shape[3]
    FT = wd.shape[2]
    H = FT * P
    E = wa.shape[1]
    N = expert_of.shape[1] - 1
    GR = 4
    NGR = -(-N // GR)
    with Stage(nc, name) as st:
        xr = st.sb("xr", [P, 2, GR, D])
        xT = st.sb("xT", [P, 2, DC, P])
        h = st.sb("h", [P, 2, H])
        hT = st.sb("hT", [P, 2, FT, P])
        y = st.sb("y", [P, 2, GR, D])
        sg = st.sb("sg", [P, 2, H])
        wb = st.sb("wb", [P, 2, DC])
        tp = [st.ps(f"tp{i}", [P, DC * P]) for i in range(2)]
        up = [st.ps(f"up{i}", [P, F]) for i in range(2)]
        th = [st.ps(f"th{i}", [P, H]) for i in range(2)]
        down = [st.ps(f"down{i}", [P, D]) for i in range(2)]
        s_xr = [st.sem(f"xr{i}") for i in range(2)]
        s_st = [st.sem(f"st{i}") for i in range(2)]
        s_tr, s_xt, s_up, s_sg, s_h, s_th, s_ht, s_dn, s_y, s_wb = (
            st.sem(n) for n in ("tr", "xt", "up", "sg", "h", "th", "ht", "dn", "y", "wb"))
        block = st.block()

        @block.sync
        def _(sp):
            if affine is not None:
                for i in range(2):
                    for c in range(DC):
                        sp.dma_start(wb[:, i, c:c + 1], affine[i][c * P:(c + 1) * P].unsqueeze(1)).then_inc(s_wb, 16)
            for g in range(NGR):
                if g >= 2:
                    sp.wait_ge(s_tr, GR * (g - 1))
                sp.dma_start(xr[:, g % 2, :, :], rows(xs[g * GR * P:(g + 1) * GR * P, :])).then_inc(s_xr[g % 2], 16)

        @block.gpsimd
        def _(pool):
            for g in range(NGR):
                n = min(GR, N - g * GR)
                pool.wait_ge(s_y, g * GR + n)
                pool.dma_start(rows(ys[g * GR * P:(g * GR + n) * P, :]), y[:, g % 2, 0:n, :]).then_inc(s_st[g % 2], 16)
            for i in range(2):
                pool.wait_ge(s_st[i], 16 * ((NGR - i + 1) // 2))

        @block.tensor
        def _(pe):
            def turn(j):
                g = j // GR
                pe.wait_ge(s_xr[g % 2], 16 * (g // 2 + 1))
                if j >= 2:
                    pe.wait_ge(s_xt, j - 1)
                for c in range(DC):
                    last = nc.tensor.transpose(tp[j % 2][:, c * P:(c + 1) * P], xr[:, g % 2, j % GR, c * P:(c + 1) * P],
                                               ident[:, :])
                last.then_inc(s_tr, 1)

            def go_up(j):
                pe.wait_ge(s_xt, j + 1)
                if j >= 2:
                    pe.wait_ge(s_h, j - 1)
                e = pe.value_load(expert_of[0:1, j:j + 1], min_val=0, max_val=E - 1)
                for c in range(DC):
                    last = nc.tensor.matmul(up[j % 2][:, :], xT[:, j % 2, c, :],
                                            wa[:, bass.ds(e, 1), c, :].rearrange("p e f -> p (e f)"),
                                            start=(c == 0), stop=(c == DC - 1))
                last.then_inc(s_up, 1)

            def turn_hidden(j):
                pe.wait_ge(s_h, j + 1)
                if j >= 2:
                    pe.wait_ge(s_ht, j - 1)
                for f in range(FT):
                    last = nc.tensor.transpose(th[j % 2][:, f * P:(f + 1) * P], h[:, j % 2, f * P:(f + 1) * P], ident[:, :])
                last.then_inc(s_th, 1)

            def go_down(j):
                pe.wait_ge(s_ht, j + 1)
                if j >= 2:
                    pe.wait_ge(s_y, j - 1)
                e = pe.value_load(expert_of[0:1, j:j + 1], min_val=0, max_val=E - 1)
                for f in range(FT):
                    last = nc.tensor.matmul(down[j % 2][:, :], hT[:, j % 2, f, :],
                                            wd[:, bass.ds(e, 1), f, :].rearrange("p e f -> p (e f)"),
                                            start=(f == 0), stop=(f == FT - 1))
                last.then_inc(s_dn, 1)

            for s in range(N + 3):
                if s < N:
                    turn(s)
                if 1 <= s < N + 1:
                    go_up(s - 1)
                if 2 <= s < N + 2:
                    turn_hidden(s - 2)
                if s >= 3:
                    go_down(s - 3)

        @block.scalar
        def _(act):
            for j in range(N):
                act.wait_ge(s_up, j + 1)
                if gated:
                    if j >= 2:
                        act.wait_ge(s_h, j - 1)
                    nc.scalar.activation(sg[:, j % 2, :], up[j % 2][:, 0:H], func).then_inc(s_sg, 1)
                else:
                    if j >= 2:
                        act.wait_ge(s_th, j - 1)
                    nc.scalar.activation(h[:, j % 2, :], up[j % 2][:, :], func).then_inc(s_h, 1)

        @block.vector
        def _(dve):
            if affine is not None:
                dve.wait_ge(s_wb, 16 * 2 * DC)
            for s in range(N + 3):
                if s < N:
                    j = s
                    dve.wait_ge(s_tr, j + 1)
                    if j >= 2:
                        dve.wait_ge(s_up, j - 1)
                    if affine is None:
                        nc.vector.tensor_copy(xT[:, j % 2, :, :], tp[j % 2][:, :].rearrange("p (c n) -> p c n", c=DC)
                                              ).then_inc(s_xt, 1)
                    else:
                        for c in range(DC):
                            last = nc.vector.tensor_scalar(xT[:, j % 2, c, :], tp[j % 2][:, c * P:(c + 1) * P],
                                                           wb[:, 0, c:c + 1], wb[:, 1, c:c + 1], ALU.mult, ALU.add)
                        last.then_inc(s_xt, 1)
                if gated and 1 <= s < N + 1:
                    j = s - 1
                    dve.wait_ge(s_sg, j + 1)
                    if j >= 2:
                        dve.wait_ge(s_th, j - 1)
                    nc.vector.tensor_tensor(h[:, j % 2, :], sg[:, j % 2, :], up[j % 2][:, H:2 * H], ALU.mult
                                            ).then_inc(s_h, 1)
                if 2 <= s < N + 2:
                    j = s - 2
                    dve.wait_ge(s_th, j + 1)
                    if j >= 2:
                        dve.wait_ge(s_dn, j - 1)
                    nc.vector.tensor_copy(hT[:, j % 2, :, :], th[j % 2][:, :].rearrange("p (f n) -> p f n", f=FT)
                                          ).then_inc(s_ht, 1)
                if s >= 3:
                    j = s - 3
                    g = j // GR
                    dve.wait_ge(s_dn, j + 1)
                    if g >= 2:
                        dve.wait_ge(s_st[g % 2], 16 * (g // 2))
                    nc.vector.tensor_copy(y[:, g % 2, j % GR, :], down[j % 2][:, :]).then_inc(s_y, 1)


def scatter_rows(pool, s_out, xn, slots, xs):
    K = slots.shape[1]
    for t in range(NT):
        for k in range(K):
            pool.indirect_dma_start(xs[:, :], bass.IndirectOffsetOnAxis(slots[:, k, t:t + 1], 0),
                                    xn[:, t, :], None).then_inc(s_out, 16)
    pool.wait_ge(s_out, 16 * NT * K)


def dispatch(nc, name, xn, slots, xs, loads=(), zeroed=None):
    with Stage(nc, name) as st:
        s_out, s_ld = st.sem("out"), st.sem("ld")
        block = st.block()

        @block.sync
        def _(sp):
            for dst, src in loads:
                sp.dma_start(dst, src).then_inc(s_ld, 16)
            if loads:
                sp.wait_ge(s_ld, 16 * len(loads))

        @block.gpsimd
        def _(pool):
            if zeroed is not None:
                pool.wait_ge(zeroed, 16 * ZEROING)
            scatter_rows(pool, s_out, xn, slots, xs)


def combine(nc, name, ys, slots, wk, x, vec):
    K = slots.shape[1]
    R = 4
    with Stage(nc, name) as st:
        vb = st.sb("vb", [P, D])
        y = st.sb("y", [P, R, K, D])
        s_vb, s_b, s_x = (st.sem(n) for n in ("vb", "b", "x"))
        s_y = [st.sem(f"y{i}") for i in range(R)]
        block = st.block()

        if vec is not None:
            @block.sync
            def _(sp):
                sp.dma_start(vb[:, :], vec.partition_broadcast(P)).then_inc(s_vb, 16)

        @block.gpsimd
        def _(pool):
            for t in range(NT):
                if t >= R:
                    pool.wait_ge(s_x, K * (t - R + 1))
                for k in range(K):
                    pool.indirect_dma_start(y[:, t % R, k, :], None, ys[:, :],
                                            bass.IndirectOffsetOnAxis(slots[:, k, t:t + 1], 0)).then_inc(s_y[t % R], 16)

        @block.vector
        def _(dve):
            if vec is not None:
                dve.wait_ge(s_vb, 16)
                for t in range(NT):
                    nc.vector.tensor_tensor(x[:, t, :], x[:, t, :], vb[:, :], ALU.add).then_inc(s_b, 1)
            for t in range(NT):
                dve.wait_ge(s_y[t % R], 16 * K * (t // R + 1))
                if vec is not None:
                    dve.wait_ge(s_b, t + 1)
                for k in range(K):
                    if k:
                        dve.wait_ge(s_x, K * t + k)
                    nc.vector.scalar_tensor_tensor(x[:, t, :], y[:, t % R, k, :], wk[:, t, k:k + 1], x[:, t, :],
                                                   ALU.mult, ALU.add).then_inc(s_x, 1)


def slot_experts(nc, name, xs, ys, w1, w2, func, ident):
    E, _, F = w1.shape
    FT = F // P
    with Stage(nc, name) as st:
        wa = st.sb("wa", [P, 2, DC, F])
        wd = st.sb("wd", [P, 2, FT, D])
        xr = st.sb("xr", [P, 2, QT, D])
        xT = st.sb("xT", [P, 2, DC, S])
        hT = st.sb("hT", [P, 2, FT, S])
        y = st.sb("y", [P, 2, QT, D])
        NU = 3
        up = [st.ps(f"up{i}", [P, S]) for i in range(NU)]
        tp = st.ps("tp", [P, S])
        down = [st.ps(f"down{i}", [P, D]) for i in range(4)]
        s_wd = [st.sem(f"wd{i}") for i in range(2)]
        s_w = [st.sem(f"w{i}") for i in range(2)]
        s_xr = [st.sem(f"xr{i}") for i in range(2)]
        s_st = [st.sem(f"st{i}") for i in range(2)]
        s_tr, s_xt, s_up, s_h, s_dn, s_y = (st.sem(n) for n in ("tr", "xt", "up", "h", "dn", "y"))
        block = st.block()

        @block.sync
        def _(sp):
            for e in range(E):
                if e >= 2:
                    sp.wait_ge(s_tr, DC * (e - 1))
                sp.dma_start(xr[:, e % 2, :, :], rows(xs[e * S:(e + 1) * S, :])).then_inc(s_xr[e % 2], 16)
                if e >= 2:
                    sp.wait_ge(s_up, FT * (e - 1))
                sp.dma_start(wa[:, e % 2, :, :], cols(w1[e])).then_inc(s_w[e % 2], 16)
                if e >= 2:
                    sp.wait_ge(s_dn, QT * (e - 1))
                sp.dma_start(wd[:, e % 2, :, :], cols(w2[e])).then_inc(s_wd[e % 2], 16)

        @block.gpsimd
        def _(pool):
            for e in range(E):
                pool.wait_ge(s_y, QT * (e + 1))
                pool.dma_start(rows(ys[e * S:(e + 1) * S, :]), y[:, e % 2, :, :]).then_inc(s_st[e % 2], 16)
            for i in range(2):
                pool.wait_ge(s_st[i], 16 * (E // 2))

        @block.tensor
        def _(pe):
            def turn(e):
                pe.wait_ge(s_xr[e % 2], 16 * (e // 2 + 1))
                for c in range(DC):
                    k = e * DC + c
                    if k >= 1:
                        pe.wait_ge(s_xt, k)
                    for i in range(QT):
                        last = nc.tensor.transpose(tp[:, i * P:(i + 1) * P], xr[:, e % 2, i, c * P:(c + 1) * P],
                                                   ident[:, :])
                    last.then_inc(s_tr, 1)

            def go_up(e):
                pe.wait_ge(s_w[e % 2], 16 * (e // 2 + 1))
                pe.wait_ge(s_xt, DC * (e + 1))
                for f in range(FT):
                    k = e * FT + f
                    if k >= NU:
                        pe.wait_ge(s_h, k - NU + 1)
                    for c in range(DC):
                        last = nc.tensor.matmul(up[k % NU][:, :], wa[:, e % 2, c, f * P:(f + 1) * P],
                                                xT[:, e % 2, c, :], start=(c == 0), stop=(c == DC - 1))
                    last.then_inc(s_up, 1)

            def go_down(e):
                pe.wait_ge(s_wd[e % 2], 16 * (e // 2 + 1))
                pe.wait_ge(s_h, FT * (e + 1))
                for i in range(QT):
                    m = e * QT + i
                    if m >= 4:
                        pe.wait_ge(s_y, m - 3)
                    for f in range(FT):
                        last = nc.tensor.matmul(down[m % 4][:, :], hT[:, e % 2, f, i * P:(i + 1) * P],
                                                wd[:, e % 2, f, :], start=(f == 0), stop=(f == FT - 1))
                    last.then_inc(s_dn, 1)

            turn(0)
            for e in range(E):
                go_up(e)
                if e + 1 < E:
                    turn(e + 1)
                if e >= 1:
                    go_down(e - 1)
            go_down(E - 1)

        @block.scalar
        def _(act):
            for k in range(E * FT):
                e, f = k // FT, k % FT
                act.wait_ge(s_up, k + 1)
                if e >= 2:
                    act.wait_ge(s_dn, QT * (e - 1))
                nc.scalar.activation(hT[:, e % 2, f, :], up[k % NU][:, :], func).then_inc(s_h, 1)

        @block.vector
        def _(dve):
            def turned(e):
                for c in range(DC):
                    dve.wait_ge(s_tr, e * DC + c + 1)
                    if e >= 2:
                        dve.wait_ge(s_up, FT * (e - 1))
                    nc.vector.tensor_copy(xT[:, e % 2, c, :], tp[:, :]).then_inc(s_xt, 1)

            def done(e):
                for i in range(QT):
                    m = e * QT + i
                    dve.wait_ge(s_dn, m + 1)
                    if e >= 2:
                        dve.wait_ge(s_st[e % 2], 16 * (e // 2))
                    nc.vector.tensor_copy(y[:, e % 2, i, :], down[m % 4][:, :]).then_inc(s_y, 1)

            turned(0)
            for e in range(E):
                if e + 1 < E:
                    turned(e + 1)
                if e >= 1:
                    done(e - 1)
            done(E - 1)


HB = 64
NP = H16 * HB // P


def tri_at(k):
    return slice(k * (k + 1) // 2 * P, (k + 1) * (k + 2) // 2 * P)


def causal_masks(nc, name, a, am, uT, sufmax, usum, ident):
    with Stage(nc, name) as st:
        later = st.sb("later", [P, QT, S])
        fill = st.sb("fill", [P, QT, S])
        mb = st.sb("mb", [P, B, S])
        sc = st.sb("sc", [P, 2, S])
        u = st.sb("u", [P, QT, S])
        ns = st.sb("ns", [P, NT])
        tp = [st.ps(f"tp{i}", [P, S]) for i in range(2)]
        s_ld, s_sc, s_mx, s_ns, s_u, s_tr, s_ev, s_am = (
            st.sem(n) for n in ("ld", "sc", "mx", "ns", "u", "tr", "ev", "am"))
        block = st.block()

        @block.sync
        def _(sp):
            sp.dma_start(later[:, :, :], a["c_later"]).then_inc(s_ld, 16)
            sp.dma_start(fill[:, :, :], a["c_fill"]).then_inc(s_ld, 16)
            sp.dma_start(mb[:, :, :].rearrange("p b n -> p (b n)"), a["addm"].partition_broadcast(P)
                         ).then_inc(s_ld, 16)
            sp.wait_ge(s_ld, 48)

        @block.vector
        def _(dve):
            dve.wait_ge(s_ld, 48)
            for m in range(NT):
                b, t = m // QT, m % QT
                nc.vector.tensor_tensor(am[:, b, tri_at(t)], mb[:, b, 0:(t + 1) * P], later[:, t, 0:(t + 1) * P], ALU.add
                                        ).then_inc(s_am, 1)
                if m >= 2:
                    dve.wait_ge(s_u, m - 1)
                nc.vector.tensor_tensor(sc[:, m % 2, :], mb[:, b, :], fill[:, t, :], ALU.add).then_inc(s_sc, 1)
                dve.wait_ge(s_sc, m + 1)
                nc.vector.tensor_reduce(sufmax[:, m:m + 1], sc[:, m % 2, :], AX.X, ALU.max).then_inc(s_mx, 1)
                dve.wait_ge(s_mx, m + 1)
                nc.vector.tensor_scalar(ns[:, m:m + 1], sufmax[:, m:m + 1], -1.0, None, ALU.mult).then_inc(s_ns, 1)

        @block.scalar
        def _(act):
            j = 0
            for m in range(NT):
                b, t = m // QT, m % QT
                act.wait_ge(s_ns, m + 1)
                if b >= 1:
                    act.wait_ge(s_tr, QT * b)
                nc.scalar.activation(u[:, t, :], sc[:, m % 2, :], ACT.Exp, bias=ns[:, m:m + 1],
                                     accum_out=usum[:, m:m + 1]).then_inc(s_u, 1)
                if t == QT - 1:
                    for k in range(QT):
                        act.wait_ge(s_tr, j + 1)
                        nc.scalar.activation(uT[:, b, tri_at(k)], tp[j % 2][:, 0:(k + 1) * P], ACT.Identity
                                             ).then_inc(s_ev, 1)
                        j += 1

        @block.tensor
        def _(pe):
            for j in range(B * QT):
                b, k = j // QT, j % QT
                pe.wait_ge(s_u, QT * (b + 1))
                if j >= 2:
                    pe.wait_ge(s_ev, j - 1)
                for t in range(k + 1):
                    last = nc.tensor.transpose(tp[j % 2][:, t * P:(t + 1) * P], u[:, t, k * P:(k + 1) * P], ident[:, :])
                last.then_inc(s_tr, 1)


def attend64(nc, name, a, xT, cT, masks, x, ident):
    am, uT, sufmax, usum = masks
    N = B * NP
    scale = HB ** -0.5
    TRI = QT * (QT + 1) // 2 * P
    with Stage(nc, name) as st:
        w = [st.sb("w" + k, [P, DC, H16 * HB]) for k in "qkv"]
        wo = st.sb("wo", [P, NP, D])
        bqk = st.sb("bqk", [P, 2, NP])
        bv = st.sb("bv", [P, H16 * HB])
        bo = st.sb("bo", [P, D])
        qT = st.sb("qT", [P, 2, S])
        kT = st.sb("kT", [P, 2, S])
        v = st.sb("v", [P, 2, QT, P])
        wmT = st.sb("wmT", [P, 2, S])
        prob = st.sb("prob", [P, 2, 2, TRI])
        probT = st.sb("probT", [P, 2, QT, S])
        rowmax = st.sb("rowmax", [P, 2, 2, QT])
        neg = st.sb("neg", [P, 2, 2, QT])
        en = st.sb("en", [P, 2, 2, QT])
        em = st.sb("em", [P, 2, 2, QT])
        tot = st.sb("tot", [P, 2, 2, QT])
        den = st.sb("den", [P, QT])
        rec = st.sb("rec", [P, QT])
        share = st.sb("share", [P, 2, QT])
        expand = st.sb("expand", [P, QT, 2, HB])
        t2 = st.sb("t2", [P, S])
        oT = st.sb("oT", [P, NP, S])
        pj = [st.ps(f"pj{i}", [P, S]) for i in range(2)]
        sq = [st.ps(f"sq{i}", [P, S]) for i in range(2)]
        tp = [st.ps(f"tp{i}", [P, S]) for i in range(2)]
        acc = st.ps("acc", [P, S])
        misc = st.ps("misc", [P, S])
        names = "w pj qk v bq wm sq max neg exp em p tr ta td pv ex fb t2 out op x own".split()
        (s_w, s_pj, s_qk, s_v, s_bq, s_wm, s_sq, s_max, s_neg, s_exp, s_em, s_p, s_tr, s_ta, s_td, s_pv, s_ex, s_fb, s_t2,
         s_out, s_op, s_x, s_own) = (st.sem(n) for n in names)
        block = st.block()

        @block.sync
        def _(sp):
            for i, k in enumerate(("WQ", "WK", "WV")):
                sp.dma_start(w[i][:, :, :], cols(a["L1_" + k])).then_inc(s_w, 16)
            sp.dma_start(wo[:, :, :], cols(a["L1_WO"])).then_inc(s_w, 16)
            for i, k in enumerate(("bQ", "bK")):
                sp.dma_start(bqk[:, i, :], a["L1_" + k]).then_inc(s_w, 16)
            sp.dma_start(bv[:, :], a["L1_bV"].partition_broadcast(P)).then_inc(s_w, 16)
            sp.dma_start(bo[:, :], a["L1_bO"].partition_broadcast(P)).then_inc(s_w, 16)
            sp.wait_ge(s_w, 16 * 8)

        @block.tensor
        def _(pe):
            def project(n, which):
                b, p = n // NP, n % NP
                bank = pj[which % 2]
                if which == 0 and n >= 1:
                    pe.wait_ge(s_v, n)
                    if p == 2 and b >= 1:
                        pe.wait_ge(s_x, QT * b)
                if which == 1 and n >= 1:
                    pe.wait_ge(s_wm, n)
                if which == 2:
                    pe.wait_ge(s_qk, 2 * n + 1)
                if which == 3:
                    pe.wait_ge(s_qk, 2 * n + 2)
                    pe.wait_ge(s_v, n + 1)
                if which < 2:
                    src = (xT, cT)[which]
                    for c in range(DC):
                        last = nc.tensor.matmul(bank[:, :], w[which][:, c, p * P:(p + 1) * P], src[:, c, b * S:(b + 1) * S],
                                                start=(c == 0), stop=(c == DC - 1))
                elif which == 2:
                    for t in range(QT):
                        for c in range(DC):
                            last = nc.tensor.matmul(bank[:, t * P:(t + 1) * P], cT[:, c, b * S + t * P:b * S + (t + 1) * P],
                                                    w[2][:, c, p * P:(p + 1) * P], start=(c == 0), stop=(c == DC - 1))
                else:
                    for t in reversed(range(QT)):
                        last = nc.tensor.matmul(bank[:, 0:(t + 1) * P], v[:, n % 2, t, :], uT[:, b, tri_at(t)],
                                                start=(t == QT - 1), stop=(t == 0), skip_group_check=True)
                last.then_inc(s_pj, 1)

            def row_scores(n, i):
                h, t = i // QT, i % QT
                k = n * 8 + i
                if k >= 2:
                    pe.wait_ge(s_max, k - 1)
                if i == 0:
                    pe.wait_ge(s_qk, 2 * n + 2)
                r = slice(h * HB, (h + 1) * HB)
                nc.tensor.matmul(sq[k % 2][:, 0:(t + 1) * P], qT[r, n % 2, t * P:(t + 1) * P],
                                 kT[r, n % 2, 0:(t + 1) * P], start=True, stop=True).then_inc(s_sq, 1)

            def turn(n, i):
                h, t = i // QT, i % QT
                j = n * 8 + i
                pe.wait_ge(s_p, 2 * n + h + 1)
                if j >= 2:
                    jn, jh, jt = (j - 2) // 8, (j - 2) % 8 // QT, (j - 2) % QT
                    pe.wait_ge((s_ta, s_td)[jh], QT * jn + jt + 1)
                for r in range(t, QT):
                    at = tri_at(r).start + t * P
                    last = nc.tensor.transpose(tp[j % 2][:, r * P:(r + 1) * P], prob[:, n % 2, h, at:at + P], ident[:, :])
                last.then_inc(s_tr, 1)

            def values(n):
                pe.wait_ge(s_ta, QT * (n + 1))
                pe.wait_ge(s_td, QT * (n + 1))
                if n >= 1:
                    pe.wait_ge(s_out, n)
                for t in reversed(range(QT)):
                    for h in range(2):
                        last = nc.tensor.matmul(acc[h * HB:(h + 1) * HB, t * P:S], v[:, n % 2, t, h * HB:(h + 1) * HB],
                                                probT[:, h, t, t * P:S], start=(t == QT - 1), stop=(t == 0),
                                                tile_position=(0, h * HB), skip_group_check=True)
                last.then_inc(s_pv, 1)

            def shares(n):
                pe.wait_ge(s_ex, n + 1)
                if n >= 1:
                    pe.wait_ge(s_t2, n)
                for t in range(QT):
                    last = nc.tensor.transpose(misc[:, t * P:(t + 1) * P],
                                               expand[:, t, :, :].rearrange("p h d -> p (h d)"), ident[:, :])
                last.then_inc(s_fb, 1)

            def output(b):
                pe.wait_ge(s_out, NP * (b + 1))
                pe.wait_ge(s_qk, 2 * min(NP * (b + 1) + 2, N))
                pe.wait_ge(s_v, min(NP * (b + 1) + 2, N))
                pe.wait_ge(s_wm, min(NP * (b + 1) + 2, N))
                for i in range(QT):
                    if i >= 2:
                        pe.wait_ge(s_x, QT * b + i - 1)
                    for p in range(NP):
                        last = nc.tensor.matmul(pj[i % 2][:, 0:D], oT[:, p, i * P:(i + 1) * P],
                                                wo[:, p, :], start=(p == 0), stop=(p == NP - 1))
                    last.then_inc(s_op, 1)

            pe.wait_ge(s_w, 16 * 8)
            for n in range(-1, N):
                now, nxt = n >= 0, n + 1 < N
                if nxt:
                    project(n + 1, 0)
                if now:
                    turn(n, 0)
                    turn(n, 1)
                if nxt:
                    project(n + 1, 1)
                if now:
                    turn(n, 2)
                    turn(n, 3)
                if nxt:
                    project(n + 1, 2)
                for i in range(QT):
                    if nxt:
                        row_scores(n + 1, i)
                    if now:
                        turn(n, QT + i)
                if now:
                    shares(n)
                if nxt:
                    project(n + 1, 3)
                    for i in range(QT, 2 * QT):
                        row_scores(n + 1, i)
                if now:
                    values(n)
                    if n % NP == 0 and n >= NP:
                        output(n // NP - 1)
            output(B - 1)

        @block.vector
        def _(dve):
            own = InOrder(dve, s_own)
            dve.wait_ge(s_w, 16 * 8)
            nc.vector.tensor_scalar(bqk[:, 0, :], bqk[:, 0, :], scale, None, ALU.mult).then_inc(s_bq, 1)
            for t in range(NT):
                last = nc.vector.tensor_tensor(x[:, t, :], x[:, t, :], bo[:, :], ALU.add)
            own.after(last)

            def keep_v(n):
                p = n % NP
                dve.wait_ge(s_pj, 4 * n + 3)
                if n >= 2:
                    dve.wait_ge(s_pv, n - 1)
                nc.vector.tensor_tensor(v[:, n % 2, :, :], pj[0][:, :].rearrange("p (t n) -> p t n", t=QT),
                                        bv[:, p * P:(p + 1) * P].unsqueeze(1).to_broadcast([P, QT, P]), ALU.add
                                        ).then_inc(s_v, 1)

            def row_max(n, i):
                h, t = i // QT, i % QT
                k = n * 8 + i
                dve.wait_ge(s_sq, k + 1)
                if n >= 2 and i == 0:
                    dve.wait_ge(s_tr, 8 * (n - 1))
                nc.vector.tensor_tensor_reduce(prob[:, n % 2, h, tri_at(t)], sq[k % 2][:, 0:(t + 1) * P],
                                               am[:, n // NP, tri_at(t)], 1.0, 3.0 * BIG,
                                               ALU.add, ALU.max, rowmax[:, n % 2, h, t:t + 1]).then_inc(s_max, 1)

            def minus_max(n, h):
                suf = sufmax[:, (n // NP) * QT:(n // NP + 1) * QT]
                m, g = rowmax[:, n % 2, h, :], neg[:, n % 2, h, :]
                dve.wait_ge(s_max, 8 * n + QT * (h + 1))
                own.after(nc.vector.tensor_tensor(m, m, suf, ALU.max))
                own.after(nc.vector.tensor_scalar(g, m, -1.0, None, ALU.mult))
                nc.vector.tensor_tensor(en[:, n % 2, h, :], g, suf, ALU.add).then_inc(s_neg, 1)

            def normalize(n, h):
                e = em[:, n % 2, h, :]
                dve.wait_ge(s_em, 2 * n + h + 1)
                own.after(nc.vector.tensor_tensor(den[:, :], e, usum[:, (n // NP) * QT:(n // NP + 1) * QT], ALU.mult))
                own.after(nc.vector.tensor_tensor(den[:, :], den[:, :], tot[:, n % 2, h, :], ALU.add))
                own.after(nc.vector.reciprocal(rec[:, :], den[:, :]))
                if n >= 1:
                    dve.wait_ge(s_ex, n)
                own.after(nc.vector.tensor_tensor(share[:, h, :], e, rec[:, :], ALU.mult))
                for t in range(QT):
                    u = prob[:, n % 2, h, tri_at(t)]
                    last = nc.vector.tensor_scalar(u, u, rec[:, t:t + 1], None, ALU.mult)
                last.then_inc(s_p, 1)
                dve.wait_ge(s_p, 2 * n + h + 1)
                if h == 1:
                    if n >= 1:
                        dve.wait_ge(s_fb, n)
                    nc.vector.tensor_copy(expand[:, :, :, :], share[:, :, :].rearrange("p h t -> p t h").unsqueeze(3)
                                          .to_broadcast([P, QT, 2, HB])).then_inc(s_ex, 1)

            def turned(n, t):
                dve.wait_ge(s_tr, n * 8 + QT + t + 1)
                if n >= 1:
                    dve.wait_ge(s_pv, n)
                nc.vector.tensor_copy(probT[:, 1, t, t * P:S], tp[(QT + t) % 2][:, t * P:S]).then_inc(s_td, 1)

            def finish(n):
                b, p = n // NP, n % NP
                dve.wait_ge(s_fb, n + 1)
                dve.wait_ge(s_wm, n + 1)
                nc.vector.tensor_tensor(t2[:, :], wmT[:, n % 2, :], misc[:, :], ALU.mult).then_inc(s_t2, 1)
                dve.wait_ge(s_t2, n + 1)
                dve.wait_ge(s_pv, n + 1)
                if b >= 1:
                    dve.wait_ge(s_op, QT * b)
                nc.vector.tensor_tensor(oT[:, p, :], acc[:, :], t2[:, :], ALU.add).then_inc(s_out, 1)

            def outputs(b):
                for i in range(QT):
                    m = b * QT + i
                    dve.wait_ge(s_op, m + 1)
                    nc.vector.tensor_tensor(x[:, m, :], x[:, m, :], pj[i % 2][:, 0:D], ALU.add
                                            ).then_inc(s_x, 1)

            for n in range(-1, N):
                now, nxt = n >= 0, n + 1 < N
                if nxt:
                    keep_v(n + 1)
                for i in range(QT):
                    if nxt:
                        row_max(n + 1, i)
                    if now:
                        turned(n, i)
                if nxt:
                    minus_max(n + 1, 0)
                    for i in range(QT, 2 * QT):
                        row_max(n + 1, i)
                    minus_max(n + 1, 1)
                    normalize(n + 1, 0)
                    normalize(n + 1, 1)
                if now:
                    if n % NP == 0 and n >= NP:
                        outputs(n // NP - 1)
                    finish(n)
            outputs(B - 1)

        @block.scalar
        def _(act):
            def exps(n, h):
                act.wait_ge(s_neg, 2 * n + h + 1)
                for t in range(QT):
                    u = prob[:, n % 2, h, tri_at(t)]
                    nc.scalar.activation(u, u, ACT.Exp, bias=neg[:, n % 2, h, t:t + 1],
                                         accum_out=tot[:, n % 2, h, t:t + 1])
                nc.scalar.activation(em[:, n % 2, h, :], en[:, n % 2, h, :], ACT.Exp).then_inc(s_em, 1)

            def keep(n, i):
                act.wait_ge(s_pj, 4 * n + i + 1)
                if n >= 2:
                    act.wait_ge(s_sq, 8 * (n - 1))
                nc.scalar.activation((qT, kT)[i][:, n % 2, :], pj[i][:, :], ACT.Identity,
                                     bias=bqk[:, i, n % NP:n % NP + 1], scale=scale if i == 0 else 1.0
                                     ).then_inc(s_qk, 1)

            act.wait_ge(s_bq, 1)
            for n in range(-1, N):
                now, nxt = n >= 0, n + 1 < N
                if nxt:
                    keep(n + 1, 0)
                if nxt and not now:
                    keep(n + 1, 1)
                if now:
                    for t in range(QT):
                        if t == 2 and nxt:
                            keep(n + 1, 1)
                        act.wait_ge(s_tr, n * 8 + t + 1)
                        if n >= 1:
                            act.wait_ge(s_pv, n)
                        nc.scalar.activation(probT[:, 0, t, t * P:S], tp[t % 2][:, t * P:S], ACT.Identity).then_inc(s_ta, 1)
                if nxt:
                    exps(n + 1, 0)
                    act.wait_ge(s_pj, 4 * (n + 2))
                    if n >= 1:
                        act.wait_ge(s_t2, n)
                    nc.scalar.activation(wmT[:, (n + 1) % 2, :], pj[1][:, :], ACT.Identity).then_inc(s_wm, 1)
                    exps(n + 1, 1)


def similarity(nc, name, a, xnT, cT, crow, hqT, mcol, ident):
    with Stage(nc, name) as st:
        w3 = st.sb("w3", [P, 3, DC])
        bsim = st.sb("bsim", [P, 1])
        e3T = st.sb("e3T", [P, DC, T])
        A = st.sb("A", [P, 2, QT, S])
        AT = st.sb("AT", [P, QT, S])
        neg = st.sb("neg", [P, NT])
        tot = st.sb("tot", [P, NT])
        sc = [st.ps(f"sc{i}", [P, S]) for i in range(2)]
        tp = [st.ps(f"tp{i}", [P, S]) for i in range(2)]
        hq = [st.ps(f"hq{i}", [P, S]) for i in range(2)]
        e1 = st.ps("e1", [P, NT])
        s_w, s_e3, s_sc, s_neg, s_exp, s_A, s_tr, s_at, s_hq, s_ev, s_e1, s_own, s_tot = (
            st.sem(n) for n in ("w", "e3", "sc", "neg", "exp", "A", "tr", "at", "hq", "ev", "e1", "own", "tot"))
        block = st.block()

        @block.sync
        def _(sp):
            sp.dma_start(w3[:, :, :], a["L2_wsim"]).then_inc(s_w, 16)
            sp.dma_start(bsim[:, :], a["L2_bsim"].partition_broadcast(P)).then_inc(s_w, 16)
            sp.wait_ge(s_w, 32)

        @block.tensor
        def _(pe):
            pe.wait_ge(s_w, 32)
            for t in range(NT):
                for c in range(DC):
                    last = nc.tensor.matmul(e1[:, t:t + 1], xnT[:, c, t * P:(t + 1) * P], w3[:, 0, c:c + 1],
                                            start=(c == 0), stop=(c == DC - 1))
            last.then_inc(s_e1, 1)

            def scores(b):
                for t in range(QT):
                    m = b * QT + t
                    pe.wait_ge(s_e3, DC * (b + 1))
                    if m >= 2:
                        pe.wait_ge(s_exp, m - 1)
                    for c in range(DC):
                        last = nc.tensor.matmul(sc[m % 2][:, :], e3T[:, c, m * P:(m + 1) * P], cT[:, c, b * S:(b + 1) * S],
                                                start=(c == 0), stop=(c == DC - 1))
                    last.then_inc(s_sc, 1)

            scores(0)
            for b in range(B):
                if b + 1 < B:
                    scores(b + 1)
                pe.wait_ge(s_A, QT * (b + 1))
                for j in range(QT):
                    k = b * QT + j
                    if k >= 2:
                        pe.wait_ge(s_at, k - 1)
                    for t in range(QT):
                        last = nc.tensor.transpose(tp[k % 2][:, t * P:(t + 1) * P], A[:, b % 2, t, j * P:(j + 1) * P],
                                                   ident[:, :])
                    last.then_inc(s_tr, 1)
                pe.wait_ge(s_at, QT * (b + 1))
                for c in range(DC):
                    if b >= 1:
                        pe.wait_ge(s_ev, DC * (b - 1) + c + 1)
                    for j in range(QT):
                        last = nc.tensor.matmul(hq[c][:, :], crow[:, b * QT + j, c * P:(c + 1) * P], AT[:, j, :],
                                                start=(j == 0), stop=(j == QT - 1))
                    last.then_inc(s_hq, 1)

        @block.vector
        def _(dve):
            own = InOrder(dve, s_own)
            dve.wait_ge(s_w, 32)
            for b in range(B):
                for c in range(DC):
                    nc.vector.tensor_scalar(e3T[:, c, b * S:(b + 1) * S], xnT[:, c, b * S:(b + 1) * S],
                                            w3[:, 2, c:c + 1], w3[:, 1, c:c + 1], ALU.mult, ALU.add).then_inc(s_e3, 1)
            for m in range(NT):
                b, t = m // QT, m % QT
                dve.wait_ge(s_sc, m + 1)
                own.after(nc.vector.tensor_reduce(mcol[:, m:m + 1], sc[m % 2][:, :], AX.X, ALU.max))
                nc.vector.tensor_scalar(neg[:, m:m + 1], mcol[:, m:m + 1], -1.0, None, ALU.mult).then_inc(s_neg, 1)
                dve.wait_ge(s_exp, m + 1)
                own.after(nc.vector.reciprocal(tot[:, m:m + 1], tot[:, m:m + 1]))
                nc.vector.tensor_scalar(A[:, b % 2, t, :], A[:, b % 2, t, :], tot[:, m:m + 1], None, ALU.mult
                                        ).then_inc(s_A, 1)
            dve.wait_ge(s_e1, 1)
            own.after(nc.vector.tensor_tensor(mcol[:, :], mcol[:, :], e1[:, :], ALU.add))
            own.after(nc.vector.tensor_scalar(mcol[:, :], mcol[:, :], bsim[:, 0:1], None, ALU.add))

        @block.scalar
        def _(act):
            def exps(b):
                for t in range(QT):
                    m = b * QT + t
                    act.wait_ge(s_neg, m + 1)
                    if b >= 2:
                        act.wait_ge(s_tr, QT * (b - 1))
                    nc.scalar.activation(A[:, b % 2, t, :], sc[m % 2][:, :], ACT.Exp, bias=neg[:, m:m + 1],
                                         accum_out=tot[:, m:m + 1]).then_inc(s_exp, 1)

            exps(0)
            for b in range(B):
                if b + 1 < B:
                    exps(b + 1)
                for j in range(QT):
                    k = b * QT + j
                    act.wait_ge(s_tr, k + 1)
                    if b >= 1:
                        act.wait_ge(s_hq, DC * b)
                    nc.scalar.activation(AT[:, j, :], tp[k % 2][:, :], ACT.Identity).then_inc(s_at, 1)
                for c in range(DC):
                    act.wait_ge(s_hq, DC * b + c + 1)
                    nc.scalar.activation(hqT[:, c, b * S:(b + 1) * S], hq[c][:, :], ACT.Identity).then_inc(s_ev, 1)


def attended_row(nc, name, xnT, hqT, mcol, xhT, xcT, ident, ones):
    with Stage(nc, name) as st:
        row = st.sb("row", [1, B, S])
        mx = st.sb("mx", [1, B])
        junk = st.sb("junk", [P, 2, S])
        hc = st.sb("hc", [P, B, DC])
        r = st.ps("r", [1, B, S])
        rb = [st.ps(f"rb{i}", [P, S]) for i in range(2)]
        s_r, s_sub, s_exp, s_row, s_rb, s_hc, s_own, s_xh = (
            st.sem(n) for n in ("r", "sub", "exp", "row", "rb", "hc", "own", "xh"))
        block = st.block()

        @block.tensor
        def _(pe):
            for t in range(NT):
                last = nc.tensor.matmul(r[:, t // QT, (t % QT) * P:(t % QT + 1) * P], mcol[:, t:t + 1], ident[:, :],
                                        start=True, stop=True)
            last.then_inc(s_r, 1)
            pe.wait_ge(s_row, 1)
            for b in range(B):
                if b >= 2:
                    pe.wait_ge(s_hc, DC * (b - 1))
                nc.tensor.matmul(rb[b % 2][:, :], ones[0:1, :], row[:, b, :], start=True, stop=True).then_inc(s_rb, 1)

        @block.scalar
        def _(act):
            act.wait_ge(s_sub, 1)
            nc.scalar.activation(row[:, :, :], row[:, :, :], ACT.Exp).then_inc(s_exp, 1)

        @block.vector
        def _(dve):
            own = InOrder(dve, s_own)
            dve.wait_ge(s_r, 1)
            own.after(nc.vector.tensor_reduce(mx[:, :], r[:, :, :], AX.X, ALU.max))
            nc.vector.tensor_tensor(row[:, :, :], r[:, :, :], mx[:, :].unsqueeze(2).to_broadcast([1, B, S]),
                                    ALU.subtract).then_inc(s_sub, 1)
            for c in range(DC):
                nc.vector.tensor_tensor(xhT[:, c, :], xnT[:, c, :], hqT[:, c, :], ALU.mult)
            dve.wait_ge(s_exp, 1)
            own.after(nc.vector.tensor_reduce(mx[:, :], row[:, :, :], AX.X, ALU.add))
            own.after(nc.vector.reciprocal(mx[:, :], mx[:, :]))
            nc.vector.tensor_tensor(row[:, :, :], row[:, :, :], mx[:, :].unsqueeze(2).to_broadcast([1, B, S]), ALU.mult
                                    ).then_inc(s_row, 1)
            for b in range(B):
                dve.wait_ge(s_rb, b + 1)
                for c in range(DC):
                    k = b * DC + c
                    if k >= 2:
                        dve.wait_ge(s_hc, k - 1)
                    nc.vector.tensor_tensor_reduce(junk[:, k % 2, :], xnT[:, c, b * S:(b + 1) * S], rb[b % 2][:, :],
                                                   1.0, 0.0, ALU.mult, ALU.add, hc[:, b, c:c + 1]).then_inc(s_hc, 1)
            dve.wait_ge(s_hc, B * DC)
            for b in range(B):
                for c in range(DC):
                    nc.vector.tensor_scalar(xcT[:, c, b * S:(b + 1) * S], xnT[:, c, b * S:(b + 1) * S],
                                            hc[:, b, c:c + 1], None, ALU.mult)


def project_parts(nc, name, parts, w_dram, b_dram, x):
    with Stage(nc, name) as st:
        K = len(parts) * DC
        w = st.sb("w", [P, K, D])
        bb = st.sb("bb", [P, D])
        pp = [st.ps(f"pp{i}", [P, D]) for i in range(4)]
        s_w, s_p, s_ev, s_b = (st.sem(n) for n in ("w", "p", "ev", "b"))
        block = st.block()

        @block.sync
        def _(sp):
            sp.dma_start(w[:, :, :], cols(w_dram)).then_inc(s_w, 16)
            sp.dma_start(bb[:, :], b_dram.partition_broadcast(P)).then_inc(s_w, 16)

        @block.tensor
        def _(pe):
            pe.wait_ge(s_w, 32)
            for t in range(NT):
                if t >= 4:
                    pe.wait_ge(s_ev, t - 3)
                for k in range(K):
                    last = nc.tensor.matmul(pp[t % 4][:, :], parts[k // DC][:, k % DC, t * P:(t + 1) * P], w[:, k, :],
                                            start=(k == 0), stop=(k == K - 1))
                last.then_inc(s_p, 1)

        @block.vector
        def _(dve):
            dve.wait_ge(s_w, 32)
            for t in range(NT):
                nc.vector.tensor_tensor(x[:, t, :], x[:, t, :], bb[:, :], ALU.add).then_inc(s_b, 1)
            for t in range(NT):
                dve.wait_ge(s_b, t + 1)
                dve.wait_ge(s_p, t + 1)
                nc.vector.tensor_tensor(x[:, t, :], x[:, t, :], pp[t % 4][:, :], ALU.add).then_inc(s_ev, 1)


def address_scores(nc, name, xT, pw, u, z):
    R = pw.shape[1]
    with Stage(nc, name) as st:
        w = st.sb("w", [P, DC, R])
        us = st.sb("us", [R, u.shape[1]])
        aT = st.sb("aT", [R, T])
        pa = [st.ps(f"pa{i}", [R, S]) for i in range(2)]
        pz = [st.ps(f"pz{i}", [P, u.shape[1]]) for i in range(2)]
        s_w, s_a, s_ae, s_z, s_ze = (st.sem(n) for n in ("w", "a", "ae", "z", "ze"))
        block = st.block()

        @block.sync
        def _(sp):
            sp.dma_start(w[:, :, :], cols(pw)).then_inc(s_w, 16)
            sp.dma_start(us[:, :], u).then_inc(s_w, 16)

        @block.tensor
        def _(pe):
            pe.wait_ge(s_w, 32)
            for b in range(B):
                if b >= 2:
                    pe.wait_ge(s_ae, b - 1)
                for c in range(DC):
                    last = nc.tensor.matmul(pa[b % 2][:, :], w[:, c, :], xT[:, c, b * S:(b + 1) * S],
                                            start=(c == 0), stop=(c == DC - 1))
                last.then_inc(s_a, 1)
            for t in range(NT):
                pe.wait_ge(s_ae, t // QT + 1)
                if t >= 2:
                    pe.wait_ge(s_ze, t - 1)
                nc.tensor.matmul(pz[t % 2][:, :], aT[:, t * P:(t + 1) * P], us[:, :], start=True, stop=True
                                 ).then_inc(s_z, 1)

        @block.scalar
        def _(act):
            for b in range(B):
                act.wait_ge(s_a, b + 1)
                nc.scalar.activation(aT[:, b * S:(b + 1) * S], pa[b % 2][:, :], ACT.Identity).then_inc(s_ae, 1)

        @block.vector
        def _(dve):
            for t in range(NT):
                dve.wait_ge(s_z, t + 1)
                nc.vector.tensor_copy(z[:, t, :], pz[t % 2][:, :]).then_inc(s_ze, 1)


def mixture(nc, name, xT, w_dram, weights, acc, fresh):
    E = w_dram.shape[0]
    with Stage(nc, name) as st:
        w = st.sb("w", [P, 2, DC, D])
        pp = [st.ps(f"pp{i}", [P, D]) for i in range(4)]
        s_w = [st.sem(f"w{i}") for i in range(2)]
        s_p, s_x = st.sem("p"), st.sem("x")
        block = st.block()

        @block.sync
        def _(sp):
            for e in range(E):
                if e >= 2:
                    sp.wait_ge(s_p, NT * (e - 1))
                sp.dma_start(w[:, e % 2, :, :], cols(w_dram[e])).then_inc(s_w[e % 2], 16)

        @block.tensor
        def _(pe):
            for m in range(E * NT):
                e, t = m // NT, m % NT
                if t == 0:
                    pe.wait_ge(s_w[e % 2], 16 * (e // 2 + 1))
                if m >= 4:
                    pe.wait_ge(s_x, m - 3)
                for c in range(DC):
                    last = nc.tensor.matmul(pp[m % 4][:, :], xT[:, c, t * P:(t + 1) * P], w[:, e % 2, c, :],
                                            start=(c == 0), stop=(c == DC - 1))
                last.then_inc(s_p, 1)

        @block.vector
        def _(dve):
            for m in range(E * NT):
                e, t = m // NT, m % NT
                dve.wait_ge(s_p, m + 1)
                if m >= NT:
                    dve.wait_ge(s_x, m - NT + 1)
                if fresh and e == 0:
                    ins = nc.vector.tensor_scalar(acc[:, t, :], pp[m % 4][:, :], weights[:, t, 0:1], None, ALU.mult)
                else:
                    ins = nc.vector.scalar_tensor_tensor(acc[:, t, :], pp[m % 4][:, :], weights[:, t, e:e + 1],
                                                         acc[:, t, :], ALU.mult, ALU.add)
                ins.then_inc(s_x, 1)


def gelu_rows(nc, name, h):
    with Stage(nc, name) as st:
        block = st.block()

        @block.scalar
        def _(act):
            for t in range(0, NT, QT):
                nc.scalar.activation(h[:, t:t + QT, :], h[:, t:t + QT, :], ACT.Gelu)


def add_choice(nc, name, weights, b2, x, ident):
    E = b2.shape[0]
    with Stage(nc, name) as st:
        b2s = st.sb("b2s", [E, D])
        wT = st.sb("wT", [E, T])
        pt = [st.ps(f"pt{i}", [E, S]) for i in range(2)]
        pp = [st.ps(f"pp{i}", [P, D]) for i in range(2)]
        s_ld, s_t, s_te, s_p, s_x = (st.sem(n) for n in ("ld", "t", "te", "p", "x"))
        block = st.block()

        @block.sync
        def _(sp):
            sp.dma_start(b2s[:, :], b2).then_inc(s_ld, 16)

        @block.tensor
        def _(pe):
            pe.wait_ge(s_ld, 16)
            for b in range(B):
                if b >= 2:
                    pe.wait_ge(s_te, b - 1)
                for i in range(QT):
                    last = nc.tensor.transpose(pt[b % 2][:, i * P:(i + 1) * P], weights[:, b * QT + i, :], ident[:, :])
                last.then_inc(s_t, 1)
            for t in range(NT):
                pe.wait_ge(s_te, t // QT + 1)
                if t >= 2:
                    pe.wait_ge(s_x, t - 1)
                nc.tensor.matmul(pp[t % 2][:, :], wT[:, t * P:(t + 1) * P], b2s[:, :], start=True, stop=True
                                 ).then_inc(s_p, 1)

        @block.scalar
        def _(act):
            for b in range(B):
                act.wait_ge(s_t, b + 1)
                nc.scalar.activation(wT[:, b * S:(b + 1) * S], pt[b % 2][:, :], ACT.Identity).then_inc(s_te, 1)

        @block.vector
        def _(dve):
            for t in range(NT):
                dve.wait_ge(s_p, t + 1)
                nc.vector.tensor_tensor(x[:, t, :], x[:, t, :], pp[t % 2][:, :], ALU.add).then_inc(s_x, 1)


def sigmoid_column(nc, name, z, out):
    with Stage(nc, name) as st:
        s_e, s_own = st.sem("e"), st.sem("own")
        block = st.block()

        @block.scalar
        def _(act):
            nc.scalar.activation(out, z, ACT.Exp, scale=-1.0).then_inc(s_e, 1)

        @block.vector
        def _(dve):
            own = InOrder(dve, s_own)
            dve.wait_ge(s_e, 1)
            own.after(nc.vector.tensor_scalar(out, out, 1.0, None, ALU.add))
            own.after(nc.vector.reciprocal(out, out))



def load(nc, name, pairs):
    with Stage(nc, name) as st:
        s_ld = st.sem("ld")
        block = st.block()

        @block.sync
        def _(sp):
            for dst, src in pairs:
                sp.dma_start(dst, src).then_inc(s_ld, 16)
            sp.wait_ge(s_ld, 16 * len(pairs))


def rows(ap):
    return ap.rearrange("(t p) n -> p t n", p=P)


def cols(ap):
    return ap.rearrange("(c p) n -> p c n", p=P)




ZEROED = 3 * T
ZEROING = 8


def network(nc, a, out):
    with ExitStack() as ctx:
        def sb(name, shape, dt=F32):
            return ctx.enter_context(nc.sbuf_tensor(name, shape, dt))

        s_stored = ctx.enter_context(nc.semaphore("stored"))
        x = sb("x", [P, NT, D])
        ident = sb("ident", [P, P])
        identb = sb("identb", [P, P], BF16)
        sel_sum = sb("sel_sum", [P, GH])
        tiny = sb("tiny", [P, 1])
        iota = sb("iota", [P, 64])
        tri = sb("tri", [P, P], BF16)
        ones = sb("ones", [P, P])
        onesb = sb("onesb", [P, P], BF16)
        sel_head = nc.dram_tensor("sel_head_bf", [MR, GH, S], BF16).ap()
        qp = nc.dram_tensor("q_parts", [NPART, D, T], BF16).ap()
        kp = nc.dram_tensor("k_parts", [NPART, D, T], BF16).ap()
        vp = nc.dram_tensor("v_padded", [T, H16 * 32], F32).ap()
        scratch = (qp, kp, vp)
        xs = nc.dram_tensor("slot_rows", [4 * T, D], F32).ap()
        ys = nc.dram_tensor("slot_results", [3 * T, D], F32).ap()
        s_zeroed = ctx.enter_context(nc.semaphore("zeroed"))
        consts = (ident, identb, sel_head, sel_sum)

        with Stage(nc, "setup") as st:
            selh = st.sb("selh", [MR, GH, S])
            trif = st.sb("trif", [P, P])
            selb = st.sb("selb", [MR, GH, S], BF16)
            s_ld, s_cp, s_st = st.sem("ld"), st.sem("cp"), st.sem("st")
            block = st.block()

            @block.sync
            def _(sp):
                for dst, src in ((x[:, :, :], rows(a["x"])), (ident[:, :], a["c_ident"]),
                                 (sel_sum[:, :], a["c_selsum"]), (selh[:, :, :], a["c_selhead"]),
                                 (iota[:, :], a["c_iota"]), (trif[:, :], a["c_tri"])):
                    sp.dma_start(dst, src).then_inc(s_ld, 16)
                sp.wait_ge(s_cp, 2)
                sp.dma_start(sel_head, selb[:, :, :]).then_inc(s_st, 16)
                sp.wait_ge(s_st, 16)
                sp.wait_ge(s_ld, 96)

            @block.gpsimd
            def _(pool):
                n = ZEROED // (ZEROING - 2)
                for to in [xs[i * n:(i + 1) * n, :] for i in range(ZEROING - 2)] + [
                        ys[i * n:(i + 1) * n, :] for i in range(ZEROING - 4, ZEROING - 2)]:
                    pool.dma_start(to, a["c_zero"]).then_inc(s_zeroed, 16)

            @block.vector
            def _(dve):
                nc.vector.memset(tiny[:, :], 1e-11)
                nc.vector.memset(ones[:, :], 1.0)
                nc.vector.memset(onesb[:, :], 1.0)
                dve.wait_ge(s_ld, 96)
                nc.vector.tensor_copy(tri[:, :], trif[:, :])
                nc.vector.tensor_copy(identb[:, :], ident[:, :]).then_inc(s_cp, 1)
                nc.vector.tensor_copy(selb[:, :, :], selh[:, :, :]).then_inc(s_cp, 1)

        def xattn16(name, w, masked):
            with Stage(nc, name) as outer:
                with Stage(nc, name + "a") as st:
                    xn, xnT, cT = st.sb("xn", [P, NT, D]), st.sb("xnT", [P, DC, T]), st.sb("cT", [P, DC, T])
                    load(nc, name + "ld", [(cT[:, :, :], cols(a["ctxT"]))])
                    layernorm(nc, name + "ln", x, xn, xnT, ident)
                    project16(nc, name + "pj", xnT, cT, w, scratch)
                outT = outer.sb("outT", [P, B * NG, S])
                masks = None
                if masked:
                    masks = {"neg_q": outer.sb("neg_q", [P, NT, S], BF16), "neg_k": outer.sb("neg_k", [P, NT, S], BF16),
                             "any_masked": outer.sb("any_masked", [P, NT]),
                             "vmasked": outer.sb("vmasked", [P, B * NG, S])}
                    masks16(nc, name + "mk", a["mask"], a["maskT"], vp, masks["neg_q"], masks["neg_k"],
                            masks["any_masked"], masks["vmasked"])
                    masks["tiny"] = tiny
                attend16(nc, name + "at", scratch, consts, outT, masks)
                output16(nc, name + "wo", outT, w["wo"], w["bo"], x)

        def sparse_moe(nc, name, logits, xn, w1s, w2, func, gated, over_all, zeroed=None, affine=None, meanwhile=None):
            E, K = logits.shape[2], 2
            F = sum(w.shape[2] for w in w1s)
            with Stage(nc, name + "x") as st:
                wk, slots = st.sb("wk", [P, NT, K]), st.sb("slots", [P, K, NT], I32)
                expert_of = st.sb("expert_of", [P, K * NT + E], I32)
                wa, wd = st.sb("wa", [P, E, DC, F]), st.sb("wd", [P, E, w2.shape[1] // P, D])
                route_tiles(nc, name + "t", logits, wk, slots, expert_of, iota, tri, onesb, over_all)
                loads, at = [], 0
                for w in w1s:
                    loads += [(wa[:, e, :, at:at + w.shape[2]], cols(w[e])) for e in range(E)]
                    at += w.shape[2]
                loads += [(wd[:, e, :, :], cols(w2[e])) for e in range(E)]
                if meanwhile is None:
                    dispatch(nc, name + "d", xn, slots, xs, loads, zeroed)
                else:
                    meanwhile((xn, slots, xs, loads))
                tile_experts(nc, name + "e", xs, ys, expert_of, wa, wd, func, gated, ident, affine)
                combine(nc, name + "c", ys, slots, wk, x, None)

        xattn16("L0", {k: a["L0_" + k] for k in ("wq", "wk", "wv", "bq", "bk", "bv", "wo", "bo")}, True)
        with Stage(nc, "L0f") as st:
            xn, xnT = st.sb("xn", [P, NT, D]), st.sb("xnT", [P, DC, T])
            layernorm(nc, "L0f0", x, xn, xnT, ident)
            with Stage(nc, "L0g") as st2:
                xn1, att = st2.sb("xn1", [P, NT, D]), st2.sb("att", [P, NT, D])
                layernorm(nc, "L0f1", xn, xn1, xnT, ident, (a["L0_ln1w"], a["L0_ln1b"]))
                small_attention(nc, "L0f2", xnT, a["L0_wqkv"], att)
                transpose_rows(nc, "L0f3", att, xnT, ident)

            def residual(own, t, psum):
                own.after(nc.vector.tensor_tensor(xn[:, t, :], xn[:, t, :], psum, ALU.add))
                return nc.vector.tensor_tensor(x[:, t, :], x[:, t, :], xn[:, t, :], ALU.add)

            project_rows(nc, "L0f4", xnT, a["L0_proj"], residual)
            xn2 = st.sb("xn2", [P, NT, D])
            layernorm(nc, "L0f5", xn, xn2, xnT, ident, (a["L0_ln2w"], a["L0_ln2b"]))
            logits = st.sb("logits", [P, NT, 8])
            project_rows(nc, "L0fr", xnT, a["L0_router"],
                         lambda own, t, psum: nc.vector.tensor_copy(logits[:, t, :], psum))
            sparse_moe(nc, "L0f", logits[:, :, :], xn2, [a["L0_w1"]], a["L0_w2"], ACT.Gelu_apprx_tanh, False, True,
                       s_zeroed, (a["L0_ln2w"], a["L0_ln2b"]))
        with Stage(nc, "L1x") as st:
            xnT, cT = st.sb("xnT", [P, DC, T]), st.sb("cT", [P, DC, T])
            with Stage(nc, "L1y") as st2:
                xn = st2.sb("xn", [P, NT, D])
                load(nc, "L1ld", [(cT[:, :, :], cols(a["ctxT"]))])
                layernorm(nc, "L1ln", x, xn, xnT, ident)
            masks = (st.sb("am", [P, B, QT * (QT + 1) // 2 * P]), st.sb("uT", [P, B, QT * (QT + 1) // 2 * P]),
                     st.sb("sufmax", [P, NT]), st.sb("usum", [P, NT]))
            causal_masks(nc, "L1m", a, *masks, ident)
            attend64(nc, "L1a", a, xnT, cT, masks, x, ident)
        with Stage(nc, "L1f") as st:
            xn, xnT = st.sb("xn", [P, NT, D]), st.sb("xnT", [P, DC, T])
            layernorm(nc, "L1f0", x, xn, xnT, ident)
            E, K, cap = 8, 2, T // 8
            logits, wk = st.sb("logits", [P, NT, E]), st.sb("wk", [P, NT, K])
            slots = (st.sb("slot_to", [P, K, NT], I32), st.sb("slot_from", [P, K, NT], I32))
            project_rows(nc, "L1fr", xnT, a["L1_router"],
                         lambda own, t, psum: nc.vector.tensor_copy(logits[:, t, :], psum))
            route(nc, "L1ft", logits, K, wk, iota, over_all=True, capacity=cap, tri=tri, ones=onesb,
                  spare=a["c_spare"], slots=slots)
            dispatch(nc, "L1fd", xn, slots[0], xs)
            slot_experts(nc, "L1fe", xs, ys, a["L1_w1"], a["L1_w2"], ACT.Gelu_apprx_tanh, ident)
            combine(nc, "L1fc", ys, slots[1], wk, x, a["L1_bias"])
        with Stage(nc, "L2x") as st:
            xnT, cT = st.sb("xnT", [P, DC, T]), st.sb("cT", [P, DC, T])
            hqT, crow = st.sb("hqT", [P, DC, T]), st.sb("crow", [P, NT, D])
            mcol = st.sb("mcol", [P, NT])
            load(nc, "L2ld", [(cT[:, :, :], cols(a["ctxT"])), (crow[:, :, :], rows(a["ctx"]))])
            with Stage(nc, "L2y") as st2:
                layernorm(nc, "L2ln", x, st2.sb("xn", [P, NT, D]), xnT, ident)
            similarity(nc, "L2s", a, xnT, cT, crow, hqT, mcol, ident)
            xhT, xcT = st.sb("xhT", [P, DC, T]), st.sb("xcT", [P, DC, T])
            attended_row(nc, "L2r", xnT, hqT, mcol, xhT, xcT, ident, ones)
            project_parts(nc, "L2p", (xnT, hqT, xhT, xcT), a["L2_Wqv"], a["L2_bqv"], x)
        with Stage(nc, "L2f") as st:
            xnT, xn = st.sb("xnT", [P, DC, T]), st.sb("xn", [P, NT, D])
            layernorm(nc, "L2f0", x, xn, xnT, ident)
            logits, weights = st.sb("logits", [P, NT, 17]), st.sb("weights", [P, NT, 1])
            project_rows(nc, "L2fr", xnT, a["L2_router"],
                         lambda own, t, psum: nc.vector.tensor_copy(logits[:, t, :], psum))
            sigmoid_column(nc, "L2fs", logits[:, :, 16:17], weights[:, :, 0:1])
            sparse_moe(nc, "L2f", logits[:, :, 0:16], xn, [a["L2_wg"][0:16], a["L2_wu"][0:16]], a["L2_wd"][0:16],
                       ACT.Silu, True, False, meanwhile=lambda beside: experts(
                           nc, "L2fg", xnT, a["L2_wg"][16:20], a["L2_wd"][16:20], weights, x, ACT.Silu,
                           a["L2_wu"][16:20], w_of=lambda e: 0, beside=beside))
        xattn16("L3", {k: a["L3_" + k] for k in ("wq", "wk", "wv", "bq", "bk", "bv", "wo", "bo")}, False)
        with Stage(nc, "L3f") as st:
            xnT, h = st.sb("xnT", [P, DC, T]), st.sb("h", [P, NT, D])
            layernorm(nc, "L3f0", x, h, xnT, ident)
            z = st.sb("z", [P, NT, 36])
            wts = [st.sb(f"wt{i}", [P, NT, 12]) for i in range(3)]
            address_scores(nc, "L3fa", xnT, a["L3_P"], a["L3_U"], z)
            for i in range(3):
                route(nc, f"L3ft{i}", z[:, :, 12 * i:12 * i + 12], 3, wts[i][:, :, :], iota)
            mixture(nc, "L3fm", xnT, a["L3_W1"], wts[0], h, True)
            gelu_rows(nc, "L3fg", h)
            transpose_rows(nc, "L3fh", h, xnT, ident)
            mixture(nc, "L3fn", xnT, a["L3_W2"], wts[1], x, False)
            add_choice(nc, "L3fb", wts[2], a["L3_b2"], x, ident)

        with Stage(nc, "store") as st:
            block = st.block()

            @block.sync
            def _(sp):
                sp.dma_start(rows(out), x[:, :, :]).then_inc(s_stored, 16)
                sp.wait_ge(s_stored, 16)


def kernel(**inputs):
    import numpy as np
    import concourse.bacc as _bacc
    from concourse.bass_utils import run_bass_kernel_spmd as _run

    i = {k: np.asarray(v) for k, v in inputs.items()}
    c = np.ascontiguousarray
    f32 = np.float32

    def pad_heads(w):
        out = np.zeros((H16, 32, w.shape[1]), f32)
        out[:, :HD] = w.reshape(H16, HD, w.shape[1])
        return out.reshape(H16 * 32, w.shape[1])

    Stage.USED.clear()
    a = {"x": i["x"].reshape(T, D), "ctxT": c(i["ctx_1024"].reshape(T, D).T),
         "mask": i["mask_BxSxS2_ik1"], "maskT": c(i["mask_BxSxS2_ik1"].transpose(0, 2, 1)),
         "c_ident": np.eye(P, dtype=f32)}
    selsum = np.zeros((P, GH), f32)
    for h in range(GH):
        selsum[32 * h + HD, h] = 1.0
    a["c_selsum"] = selsum
    selhead = np.zeros((NPART, GH, GH, S), f32)
    for h in range(GH):
        selhead[:, h, h, :] = 1.0
    a["c_selhead"] = selhead.reshape(MR, GH, S)
    for k in ("wq", "wk", "wv"):
        a["L0_" + k] = c(i["L0_xattn_" + k].T)
    for k in ("bq", "bk", "bv", "bo"):
        a["L0_" + k] = i["L0_xattn_" + k]
    a["L0_wo"] = pad_heads(i["L0_xattn_wo"].T)
    a["c_iota"] = np.tile(np.arange(64, dtype=f32), (P, 1))
    a["c_zero"] = np.zeros((ZEROED // (ZEROING - 2), D), f32)
    a["c_tri"] = np.triu(np.ones((P, P), f32), 1)
    for k in ("ln1w", "ln1b", "ln2w", "ln2b"):
        a["L0_" + k] = i["L0_ffn_" + k[:3] + {"w": "_weight", "b": "_bias"}[k[3]]]
    a["L0_wqkv"] = c(i["L0_ffn_qkv_weight"].T)
    a["L0_proj"] = c(i["L0_ffn_proj_weight"].T)
    a["L0_router"] = c(i["L0_ffn_router_weight"].T)
    a["L0_w1"], a["L0_w2"] = i["L0_ffn_moe_w1"], i["L0_ffn_moe_w2"]
    for k in "QKV":
        a["L1_W" + k] = c(i["L1_xattn_W_" + k].transpose(1, 0, 2).reshape(D, H16 * HB))
    for k in "QK":
        a["L1_b" + k] = c(i["L1_xattn_b_" + k].reshape(NP, P).T)
    a["L1_bV"] = i["L1_xattn_b_V"].reshape(-1)
    a["L1_WO"], a["L1_bO"] = i["L1_xattn_W_O"].reshape(H16 * HB, D), i["L1_xattn_b_O"]
    a["addm"] = i["mask_Bx1x1xS2_ff0"].reshape(T)
    is_later = np.arange(S)[None, :] > np.arange(S)[:, None]
    a["c_later"] = c(np.where(is_later, f32(BIG), f32(0)).reshape(QT, P, S).transpose(1, 0, 2))
    a["c_fill"] = c(np.where(is_later, f32(-1e5), f32(BIG)).reshape(QT, P, S).transpose(1, 0, 2))
    a["L1_router"] = i["L1_ffn_router_w"]
    a["L1_w1"], a["L1_w2"], a["L1_bias"] = i["L1_ffn_w1"], i["L1_ffn_w2"], i["L1_ffn_bias"].reshape(D)
    a["c_spare"] = c((2 * T + np.arange(2 * T, dtype=f32)).reshape(2, NT, P).transpose(2, 0, 1))
    a["ctx"] = i["ctx_1024"].reshape(T, D)
    a["L2_wsim"] = c(i["L2_xattn_w_sim"].reshape(3, DC, P).transpose(2, 0, 1))
    a["L2_bsim"], a["L2_Wqv"], a["L2_bqv"] = i["L2_xattn_b_sim"], i["L2_xattn_W_qv"], i["L2_xattn_b_qv"]
    a["L2_router"] = c(np.concatenate([i["L2_ffn_Wg"], i["L2_ffn_Wsg"]]).T)
    for k, n in (("g", "gate"), ("u", "up")):
        shared = i["L2_ffn_Ws_" + n].reshape(4, P, D)
        a["L2_w" + k] = c(np.concatenate([i["L2_ffn_We_" + n], shared]).transpose(0, 2, 1))
    shared = i["L2_ffn_Ws_down"].T.reshape(4, P, D)
    a["L2_wd"] = c(np.concatenate([i["L2_ffn_We_down"].transpose(0, 2, 1), shared]))
    kv = i["L3_xattn_Wkv"].reshape(D, H16, 2, HD)
    bkv = i["L3_xattn_bkv"].reshape(H16, 2, HD)
    a["L3_wq"], a["L3_bq"] = i["L3_xattn_Wq"], i["L3_xattn_bq"]
    for j, k in enumerate("kv"):
        a["L3_w" + k], a["L3_b" + k] = c(kv[:, :, j].reshape(D, D)), c(bkv[:, j].reshape(D))
    a["L3_wo"], a["L3_bo"] = pad_heads(i["L3_xattn_Wp"]), i["L3_xattn_bp"]
    a["L3_P"] = c(i["L3_ffn_P_w"].T)
    a["L3_U"] = c(np.concatenate([i["L3_ffn_U1"], i["L3_ffn_U2"], i["L3_ffn_U3"]]).T)
    a["L3_W1"], a["L3_W2"] = c(i["L3_ffn_W1"].transpose(0, 2, 1)), c(i["L3_ffn_W2"].transpose(0, 2, 1))
    a["L3_b2"] = i["L3_ffn_b2"]

    nc = _bacc.Bacc("TRN2", target_bir_lowering=False, num_devices=1)
    arrays, aps = {}, {}
    for name, v in a.items():
        v = c(v)
        arrays[f"in_{name}"] = v
        aps[name] = nc.dram_tensor(f"in_{name}", v.shape, mybir.dt.from_np(v.dtype), kind="ExternalInput").ap()
    out = nc.dram_tensor("out_0", (T, D), F32, kind="ExternalOutput").ap()
    network(nc, aps, out)
    r = _run(nc, [arrays], core_ids=[0])
    return r.results[0]["out_0"].reshape(B, S, D)
```
